# Optimizing a Trainium2 kernel written in Bass

```python
import numpy as np
import jax
import jax.numpy as jnp

def _softmax(x, axis=-1):
    return jax.nn.softmax(x, axis=axis)

def _gelu(x):
    return jax.nn.gelu(x, approximate=True)

def _silu(x):
    return jax.nn.silu(x)

def _sigmoid(x):
    return jax.nn.sigmoid(x)

def _layernorm(x, axis=-1, eps=1e-05):
    m = jnp.mean(x, axis=axis, keepdims=True)
    v = jnp.var(x, axis=axis, keepdims=True)
    return (x - m) / jnp.sqrt(v + eps)

def _scatter_add(tgt, idx, src, axis=0):
    return tgt.at[idx].add(src)

def _segment_sum(src, seg, n):
    return jax.ops.segment_sum(src, seg, n)
kernel_name = 'mk_adaln_d4_jaxref_r8_877899'

def setup_inputs(seed: int=0):
    np.random.seed(seed)
    _w = jnp.asarray

    def _L0_attn_setup():
        import jax, jax.numpy as jnp
        import numpy as np
        HEADS = 16
        DIM_HEAD = 64
        EPS = 1e-08
        key = jax.random.key(seed)
        ks = jax.random.split(key, 5)
        B, N, D = (2, 256, 128)
        inner = HEADS * DIM_HEAD
        return {'x': jax.random.normal(ks[0], (B, N, D), jnp.float32), 'Wq': jax.random.normal(ks[1], (D, inner), jnp.float32) * D ** (-0.5), 'Wkv': jax.random.normal(ks[2], (D, 2 * inner), jnp.float32) * D ** (-0.5), 'Wo': jax.random.normal(ks[3], (inner, D), jnp.float32) * inner ** (-0.5), 'bo': jax.random.normal(ks[4], (D,), jnp.float32) * 0.02}
    _L0_attn_in = _L0_attn_setup()

    def _L0_ffn_setup():
        import jax, jax.numpy as jnp
        import numpy as np
        B, L, D = (2, 256, 128)
        E = 15
        H = D * 1
        K = 3
        T = 1.0
        key = jax.random.key(seed)
        ks = jax.random.split(key, 12)
        s = 0.02
        return {'x': jax.random.normal(ks[0], (B, L, D), dtype=jnp.float32), 'router_W': jax.random.normal(ks[1], (D, E), dtype=jnp.float32) * s, 'router_b': jnp.zeros((E,), dtype=jnp.float32), 'sW1': jax.random.normal(ks[2], (D, H), dtype=jnp.float32) * s, 'sb1': jnp.zeros((H,), dtype=jnp.float32), 'sW2': jax.random.normal(ks[3], (H, D), dtype=jnp.float32) * s, 'sb2': jnp.zeros((D,), dtype=jnp.float32), 'eW1': jax.random.normal(ks[4], (E, D, H), dtype=jnp.float32) * s, 'eb1': jnp.zeros((E, H), dtype=jnp.float32), 'eW2': jax.random.normal(ks[5], (E, H, D), dtype=jnp.float32) * s, 'eb2': jnp.zeros((E, D), dtype=jnp.float32)}
    _L0_ffn_in = _L0_ffn_setup()
    _L0_c = _w((lambda *s: np.random.randn(*s).astype(np.float32) * 0.05)(16, 128))
    _L0_wmod = _w((lambda *s: np.random.randn(*s).astype(np.float32) * 0.05)(128, 6 * 128) * 128 ** (-0.5))

    def _L1_attn_setup():
        import math
        import jax, jax.numpy as jnp
        import numpy as np
        from jax.scipy.special import xlogy, gammaln

        def get_positional_embed(seq_len, feature_size):
            distances = jnp.arange(-seq_len + 1, seq_len, dtype=jnp.float32)
            n = feature_size // 6
            absd = jnp.abs(distances)[:, None]
            max_range = math.log(seq_len) / math.log(2.0)
            half_life = 2.0 ** jnp.linspace(3.0, max_range, n)
            feat_exp = jnp.exp(-math.log(2.0) / half_life[None, :] * absd)
            center_widths = 2.0 ** jnp.arange(1, n + 1, dtype=jnp.float32) - 1.0
            feat_cm = (center_widths[None, :] > absd).astype(jnp.float32)
            stddev = seq_len / (2.0 * n)
            start_mean = seq_len / n
            mean = jnp.linspace(start_mean, float(seq_len), n)[None, :]
            conc = (mean / stddev) ** 2
            rate = mean / stddev ** 2
            log_unnorm = xlogy(conc - 1.0, absd) - rate * absd
            log_norm = gammaln(conc) - conc * jnp.log(rate)
            probs = jnp.exp(log_unnorm - log_norm) + 1e-08
            feat_gamma = probs / jnp.max(probs, axis=-1, keepdims=True)
            emb = jnp.concatenate([feat_exp, feat_cm, feat_gamma], axis=-1)
            emb = jnp.concatenate([emb, jnp.sign(distances)[:, None] * emb], axis=-1)
            return emb

        def relative_shift(x):
            b, h, t1, t2m1 = x.shape
            x = jnp.pad(x, ((0, 0), (0, 0), (0, 0), (1, 0)))
            t2 = t2m1 + 1
            x = x.reshape(b, h, t2, t1)
            x = x[:, :, 1:, :]
            x = x.reshape(b, h, t1, t2 - 1)
            return x[..., :(t2 + 1) // 2]
        key = jax.random.key(seed)
        ks = jax.random.split(key, 9)
        B, L, D = (2, 128, 128)
        H, Dk, Dv = (8, 128, 128)
        R = 192
        sq = math.sqrt(2.0 / (D + Dk))
        sv = math.sqrt(2.0 / (D + Dv))
        return {'q': jax.random.normal(ks[0], (B, L, D), jnp.float32), 'w_qs': jax.random.normal(ks[1], (D, H * Dk), jnp.float32) * sq, 'w_ks': jax.random.normal(ks[2], (D, H * Dk), jnp.float32) * sq, 'w_vs': jax.random.normal(ks[3], (D, H * Dv), jnp.float32) * sv, 'w_rel_pos_k': jax.random.normal(ks[4], (R, H * Dk), jnp.float32) * 0.05, 'rel_embed_bias': jax.random.normal(ks[5], (1, H, 1, Dk), jnp.float32), 'rel_pos_bias': jax.random.normal(ks[6], (1, H, 1, Dk), jnp.float32), 'w_out': jax.random.normal(ks[7], (H * Dv, D), jnp.float32) * 0.02, 'b_out': jax.random.normal(ks[8], (D,), jnp.float32) * 0.02}
    _L1_attn_in = _L1_attn_setup()

    def _L1_ffn_setup():
        import jax, jax.numpy as jnp
        import numpy as np
        TOP_K = 2
        key = jax.random.key(seed)
        k1, k2, k3, k4 = jax.random.split(key, 4)
        B, T, D, H, E = (2, 256, 128, 256, 8)
        x = jax.random.normal(k1, (B, T, D), dtype=jnp.float32)
        w12 = jax.random.normal(k2, (E, 2 * H, D), dtype=jnp.float32) * D ** (-0.5)
        w3 = jax.random.normal(k3, (E, D, H), dtype=jnp.float32) * H ** (-0.5)
        gate_w = jax.random.normal(k4, (E, D), dtype=jnp.float32) * D ** (-0.5)
        return {'x': x, 'w12': w12, 'w3': w3, 'gate_w': gate_w}
    _L1_ffn_in = _L1_ffn_setup()
    _L1_c = _w((lambda *s: np.random.randn(*s).astype(np.float32) * 0.05)(16, 128))
    _L1_wmod = _w((lambda *s: np.random.randn(*s).astype(np.float32) * 0.05)(128, 6 * 128) * 128 ** (-0.5))

    def _L2_attn_setup():
        import jax, jax.numpy as jnp
        import numpy as np
        import math
        N_HEAD = 16
        N_EMBD = 128
        HEAD_DIM = N_EMBD // N_HEAD
        ROPE_BASE = 10000.0

        def _rope_cos_sin(T, dh, dtype):
            inv_freq = 1.0 / ROPE_BASE ** (jnp.arange(0, dh, 2, dtype=jnp.float32) / dh)
            freqs = jnp.arange(T, dtype=jnp.float32)[:, None] * inv_freq[None, :]
            cos = jnp.repeat(jnp.cos(freqs), 2, axis=-1).astype(dtype)
            sin = jnp.repeat(jnp.sin(freqs), 2, axis=-1).astype(dtype)
            return (cos, sin)

        def _apply_rope(x, cos, sin):
            x_even = x[..., ::2]
            x_odd = x[..., 1::2]
            x_rot = jnp.stack((-x_odd, x_even), axis=-1).reshape(x.shape)
            return x * cos + x_rot * sin
        key = jax.random.key(seed)
        k1, k2, k3 = jax.random.split(key, 3)
        B, T, C = (2, 256, N_EMBD)
        x = jax.random.normal(k1, (B, T, C), dtype=jnp.float32)
        Wqkv = jax.random.normal(k2, (C, 3 * C), dtype=jnp.float32) * (1.0 / math.sqrt(C))
        Wproj = jax.random.normal(k3, (C, C), dtype=jnp.float32) * (1.0 / math.sqrt(C))
        return {'x': x, 'Wqkv': Wqkv, 'Wproj': Wproj}
    _L2_attn_in = _L2_attn_setup()

    def _L2_ffn_setup():
        import jax, jax.numpy as jnp
        import numpy as np
        B, S, H, F, E = (8, 256, 128, 512, 8)
        INIT_LAMBDA = 0.2
        key = jax.random.key(seed)
        ks = jax.random.split(key, 12)
        std = 0.02
        return {'hidden_states': jax.random.normal(ks[0], (B, S, H), jnp.float32), 'gate_w1': jax.random.normal(ks[1], (H, H), jnp.float32) * 0.01, 'gate_b1': jnp.zeros((H,), jnp.float32), 'gate_w2': jax.random.normal(ks[2], (E, H), jnp.float32) * 0.01, 'gate_b2': jnp.full((E,), INIT_LAMBDA, jnp.float32), 'W1': jax.random.normal(ks[3], (F, H), jnp.float32) * std, 'b1': jax.random.normal(ks[4], (F,), jnp.float32) * std, 'W2': jax.random.normal(ks[5], (H, F), jnp.float32) * std, 'b2': jax.random.normal(ks[6], (H,), jnp.float32) * std, 'TW1': jax.random.normal(ks[7], (E, F, H), jnp.float32) * std, 'Tb1': jax.random.normal(ks[8], (E, F), jnp.float32) * std, 'TW2': jax.random.normal(ks[9], (E, H, F), jnp.float32) * std, 'Tb2': jax.random.normal(ks[10], (E, H), jnp.float32) * std}
    _L2_ffn_in = _L2_ffn_setup()
    _L2_c = _w((lambda *s: np.random.randn(*s).astype(np.float32) * 0.05)(16, 128))
    _L2_wmod = _w((lambda *s: np.random.randn(*s).astype(np.float32) * 0.05)(128, 6 * 128) * 128 ** (-0.5))

    def _L3_attn_setup():
        import jax, jax.numpy as jnp
        import numpy as np
        D_MODEL = 128
        NUM_HEADS = 16
        D_K = D_MODEL // NUM_HEADS
        ROPE_THETA = 10000.0
        MAX_SEQ_LEN = 256

        def _rope_tables():
            dim_index = jnp.arange(D_K // 2, dtype=jnp.float32)
            pos = jnp.arange(MAX_SEQ_LEN, dtype=jnp.float32)
            theta_inv = ROPE_THETA ** (-2.0 * dim_index / D_K)
            ang = pos[:, None] * theta_inv[None, :]
            return (jnp.sin(ang), jnp.cos(ang))

        def _apply_rope(x, positions, sin, cos):
            s = sin[positions]
            c = cos[positions]
            x_even = x[..., ::2]
            x_odd = x[..., 1::2]
            y_even = x_even * c - x_odd * s
            y_odd = x_even * s + x_odd * c
            y = jnp.stack([y_even, y_odd], axis=-1)
            return y.reshape(x.shape)
        key = jax.random.key(seed)
        k0, k1, k2, k3, k4 = jax.random.split(key, 5)
        std = np.sqrt(2.0 / (D_MODEL + D_MODEL))
        in_features = jax.random.normal(k0, (2, 256, D_MODEL), dtype=jnp.float32)
        W_q = jax.random.normal(k1, (D_MODEL, D_MODEL), dtype=jnp.float32) * std
        W_k = jax.random.normal(k2, (D_MODEL, D_MODEL), dtype=jnp.float32) * std
        W_v = jax.random.normal(k3, (D_MODEL, D_MODEL), dtype=jnp.float32) * std
        W_o = jax.random.normal(k4, (D_MODEL, D_MODEL), dtype=jnp.float32) * std
        return {'in_features': in_features, 'W_q': W_q, 'W_k': W_k, 'W_v': W_v, 'W_o': W_o}
    _L3_attn_in = _L3_attn_setup()

    def _L3_ffn_setup():
        import jax, jax.numpy as jnp
        import numpy as np
        TOP_K = 6

        def _glu_mlp(x, wg, wu, wd):
            return jax.nn.silu(x @ wg) * (x @ wu) @ wd
        key = jax.random.key(seed)
        ks = jax.random.split(key, 8)
        B, S, D, E, F, FS = (2, 256, 128, 8, 64, 128)
        sc = 0.02
        return {'hidden_states': jax.random.normal(ks[0], (B, S, D), jnp.float32), 'router_w': jax.random.normal(ks[1], (D, E), jnp.float32) * sc, 'w_gate': jax.random.normal(ks[2], (E, D, F), jnp.float32) * sc, 'w_up': jax.random.normal(ks[3], (E, D, F), jnp.float32) * sc, 'w_down': jax.random.normal(ks[4], (E, F, D), jnp.float32) * sc, 'ws_gate': jax.random.normal(ks[5], (D, FS), jnp.float32) * sc, 'ws_up': jax.random.normal(ks[6], (D, FS), jnp.float32) * sc, 'ws_down': jax.random.normal(ks[7], (FS, D), jnp.float32) * sc}
    _L3_ffn_in = _L3_ffn_setup()
    _L3_c = _w((lambda *s: np.random.randn(*s).astype(np.float32) * 0.05)(16, 128))
    _L3_wmod = _w((lambda *s: np.random.randn(*s).astype(np.float32) * 0.05)(128, 6 * 128) * 128 ** (-0.5))
    _d = {'L0_attn_x': _L0_attn_in['x'], 'L0_attn_Wq': _L0_attn_in['Wq'], 'L0_attn_Wkv': _L0_attn_in['Wkv'], 'L0_attn_Wo': _L0_attn_in['Wo'], 'L0_attn_bo': _L0_attn_in['bo'], 'L0_ffn_router_W': _L0_ffn_in['router_W'], 'L0_ffn_router_b': _L0_ffn_in['router_b'], 'L0_ffn_sW1': _L0_ffn_in['sW1'], 'L0_ffn_sb1': _L0_ffn_in['sb1'], 'L0_ffn_sW2': _L0_ffn_in['sW2'], 'L0_ffn_sb2': _L0_ffn_in['sb2'], 'L0_ffn_eW1': _L0_ffn_in['eW1'], 'L0_ffn_eb1': _L0_ffn_in['eb1'], 'L0_ffn_eW2': _L0_ffn_in['eW2'], 'L0_ffn_eb2': _L0_ffn_in['eb2'], 'L0_c': _L0_c, 'L0_wmod': _L0_wmod, 'L1_attn_w_qs': _L1_attn_in['w_qs'], 'L1_attn_w_ks': _L1_attn_in['w_ks'], 'L1_attn_w_vs': _L1_attn_in['w_vs'], 'L1_attn_w_rel_pos_k': _L1_attn_in['w_rel_pos_k'], 'L1_attn_rel_embed_bias': _L1_attn_in['rel_embed_bias'], 'L1_attn_rel_pos_bias': _L1_attn_in['rel_pos_bias'], 'L1_attn_w_out': _L1_attn_in['w_out'], 'L1_attn_b_out': _L1_attn_in['b_out'], 'L1_ffn_w12': _L1_ffn_in['w12'], 'L1_ffn_w3': _L1_ffn_in['w3'], 'L1_ffn_gate_w': _L1_ffn_in['gate_w'], 'L1_c': _L1_c, 'L1_wmod': _L1_wmod, 'L2_attn_Wqkv': _L2_attn_in['Wqkv'], 'L2_attn_Wproj': _L2_attn_in['Wproj'], 'L2_ffn_gate_w1': _L2_ffn_in['gate_w1'], 'L2_ffn_gate_b1': _L2_ffn_in['gate_b1'], 'L2_ffn_gate_w2': _L2_ffn_in['gate_w2'], 'L2_ffn_gate_b2': _L2_ffn_in['gate_b2'], 'L2_ffn_W1': _L2_ffn_in['W1'], 'L2_ffn_b1': _L2_ffn_in['b1'], 'L2_ffn_W2': _L2_ffn_in['W2'], 'L2_ffn_b2': _L2_ffn_in['b2'], 'L2_ffn_TW1': _L2_ffn_in['TW1'], 'L2_ffn_Tb1': _L2_ffn_in['Tb1'], 'L2_ffn_TW2': _L2_ffn_in['TW2'], 'L2_ffn_Tb2': _L2_ffn_in['Tb2'], 'L2_c': _L2_c, 'L2_wmod': _L2_wmod, 'L3_attn_W_q': _L3_attn_in['W_q'], 'L3_attn_W_k': _L3_attn_in['W_k'], 'L3_attn_W_v': _L3_attn_in['W_v'], 'L3_attn_W_o': _L3_attn_in['W_o'], 'L3_ffn_router_w': _L3_ffn_in['router_w'], 'L3_ffn_w_gate': _L3_ffn_in['w_gate'], 'L3_ffn_w_up': _L3_ffn_in['w_up'], 'L3_ffn_w_down': _L3_ffn_in['w_down'], 'L3_ffn_ws_gate': _L3_ffn_in['ws_gate'], 'L3_ffn_ws_up': _L3_ffn_in['ws_up'], 'L3_ffn_ws_down': _L3_ffn_in['ws_down'], 'L3_c': _L3_c, 'L3_wmod': _L3_wmod}
    _x0 = _d['L0_attn_x']
    _d['L0_attn_x'] = jax.random.normal(jax.random.fold_in(jax.random.key(seed), 1), (16, 256, 128), dtype=_x0.dtype)
    del _x0
    return _d

def reference(L0_attn_x, L0_attn_Wq, L0_attn_Wkv, L0_attn_Wo, L0_attn_bo, L0_ffn_router_W, L0_ffn_router_b, L0_ffn_sW1, L0_ffn_sb1, L0_ffn_sW2, L0_ffn_sb2, L0_ffn_eW1, L0_ffn_eb1, L0_ffn_eW2, L0_ffn_eb2, L0_c, L0_wmod, L1_attn_w_qs, L1_attn_w_ks, L1_attn_w_vs, L1_attn_w_rel_pos_k, L1_attn_rel_embed_bias, L1_attn_rel_pos_bias, L1_attn_w_out, L1_attn_b_out, L1_ffn_w12, L1_ffn_w3, L1_ffn_gate_w, L1_c, L1_wmod, L2_attn_Wqkv, L2_attn_Wproj, L2_ffn_gate_w1, L2_ffn_gate_b1, L2_ffn_gate_w2, L2_ffn_gate_b2, L2_ffn_W1, L2_ffn_b1, L2_ffn_W2, L2_ffn_b2, L2_ffn_TW1, L2_ffn_Tb1, L2_ffn_TW2, L2_ffn_Tb2, L2_c, L2_wmod, L3_attn_W_q, L3_attn_W_k, L3_attn_W_v, L3_attn_W_o, L3_ffn_router_w, L3_ffn_w_gate, L3_ffn_w_up, L3_ffn_w_down, L3_ffn_ws_gate, L3_ffn_ws_up, L3_ffn_ws_down, L3_c, L3_wmod):

    def _L0_attn_ref(x, Wq, Wkv, Wo, bo):
        import jax, jax.numpy as jnp
        import numpy as np
        HEADS = 16
        DIM_HEAD = 64
        EPS = 1e-08
        B, N, D = x.shape
        H, Dh = (HEADS, DIM_HEAD)
        scale = Dh ** (-0.5)
        q = (x @ Wq).reshape(B, N, H, Dh).transpose(0, 2, 1, 3)
        kv = x @ Wkv
        k = kv[..., :H * Dh].reshape(B, N, H, Dh).transpose(0, 2, 1, 3)
        v = kv[..., H * Dh:].reshape(B, N, H, Dh).transpose(0, 2, 1, 3)
        s = jnp.einsum('bhid,bhjd->bhij', q * scale, k)
        gm = jax.lax.stop_gradient(jnp.max(s, axis=-1, keepdims=True))
        causal_mask = jnp.triu(jnp.ones((N, N), bool), 1)
        p = jnp.where(causal_mask, 0.0, jnp.exp(s - gm))
        num = jnp.einsum('bhij,bhjd->bhid', p, v)
        out = num / (jnp.sum(p, axis=-1, keepdims=True) + EPS)
        out = out.transpose(0, 2, 1, 3).reshape(B, N, H * Dh)
        return out @ Wo + bo

    def _L0_ffn_ref(x, router_W, router_b, sW1, sb1, sW2, sb2, eW1, eb1, eW2, eb2):
        import jax, jax.numpy as jnp
        import numpy as np
        B, L, D = (2, 256, 128)
        E = 15
        H = D * 1
        K = 3
        T = 1.0
        b, l, d = x.shape
        n = b * l
        xt = x.reshape(n, d)
        shared = jax.nn.relu(xt @ sW1 + sb1) @ sW2 + sb2
        logits = xt @ router_W + router_b
        probs = jax.nn.softmax(logits / T, axis=-1)
        top_p, top_i = jax.lax.top_k(probs, K)
        cw = jnp.zeros((n, E), dtype=probs.dtype)
        cw = cw.at[jnp.arange(n)[:, None], top_i].set(top_p)
        h = jax.nn.relu(jnp.einsum('nd,edh->neh', xt, eW1) + eb1)
        ye = jnp.einsum('neh,ehd->ned', h, eW2) + eb2
        routed = jnp.einsum('ned,ne->nd', ye, cw)
        return (shared + routed).reshape(b, l, d)

    def _L1_attn_ref(q, w_qs, w_ks, w_vs, w_rel_pos_k, rel_embed_bias, rel_pos_bias, w_out, b_out):
        import math
        import jax, jax.numpy as jnp
        import numpy as np
        from jax.scipy.special import xlogy, gammaln

        def get_positional_embed(seq_len, feature_size):
            distances = jnp.arange(-seq_len + 1, seq_len, dtype=jnp.float32)
            n = feature_size // 6
            absd = jnp.abs(distances)[:, None]
            max_range = math.log(seq_len) / math.log(2.0)
            half_life = 2.0 ** jnp.linspace(3.0, max_range, n)
            feat_exp = jnp.exp(-math.log(2.0) / half_life[None, :] * absd)
            center_widths = 2.0 ** jnp.arange(1, n + 1, dtype=jnp.float32) - 1.0
            feat_cm = (center_widths[None, :] > absd).astype(jnp.float32)
            stddev = seq_len / (2.0 * n)
            start_mean = seq_len / n
            mean = jnp.linspace(start_mean, float(seq_len), n)[None, :]
            conc = (mean / stddev) ** 2
            rate = mean / stddev ** 2
            log_unnorm = xlogy(conc - 1.0, absd) - rate * absd
            log_norm = gammaln(conc) - conc * jnp.log(rate)
            probs = jnp.exp(log_unnorm - log_norm) + 1e-08
            feat_gamma = probs / jnp.max(probs, axis=-1, keepdims=True)
            emb = jnp.concatenate([feat_exp, feat_cm, feat_gamma], axis=-1)
            emb = jnp.concatenate([emb, jnp.sign(distances)[:, None] * emb], axis=-1)
            return emb

        def relative_shift(x):
            b, h, t1, t2m1 = x.shape
            x = jnp.pad(x, ((0, 0), (0, 0), (0, 0), (1, 0)))
            t2 = t2m1 + 1
            x = x.reshape(b, h, t2, t1)
            x = x[:, :, 1:, :]
            x = x.reshape(b, h, t1, t2 - 1)
            return x[..., :(t2 + 1) // 2]
        B, L, _ = q.shape
        H, Dk = (rel_embed_bias.shape[1], rel_embed_bias.shape[3])
        Dv = w_vs.shape[1] // H
        scale = Dk ** (-0.5)
        Q = (q @ w_qs).reshape(B, L, H, Dk).transpose(0, 2, 1, 3) * scale
        K = (q @ w_ks).reshape(B, L, H, Dk).transpose(0, 2, 1, 3)
        V = (q @ w_vs).reshape(B, L, H, Dv).transpose(0, 2, 1, 3)
        attn = jnp.einsum('bnqd,bnkd->bnqk', Q + rel_embed_bias, K)
        positions = get_positional_embed(L, w_rel_pos_k.shape[0])
        rel_k = (positions @ w_rel_pos_k).reshape(-1, H, Dk).transpose(1, 0, 2)
        attn_pos = jnp.einsum('bnqd,nkd->bnqk', Q + rel_pos_bias, rel_k)
        attn_pos = relative_shift(attn_pos)
        a = jax.nn.softmax(attn + attn_pos, axis=-1)
        out = jnp.einsum('bnqk,bnkd->bnqd', a, V)
        out = out.transpose(0, 2, 1, 3).reshape(B, L, H * Dv)
        return out @ w_out + b_out

    def _L1_ffn_ref(x, w12, w3, gate_w):
        import jax, jax.numpy as jnp
        import numpy as np
        TOP_K = 2
        E = gate_w.shape[0]
        H = w3.shape[-1]
        scores = jnp.einsum('btd,ed->bte', x, gate_w)
        topk_scores, topk_idx = jax.lax.top_k(scores, TOP_K)
        topk_probs = jax.nn.softmax(topk_scores, axis=-1)
        total_probs = jnp.sum(jax.nn.one_hot(topk_idx, E, dtype=topk_probs.dtype) * topk_probs[..., None], axis=-2)
        h12 = jnp.einsum('btd,ehd->bteh', x, w12)
        h1, h2 = (h12[..., :H], h12[..., H:])
        hidden = jax.nn.silu(h1) * h2
        expert_out = jnp.einsum('bteh,edh->bted', hidden, w3)
        y = jnp.sum(total_probs[..., None] * expert_out, axis=-2)
        return y

    def _L2_attn_ref(x, Wqkv, Wproj):
        import jax, jax.numpy as jnp
        import numpy as np
        import math
        N_HEAD = 16
        N_EMBD = 128
        HEAD_DIM = N_EMBD // N_HEAD
        ROPE_BASE = 10000.0

        def _rope_cos_sin(T, dh, dtype):
            inv_freq = 1.0 / ROPE_BASE ** (jnp.arange(0, dh, 2, dtype=jnp.float32) / dh)
            freqs = jnp.arange(T, dtype=jnp.float32)[:, None] * inv_freq[None, :]
            cos = jnp.repeat(jnp.cos(freqs), 2, axis=-1).astype(dtype)
            sin = jnp.repeat(jnp.sin(freqs), 2, axis=-1).astype(dtype)
            return (cos, sin)

        def _apply_rope(x, cos, sin):
            x_even = x[..., ::2]
            x_odd = x[..., 1::2]
            x_rot = jnp.stack((-x_odd, x_even), axis=-1).reshape(x.shape)
            return x * cos + x_rot * sin
        B, T, C = x.shape
        H, Dh = (N_HEAD, HEAD_DIM)
        qkv = x @ Wqkv
        q, k, v = jnp.split(qkv, 3, axis=-1)
        Q = q.reshape(B, T, H, Dh).transpose(0, 2, 1, 3)
        K = k.reshape(B, T, H, Dh).transpose(0, 2, 1, 3)
        V = v.reshape(B, T, H, Dh).transpose(0, 2, 1, 3)
        cos, sin = _rope_cos_sin(T, Dh, x.dtype)
        Q = _apply_rope(Q, cos, sin)
        K = _apply_rope(K, cos, sin)
        scores = jnp.einsum('bhqd,bhkd->bhqk', Q, K) / math.sqrt(Dh)
        causal = jnp.tril(jnp.ones((T, T), dtype=bool))
        scores = jnp.where(causal, scores, jnp.finfo(scores.dtype).min)
        attn = jax.nn.softmax(scores, axis=-1)
        y = jnp.einsum('bhqk,bhkd->bhqd', attn, V)
        y = y.transpose(0, 2, 1, 3).reshape(B, T, C)
        return y @ Wproj

    def _L2_ffn_ref(hidden_states, gate_w1, gate_b1, gate_w2, gate_b2, W1, b1, W2, b2, TW1, Tb1, TW2, Tb2):
        import jax, jax.numpy as jnp
        import numpy as np
        B, S, H, F, E = (8, 256, 128, 512, 8)
        INIT_LAMBDA = 0.2
        x = hidden_states
        h = jax.nn.relu(jnp.einsum('bsh,oh->bso', x, gate_w1) + gate_b1)
        g = jnp.einsum('bso,eo->bse', h, gate_w2) + gate_b2
        g = g.mean(axis=1)
        mW1 = W1 + jnp.einsum('be,efh->bfh', g, TW1)
        mb1 = b1 + g @ Tb1
        mW2 = W2 + jnp.einsum('be,ehf->bhf', g, TW2)
        mb2 = b2 + g @ Tb2
        u = jax.nn.gelu(jnp.einsum('bsh,bfh->bsf', x, mW1) + mb1[:, None, :])
        out = jnp.einsum('bsf,bhf->bsh', u, mW2) + mb2[:, None, :]
        return out

    def _L3_attn_ref(in_features, W_q, W_k, W_v, W_o):
        import jax, jax.numpy as jnp
        import numpy as np
        D_MODEL = 128
        NUM_HEADS = 16
        D_K = D_MODEL // NUM_HEADS
        ROPE_THETA = 10000.0
        MAX_SEQ_LEN = 256

        def _rope_tables():
            dim_index = jnp.arange(D_K // 2, dtype=jnp.float32)
            pos = jnp.arange(MAX_SEQ_LEN, dtype=jnp.float32)
            theta_inv = ROPE_THETA ** (-2.0 * dim_index / D_K)
            ang = pos[:, None] * theta_inv[None, :]
            return (jnp.sin(ang), jnp.cos(ang))

        def _apply_rope(x, positions, sin, cos):
            s = sin[positions]
            c = cos[positions]
            x_even = x[..., ::2]
            x_odd = x[..., 1::2]
            y_even = x_even * c - x_odd * s
            y_odd = x_even * s + x_odd * c
            y = jnp.stack([y_even, y_odd], axis=-1)
            return y.reshape(x.shape)
        B, S, _ = in_features.shape
        sin, cos = _rope_tables()
        positions = jnp.arange(S)

        def proj(W):
            y = jnp.einsum('bsd,od->bso', in_features, W)
            return y.reshape(B, S, NUM_HEADS, D_K).transpose(0, 2, 1, 3)
        Q = _apply_rope(proj(W_q), positions, sin, cos)
        K = _apply_rope(proj(W_k), positions, sin, cos)
        V = proj(W_v)
        scores = jnp.einsum('bhnd,bhmd->bhnm', Q, K) / jnp.sqrt(jnp.float32(D_K))
        causal = jnp.tril(jnp.ones((S, S), dtype=bool))
        scores = jnp.where(causal[None, None], scores, -jnp.inf)
        attn = jax.nn.softmax(scores, axis=-1)
        head = jnp.einsum('bhnm,bhmd->bhnd', attn, V)
        head = head.transpose(0, 2, 1, 3).reshape(B, S, D_MODEL)
        return jnp.einsum('bso,do->bsd', head, W_o.T.T) if False else jnp.einsum('bsi,oi->bso', head, W_o)

    def _L3_ffn_ref(hidden_states, router_w, w_gate, w_up, w_down, ws_gate, ws_up, ws_down):
        import jax, jax.numpy as jnp
        import numpy as np
        TOP_K = 6

        def _glu_mlp(x, wg, wu, wd):
            return jax.nn.silu(x @ wg) * (x @ wu) @ wd
        B, S, D = hidden_states.shape
        x = hidden_states.reshape(-1, D)
        scores = jax.nn.softmax(x @ router_w, axis=-1)
        topk_w, topk_idx = jax.lax.top_k(scores, TOP_K)
        g = jnp.einsum('td,edf->etf', x, w_gate)
        u = jnp.einsum('td,edf->etf', x, w_up)
        f_all = jnp.einsum('etf,efd->ted', jax.nn.silu(g) * u, w_down)
        picked = jnp.take_along_axis(f_all, topk_idx[:, :, None], axis=1)
        y = jnp.sum(picked * topk_w[:, :, None], axis=1).reshape(B, S, D)
        y = y + _glu_mlp(hidden_states, ws_gate, ws_up, ws_down)
        return y
    x = L0_attn_x
    mod = (_silu(L0_c) @ L0_wmod).reshape(L0_c.shape[0], 6, 1, -1)
    sa, ca, ga, sb, cb, gb = (mod[:, 0], mod[:, 1], mod[:, 2], mod[:, 3], mod[:, 4], mod[:, 5])
    ga = (2 * (ga >= 0) - 1) * jnp.maximum(jnp.abs(ga), 0.25)
    gb = (2 * (gb >= 0) - 1) * jnp.maximum(jnp.abs(gb), 0.25)
    h = _layernorm(x, axis=-1) * (1 + ca) + sa
    x = x + ga * _L0_attn_ref(h, L0_attn_Wq, L0_attn_Wkv, L0_attn_Wo, L0_attn_bo)
    h = _layernorm(x, axis=-1) * (1 + cb) + sb
    x = x + gb * _L0_ffn_ref(h, L0_ffn_router_W, L0_ffn_router_b, L0_ffn_sW1, L0_ffn_sb1, L0_ffn_sW2, L0_ffn_sb2, L0_ffn_eW1, L0_ffn_eb1, L0_ffn_eW2, L0_ffn_eb2)
    mod = (_silu(L1_c) @ L1_wmod).reshape(L1_c.shape[0], 6, 1, -1)
    sa, ca, ga, sb, cb, gb = (mod[:, 0], mod[:, 1], mod[:, 2], mod[:, 3], mod[:, 4], mod[:, 5])
    ga = (2 * (ga >= 0) - 1) * jnp.maximum(jnp.abs(ga), 0.25)
    gb = (2 * (gb >= 0) - 1) * jnp.maximum(jnp.abs(gb), 0.25)
    h = _layernorm(x, axis=-1) * (1 + ca) + sa
    x = x + ga * _L1_attn_ref(h, L1_attn_w_qs, L1_attn_w_ks, L1_attn_w_vs, L1_attn_w_rel_pos_k, L1_attn_rel_embed_bias, L1_attn_rel_pos_bias, L1_attn_w_out, L1_attn_b_out)
    h = _layernorm(x, axis=-1) * (1 + cb) + sb
    x = x + gb * _L1_ffn_ref(h, L1_ffn_w12, L1_ffn_w3, L1_ffn_gate_w)
    mod = (_silu(L2_c) @ L2_wmod).reshape(L2_c.shape[0], 6, 1, -1)
    sa, ca, ga, sb, cb, gb = (mod[:, 0], mod[:, 1], mod[:, 2], mod[:, 3], mod[:, 4], mod[:, 5])
    ga = (2 * (ga >= 0) - 1) * jnp.maximum(jnp.abs(ga), 0.25)
    gb = (2 * (gb >= 0) - 1) * jnp.maximum(jnp.abs(gb), 0.25)
    h = _layernorm(x, axis=-1) * (1 + ca) + sa
    x = x + ga * _L2_attn_ref(h, L2_attn_Wqkv, L2_attn_Wproj)
    h = _layernorm(x, axis=-1) * (1 + cb) + sb
    x = x + gb * _L2_ffn_ref(h, L2_ffn_gate_w1, L2_ffn_gate_b1, L2_ffn_gate_w2, L2_ffn_gate_b2, L2_ffn_W1, L2_ffn_b1, L2_ffn_W2, L2_ffn_b2, L2_ffn_TW1, L2_ffn_Tb1, L2_ffn_TW2, L2_ffn_Tb2)
    mod = (_silu(L3_c) @ L3_wmod).reshape(L3_c.shape[0], 6, 1, -1)
    sa, ca, ga, sb, cb, gb = (mod[:, 0], mod[:, 1], mod[:, 2], mod[:, 3], mod[:, 4], mod[:, 5])
    ga = (2 * (ga >= 0) - 1) * jnp.maximum(jnp.abs(ga), 0.25)
    gb = (2 * (gb >= 0) - 1) * jnp.maximum(jnp.abs(gb), 0.25)
    h = _layernorm(x, axis=-1) * (1 + ca) + sa
    x = x + ga * _L3_attn_ref(h, L3_attn_W_q, L3_attn_W_k, L3_attn_W_v, L3_attn_W_o)
    h = _layernorm(x, axis=-1) * (1 + cb) + sb
    x = x + gb * _L3_ffn_ref(h, L3_ffn_router_w, L3_ffn_w_gate, L3_ffn_w_up, L3_ffn_w_down, L3_ffn_ws_gate, L3_ffn_ws_up, L3_ffn_ws_down)
    return x

_drawn_inputs = setup_inputs


def setup_inputs(seed=0):
    import zlib

    import numpy as np

    out = dict(_drawn_inputs(seed))
    spreads = {'L0_ffn_router_b': (0.0, 0.8),
     'L0_ffn_sb1': (0.0, 0.8),
     'L0_ffn_sb2': (0.0, 0.1),
     'L0_ffn_eb1': (0.0, 0.8),
     'L0_ffn_eb2': (0.0, 0.8),
     'L2_ffn_gate_b1': (0.0, 0.8),
     'L2_ffn_gate_b2': (0.20000000298023224, 0.6)}
    factors = {'L0_attn_bo': 7.246,
     'L0_ffn_router_W': 8.0,
     'L0_ffn_sW1': 5.068,
     'L0_ffn_sW2': 4.188,
     'L0_ffn_eW1': 8.0,
     'L0_ffn_eW2': 8.0,
     'L1_attn_b_out': 7.107,
     'L2_ffn_gate_w1': 8.0,
     'L2_ffn_gate_w2': 8.0,
     'L2_ffn_W1': 3.699,
     'L2_ffn_b1': 8.0,
     'L2_ffn_W2': 3.622,
     'L2_ffn_b2': 8.0,
     'L2_ffn_TW1': 6.189,
     'L2_ffn_Tb1': 8.0,
     'L2_ffn_TW2': 6.188,
     'L2_ffn_Tb2': 8.0,
     'L3_ffn_router_w': 8.0,
     'L3_ffn_w_gate': 8.0,
     'L3_ffn_w_up': 8.0,
     'L3_ffn_w_down': 8.0,
     'L3_ffn_ws_gate': 8.0,
     'L3_ffn_ws_up': 8.0,
     'L3_ffn_ws_down': 8.0,
     'L3_attn_W_q': 2.751,
     'L3_attn_W_k': 2.722}
    for name, (base, spread) in spreads.items():
        noise = np.random.default_rng([zlib.crc32(name.encode()), seed]).standard_normal(out[name].shape)
        drawn = base * np.exp(spread * noise) if base else spread * noise
        out[name] = jnp.asarray(drawn.astype(out[name].dtype))
    for name, factor in factors.items():
        out[name] = (out[name] * factor).astype(out[name].dtype)
    return out
```

```python
import math
from contextlib import ExitStack

import numpy as np

import concourse.bass as bass
from concourse import mybir

F32 = mybir.dt.float32
BF16 = mybir.dt.bfloat16
ALU = mybir.AluOpType
ACT = mybir.ActivationFunctionType
AX_X = mybir.AxisListType.X

NB = 16
T = 256
P = 128
NT = T // P
LN_EPS = 1e-5
MASKED = -1e30
ARENA = 11264


class Step:

    def __init__(self, base, s, per):
        self.base, self.s, self.per = base, s, per
        self.item = base + s // per
        self.count = base * per + s
        self.p = s % per

    def shift(self, by):
        return Step(self.base, self.s + by, self.per)

    @property
    def real(self):
        return not isinstance(self.base, int) or 0 <= self.count < NB * self.per

    def ring(self, n):
        return self.s % n


def walk(eng, per, unroll, lead, lag, step):
    for s in range(-lead, unroll * per):
        step(Step(0, s, per))
    with eng.Fori(1, NB // unroll - 1) as lap:
        for s in range(unroll * per):
            step(Step(lap * unroll, s, per))
    for s in range((NB - unroll) * per, NB * per + lag):
        step(Step(0, s, per))


def wait(eng, sem, step, each=1, extra=0, item=False):
    if not step.real:
        return
    n = (step.item if item else step.count) * each + each - extra
    eng.wait_ge(sem, n)


def hold(dve, spare):
    dve.memset(spare, 0.0)


def wait_ring(eng, sems, step):
    if step.real:
        eng.wait_ge(sems[step.ring(len(sems))], (step.base * (step.per // len(sems)) + step.s // len(sems)) * 16 + 16)


def signals(nc, ctx, prefix, names):
    sems = {x: nc.alloc_semaphore(f"{prefix}{x}") for x in names}

    def give_back():
        nc.clear_and_free_semaphores(list(sems.values()))
        nc.all_engine_barrier(sem_only=True)

    ctx.callback(give_back)
    return sems


class Norms:

    def __init__(self, nc, ctx):
        def sb(name, shape):
            return ctx.enter_context(nc.sbuf_tensor(name, shape, F32))

        self.x = sb("x", [P, NB, NT, P])
        self.stats = sb("row_stats", [P, NB, NT, 6])
        self.mean = sb("row_mean", [P, NB, NT])
        self.half_gap = sb("row_half_gap", [P, NB, NT])
        self.m2 = sb("row_m2", [P, NB, NT])
        self.var = sb("row_var", [P, NB, NT])
        self.std = sb("row_std", [P, NB, NT])
        self.rstd = sb("row_rstd", [P, NB, NT])
        self.xn = sb("xn", [P, NT, P])
        self.delta = sb("delta", [P, NT, P])
        self.hT = sb("hT", [P, 2, T])


def var_of_rows(dve, n, chain, var_ready):
    s = n.stats
    dve.tensor_tensor(n.mean[:], s[:, :, :, 1], s[:, :, :, 4], ALU.add)
    dve.tensor_tensor(n.half_gap[:], s[:, :, :, 1], s[:, :, :, 4], ALU.subtract)
    dve.tensor_tensor(n.m2[:], s[:, :, :, 2], s[:, :, :, 5], ALU.add).then_inc(chain, 1)
    dve.wait_ge(chain, 1)
    dve.tensor_scalar(n.mean[:], n.mean[:], 0.5, None, ALU.mult)
    dve.tensor_scalar(n.m2[:], n.m2[:], 1.0 / P, LN_EPS, ALU.mult, ALU.add)
    dve.scalar_tensor_tensor(out=n.half_gap[:], in0=n.half_gap[:], scalar=0.25, in1=n.half_gap[:],
                             op0=ALU.mult, op1=ALU.mult).then_inc(chain, 1)
    dve.wait_ge(chain, 2)
    dve.tensor_tensor(n.var[:], n.m2[:], n.half_gap[:], ALU.add).then_inc(var_ready, 1)


def std_of_rows(act, n, var_ready, std_ready):
    act.wait_ge(var_ready, 1)
    act.activation(n.std[:], n.var[:], ACT.Sqrt).then_inc(std_ready, 1)


def rstd_of_rows(dve, n, std_ready, rstd_ready):
    dve.wait_ge(std_ready, 1)
    dve.reciprocal(n.rstd[:], n.std[:]).then_inc(rstd_ready, 1)
    dve.wait_ge(rstd_ready, 1)


def normalise(dve, n, at, xn_used, xn_ready):
    wait(dve, xn_used, at.shift(-at.per), item=True)
    for t in range(NT):
        k = dve.tensor_scalar(n.xn[:, t, :], n.x[:, at.item, t, :], n.mean[:, at.item, t:t + 1],
                              n.rstd[:, at.item, t:t + 1], ALU.subtract, ALU.mult)
    k.then_inc(xn_ready, 1)


def add_residual(dve, n, at, y, gate, bias, chain, per_item, y_used, chain0=2):
    k = at.item * per_item + chain0
    if bias is not None:
        dve.tensor_tensor(n.delta[:], y, bias, ALU.add).then_inc(chain, 1)
        dve.wait_ge(chain, k + 1)
        y, k = n.delta[:], k + 1
    g = gate[:, at.item, :].unsqueeze(1).to_broadcast([P, NT, P])
    dve.tensor_tensor(n.delta[:], y, g, ALU.mult).then_inc(chain, 1)
    if y_used is not None:
        y_used()
    dve.wait_ge(chain, k + 1)
    dve.tensor_tensor(n.x[:, at.item, :, :], n.x[:, at.item, :, :], n.delta[:],
                      ALU.add).then_inc(chain, 1)
    dve.wait_ge(chain, k + 2)
    for t in range(NT):
        k2 = dve.bn_stats(n.stats[:, at.item, t, :], n.x[:, at.item, t, :])
    return k2


def prologue(nc, d, k, first):
    with ExitStack() as ctx:
        n = k.norms
        cT = ctx.enter_context(nc.sbuf_tensor("cT", [P, 4 * NB], F32))
        silu_c = ctx.enter_context(nc.sbuf_tensor("silu_c", [P, 4 * NB], F32))
        wmod = ctx.enter_context(nc.sbuf_tensor("wmod", [P, 4, 6 * P], F32))
        mag = ctx.enter_context(nc.sbuf_tensor("gate_size", [NB, 8, P], F32))
        sign = ctx.enter_context(nc.sbuf_tensor("gate_sign", [NB, 8, P], F32))
        gates = ctx.enter_context(nc.sbuf_tensor("gates", [NB, 8, P], F32))
        maskf = ctx.enter_context(nc.sbuf_tensor("maskf", [P, P], F32))
        mod_ps, gate_ps = k.banks[0][:, 0:16 * NB], [k.banks[1 + h][0:NB, :] for h in range(2)]
        sems = signals(nc, ctx, "pro_", ("mod_in", "x_in", "consts_in", "silu", "mod_mm", "gates", "gate_abs",
                                         "gate_steps", "gates_out"))
        with nc.Block() as block:

            @block.sync
            def _(sp):
                sp.dma_start(cT[:], d["cT"]).then_inc(sems["mod_in"], 16)
                sp.dma_start(wmod[:], d["wmod"]).then_inc(sems["mod_in"], 16)
                for g in range(4):
                    sp.dma_start(n.x[:, 4 * g:4 * g + 4], d["x"].rearrange("b (t p) d -> p b t d", p=P)[:, 4 * g:4 * g + 4]
                                 ).then_inc(sems["x_in"], 16)
                sp.dma_start(k.ident[:], d["ident"]).then_inc(sems["consts_in"], 16)
                sp.dma_start(maskf[:], d["causal"]).then_inc(sems["consts_in"], 16)
                load_weights(sp, nc, k, d, first)
                sp.wait_ge(sems["gates"], 1)
                sp.dma_start(k.gates_dram, gates[:]).then_inc(sems["gates_out"], 16)
                sp.wait_ge(sems["gates_out"], 16)
                load_gate(sp, k, first)

            @block.scalar
            def _(act):
                act.wait_ge(sems["mod_in"], 32)
                act.activation(silu_c[:], cT[:], ACT.Silu).then_inc(sems["silu"], 1)
                act.wait_ge(sems["mod_mm"], 1)
                for h in range(2):
                    i = act.activation(mag[:, 4 * h:4 * h + 4, :], gate_ps[h].rearrange("b (s d) -> b s d", s=4), ACT.Abs)
                i.then_inc(sems["gate_abs"], 1)

            @block.tensor
            def _(pe):
                pe.wait_ge(sems["mod_in"], 32)
                pe.wait_ge(sems["silu"], 1)
                for layer in range(4):
                    c = silu_c[:, layer * NB:(layer + 1) * NB]
                    for j, kind in enumerate((0, 1, 3, 4)):
                        at = (layer * 4 + j) * NB
                        pe.matmul(mod_ps[:, at:at + NB], wmod[:, layer, kind * P:(kind + 1) * P], c,
                                  start=True, stop=True)
                    for j, kind in enumerate((2, 5)):
                        at = ((layer * 2 + j) % 4) * P
                        mm = pe.matmul(gate_ps[layer // 2][:, at:at + P], c,
                                       wmod[:, layer, kind * P:(kind + 1) * P], start=True, stop=True)
                mm.then_inc(sems["mod_mm"], 1)

            @block.vector
            def _(dve):
                dve.wait_ge(sems["mod_mm"], 1)
                m = mod_ps.rearrange("p (l j b) -> p l j b", l=8, j=2)
                dve.tensor_copy(k.mod[:, :, 0, :], m[:, :, 0, :])
                dve.tensor_scalar(k.mod[:, :, 1, :], m[:, :, 1, :], 1.0, None, ALU.add)
                dve.wait_ge(sems["gate_abs"], 1)
                for h in range(2):
                    g = gate_ps[h].rearrange("b (s d) -> b s d", s=4)
                    i = dve.tensor_scalar(sign[:, 4 * h:4 * h + 4, :], g, 0.0, 2.0, ALU.is_ge, ALU.mult)
                dve.tensor_scalar(mag[:], mag[:], 0.25, None, ALU.max).then_inc(sems["gate_steps"], 1)
                dve.wait_ge(sems["gate_steps"], 1)
                dve.scalar_tensor_tensor(out=gates[:], in0=sign[:], scalar=-1.0, in1=mag[:],
                                         op0=ALU.add, op1=ALU.mult).then_inc(sems["gates"], 1)
                dve.wait_ge(sems["consts_in"], 32)
                dve.tensor_copy(k.ident_bf[:], k.ident[:])
                dve.tensor_copy(k.causal_bf[:], maskf[:])
                for b in range(NB):
                    if b % 4 == 0:
                        dve.wait_ge(sems["x_in"], 4 * b + 16)
                    for t in range(NT):
                        dve.bn_stats(n.stats[:, b, t, :], n.x[:, b, t, :])


def load_gate(sp, k, phase):
    sp.dma_start(k.gate[phase % 2][:], k.gates_dram[:, phase, :].partition_broadcast(P)).then_inc(k.gate_in[phase], 16)


def load_weights(sp, nc, k, d, phase):
    at = 0
    for name, shape, parts in WEIGHTS[phase]:
        size = int(np.prod(shape))
        sp.dma_start(k.arena[phase % 2][0:parts, at:at + size], d[name]).then_inc(k.weights_in[phase], 16)
        at += size
    assert at <= ARENA


def weights(k, phase):
    at, views = 0, {}
    for name, shape, parts in WEIGHTS[phase]:
        size = int(np.prod(shape))
        v = k.arena[phase % 2][0:parts, at:at + size]
        if len(shape) == 2:
            v = v.rearrange("p (a b) -> p a b", a=shape[0])
        elif len(shape) == 3:
            v = v.rearrange("p (a b c) -> p a b c", a=shape[0], b=shape[1])
        views[name] = v
        at += size
    return views


class Shared:
    pass


ROPE_WEIGHTS = [[(f"wqk{x}", (4, P), P), (f"wv{x}", (P,), P), (f"wproj{x}", (P,), P), (f"rope_q{x}", (2, T), P),
                 (f"rope_k{x}", (2, T), P), (f"head_rows{x}", (P,), 16)]
                for x in (2, 3)]
WEIGHTS = [
    [("wqkv0", (3, 1024), P), ("wo0", (8, P), P), ("bo0", (P,), P)],
    [("e1w", (16, P), P), ("e2w", (16, P), P), ("e1b", (16,), P), ("rw", (15,), P), ("rb", (15,), P),
     ("e2b", (P,), 16)],
    [("wqkv1", (3, 1024), P), ("wo1", (8, P), P), ("bo1", (P,), P), ("qb1", (2, 8), P), ("w_rel", (2, 1024), 96),
     ("positions", (2, 512), 96)],
    [("w12", (8, 512), P), ("w3", (8, 2, P), P), ("gw1", (8,), P)],
    ROPE_WEIGHTS[0],
    [("base", (1156,), P), ("task", (8, 1156), P), ("gw1_2", (P,), P), ("gb1", (1,), P), ("gw2", (8,), P),
     ("gb2", (8,), P)],
    ROPE_WEIGHTS[1],
    [("gu", (5, 2, P), P), ("down", (4, 2 * P), P), ("shared", (P,), P), ("rw3", (8,), P)],
]


def causal_transposes(pe, pT, p, ident):
    for block in range(3):
        mm = pe.transpose(pT[:, block * P:(block + 1) * P], p[:, block * P:(block + 1) * P], ident)
    return mm


def modulated(act, k, phase, at, ps, hT, sem):
    act.activation(hT, ps, ACT.Identity, scale=k.mod[:, phase, 1, bass.ds(at.item, 1)],
                   bias=k.mod[:, phase, 0, bass.ds(at.item, 1)]).then_inc(sem, 1)


def attention0(nc, d, k):
    phase, PER = 0, 8
    n = k.norms
    w = weights(k, phase)
    EPS = 1e-8
    C = 3 * P
    with ExitStack() as ctx:
        def sb(name, shape):
            return ctx.enter_context(nc.sbuf_tensor("a0_" + name, shape, F32))

        qz = sb("qz", [P, 2, 2, T])
        kT = sb("kT", [P, 2, T])
        v = sb("v", [P, 4, NT, P])
        p = sb("p", [P, 2, 2, C])
        pT = sb("pT", [P, 2, 2, C])
        oT = sb("oT", [P, 2, T])
        nmax = sb("nmax", [P, 2, 2, NT])
        sums = sb("sums", [P, 2, 2, NT])
        den = sb("den", [P, 2, 2, NT])
        rec = sb("rec", [P, 2, 2, NT])
        qh_ps, kv_ps = k.banks[0], k.banks[1]
        s_ps, pT_ps = k.banks[2:4], k.banks[4:6]
        o_ps, y_ps = k.banks[6], k.banks[7]
        names = ("chain", "var", "std", "rstd", "xn", "ht_mm", "ht", "q_mm", "q", "kv_mm", "kv", "s_mm",
                 "nmax", "masked", "exp", "den", "rec", "p", "pT_mm", "pT0", "pT1", "o_mm", "oT", "y_mm", "res", "qz0")
        s = signals(nc, ctx, "a0_", names)
        LAST = PER - 1

        with nc.Block() as block:

            @block.sync
            def _(sp):
                prefetch(sp, nc, k, d, phase)

            @block.scalar
            def _(act):
                std_of_rows(act, n, s["var"], s["std"])

                def step(at):
                    nx, b1, b2 = at.shift(1), at.shift(-1), at.shift(-2)
                    if b2.real:
                        wait(act, s["o_mm"], b2)
                        wait(act, s["y_mm"], b2.shift(-2))
                        act.copy(oT[:, b2.ring(2), :], o_ps[:, 0:T]).then_inc(s["oT"], 1)
                    if nx.real:
                        wait(act, s["kv_mm"], nx)
                        wait(act, s["s_mm"], nx.shift(-2), 2)
                        act.copy(kT[:, nx.ring(2), :], kv_ps[:, 0:T])
                        wait(act, s["o_mm"], nx.shift(-4))
                        act.copy(v[:, nx.ring(4)], kv_ps[:, T:2 * T].rearrange("p (t d) -> p t d", t=NT)).then_inc(s["kv"], 1)
                    if at.p == 6:
                        ni = at.shift(2)
                        if ni.real:
                            wait(act, s["ht_mm"], ni, item=True)
                            modulated(act, k, phase, ni, qh_ps[:, T:2 * T], n.hT[:, 0, :], s["ht"])
                    if b1.real:
                        wait(act, s["pT_mm"], b1, 2)
                        wait(act, s["o_mm"], b1.shift(-2))
                        act.copy(pT[:, b1.ring(2), 1, :], pT_ps[1][:, 0:C]).then_inc(s["pT1"], 1)
                    if at.real:
                        r = at.ring(2)
                        for h in range(2):
                            wait(act, s["nmax"], at, 2, 1 - h)
                            wait(act, s["masked"], at, 2, 1 - h)
                            wait(act, s["pT_mm"], at.shift(-2), 2)
                            act.activation(p[:, r, h, 0:P], s_ps[h][:, 0:P], ACT.Exp,
                                           bias=nmax[:, r, h, 0:1], accum_out=sums[:, r, h, 0:1])
                            act.activation(p[:, r, h, P:C], s_ps[h][:, T:2 * T], ACT.Exp,
                                           bias=nmax[:, r, h, 1:2], accum_out=sums[:, r, h, 1:2]
                                           ).then_inc(s["exp"], 1)

                walk(act, PER, 1, 4, 3, step)

            @block.tensor
            def _(pe):
                pe.wait_ge(k.weights_in[phase], 16 * len(WEIGHTS[phase]))
                pe.wait_ge(s["qz0"], 1)

                def step(at):
                    nx, b1, b2 = at.shift(1), at.shift(-1), at.shift(-2)
                    if nx.real:
                        pe_ = nx.p * P
                        if nx.p == 0:
                            wait(pe, s["ht"], nx, item=True)
                        wait(pe, s["q"], nx.shift(-1))
                        pe.matmul(qh_ps[:, 0:T], w["wqkv0"][:, 0, pe_:pe_ + P], n.hT[:, 0, :], start=True,
                                  stop=True).then_inc(s["q_mm"], 1)
                        wait(pe, s["kv"], nx.shift(-1))
                        pe.matmul(kv_ps[:, 0:T], w["wqkv0"][:, 1, pe_:pe_ + P], n.hT[:, 0, :], start=True, stop=True)
                        for t in range(NT):
                            mm = pe.matmul(kv_ps[:, T + t * P:T + (t + 1) * P], n.hT[:, 0, t * P:(t + 1) * P],
                                           w["wqkv0"][:, 2, pe_:pe_ + P], start=True, stop=True)
                        mm.then_inc(s["kv_mm"], 1)
                    if at.real:
                        r = at.ring(2)
                        wait(pe, s["q"], at)
                        wait(pe, s["kv"], at)
                        for h in range(2):
                            wait(pe, s["exp"], at.shift(-1), 2, 1 - h)
                            pe.matmul(s_ps[h][:, 0:T], qz[:, r, h, 0:P], kT[:, r, :], start=True, stop=False,
                                      skip_group_check=True)
                            pe.matmul(s_ps[h][:, T:2 * T], qz[:, r, h, P:T], kT[:, r, :], start=False, stop=True,
                                      skip_group_check=True).then_inc(s["s_mm"], 1)
                    ni = at.shift(2)
                    if at.p == 6 and ni.real:
                        wait(pe, s["xn"], ni, item=True)
                        wait(pe, s["q"], nx)
                        for t in range(NT):
                            mm = pe.transpose(qh_ps[:, T + t * P:T + (t + 1) * P], n.xn[:, t, :], k.ident[:])
                        mm.then_inc(s["ht_mm"], 1)
                    if b1.real:
                        wait(pe, s["p"], b1)
                        wait(pe, s["pT0"], b1.shift(-1))
                        wait(pe, s["pT1"], b1.shift(-1))
                        for h in range(2):
                            causal_transposes(pe, pT_ps[h], p[:, b1.ring(2), h, :], k.ident[:]).then_inc(s["pT_mm"], 1)
                    if b2.real:
                        wait(pe, s["oT"], b2)
                        if b2.p == 0:
                            wait(pe, s["res"], b2.shift(-PER), item=True)
                        for t in range(NT):
                            mm = pe.matmul(y_ps[:, t * P:(t + 1) * P], oT[:, b2.ring(2), t * P:(t + 1) * P],
                                           w["wo0"][:, b2.p, :], start=(b2.p == 0 and t == 0),
                                           stop=(b2.p == LAST), skip_group_check=True)
                        mm.then_inc(s["y_mm"], 1)
                    if at.real:
                        for h in range(2):
                            wait(pe, s["nmax"], at, 2, 1 - h)
                            pe.matmul(s_ps[h][:, 0:P], k.ident_bf[:], k.causal_bf[:], start=False, stop=True,
                                      skip_group_check=True)
                            pe.matmul(s_ps[h][:, T + P:2 * T], k.ident_bf[:], k.causal_bf[:], start=False, stop=True,
                                      skip_group_check=True).then_inc(s["masked"], 1)
                    if b1.real:
                        wait(pe, s["pT0"], b1)
                        wait(pe, s["pT1"], b1)
                        wait(pe, s["kv"], b1)
                        wait(pe, s["oT"], b1.shift(-1))
                        r = b1.ring(2)
                        for j in range(NT):
                            for h in range(2):
                                mm = pe.matmul(o_ps[64 * h:64 * h + 64, j * P:T],
                                               v[:, b1.ring(4), j, 64 * h:64 * h + 64],
                                               pT[:, r, h, 0:T] if j == 0 else pT[:, r, h, T:C],
                                               start=(j == 0), stop=(j == 1), skip_group_check=True)
                        mm.then_inc(s["o_mm"], 1)

                walk(pe, PER, 1, 4, 3, step)

            @block.vector
            def _(dve):
                var_of_rows(dve, n, s["chain"], s["var"])
                dve.memset(qz[:], 0.0).then_inc(s["qz0"], 1)
                dve.wait_ge(s["qz0"], 1)
                rstd_of_rows(dve, n, s["std"], s["rstd"])
                dve.wait_ge(k.weights_in[phase], 16 * len(WEIGHTS[phase]))
                dve.wait_ge(k.gate_in[phase], 16)
                chain0 = 2

                def step(at):
                    nx, b1, b2 = at.shift(1), at.shift(-1), at.shift(-2)
                    if at.p == 4 and at.shift(4).real:
                        normalise(dve, n, at.shift(4), s["ht_mm"], s["xn"])
                    if b1.real:
                        r = b1.ring(2)
                        wait(dve, s["exp"], b1, 2)
                        dve.tensor_scalar(den[:, r], sums[:, r], EPS, None, ALU.add).then_inc(s["den"], 1)
                        wait(dve, s["den"], b1)
                        dve.reciprocal(rec[:, r], den[:, r]).then_inc(s["rec"], 1)
                        wait(dve, s["rec"], b1)
                        for h in range(2):
                            for t in range(NT):
                                c = p[:, r, h, 0:P] if t == 0 else p[:, r, h, P:C]
                                i = dve.tensor_scalar(c, c, rec[:, r, h, t:t + 1], None, ALU.mult)
                        i.then_inc(s["p"], 1)
                    if nx.real:
                        wait(dve, s["q_mm"], nx)
                        wait(dve, s["s_mm"], nx.shift(-2), 2)
                        for h in range(2):
                            i = dve.tensor_scalar(qz[64 * h:64 * h + 64, nx.ring(2), h, :],
                                                  qh_ps[64 * h:64 * h + 64, 0:T], 64 ** -0.5, None, ALU.mult)
                        i.then_inc(s["q"], 1)
                    if at.real:
                        for h in range(2):
                            wait(dve, s["s_mm"], at, 2, 1 - h)
                            wait(dve, s["exp"], at.shift(-2), 2)
                            dve.tensor_reduce(nmax[:, at.ring(2), h, :],
                                              s_ps[h][:].rearrange("p (t k) -> p t k", t=NT), AX_X, ALU.max,
                                              negate=True).then_inc(s["nmax"], 1)
                    if b1.real:
                        wait(dve, s["pT_mm"], b1, 2, 1)
                        wait(dve, s["o_mm"], b1.shift(-2))
                        dve.tensor_copy(pT[:, b1.ring(2), 0, :], pT_ps[0][:, 0:C]).then_inc(s["pT0"], 1)
                    b3 = at.shift(-2)
                    if b3.real and b3.p == LAST:
                        wait(dve, s["y_mm"], b3)
                        add_residual(dve, n, b3, y_ps[:, 0:T].rearrange("p (t d) -> p t d", t=NT), k.gate[phase % 2],
                                     w["bo0"].unsqueeze(1).to_broadcast([P, NT, P]), s["chain"], 3, None, chain0
                                     ).then_inc(s["res"], 1)

                walk(dve, PER, 1, 4, 3, step)


def prefetch(sp, nc, k, d, phase):
    if phase + 1 < len(WEIGHTS):
        load_weights(sp, nc, k, d, phase + 1)
        load_gate(sp, k, phase + 1)


def build(nc, d, out, phases, first=0):
    with ExitStack() as ctx:
        k = Shared()
        k.norms = Norms(nc, ctx)
        k.banks = [ctx.enter_context(nc.psum_tensor(f"bank{i}", [P, 512], F32)) for i in range(8)]
        k.ident = ctx.enter_context(nc.sbuf_tensor("ident", [P, P], F32))
        k.ident_bf = ctx.enter_context(nc.sbuf_tensor("ident_bf", [P, P], BF16))
        k.causal_bf = ctx.enter_context(nc.sbuf_tensor("causal_bf", [P, P], BF16))
        k.spare = ctx.enter_context(nc.sbuf_tensor("spare", [1, 1], F32))[:]
        k.mod = ctx.enter_context(nc.sbuf_tensor("mod", [P, 8, 2, NB], F32))
        k.gate = [ctx.enter_context(nc.sbuf_tensor(f"gate{i}", [P, NB, P], F32)) for i in range(2)]
        k.arena = [ctx.enter_context(nc.sbuf_tensor(f"arena{i}", [P, ARENA], F32)) for i in range(2)]
        k.gates_dram = nc.dram_tensor("gates_dram", (NB, 8, P), F32, kind="Internal").ap()
        k.weights_in = [ctx.enter_context(nc.semaphore(f"weights_in{i}")) for i in range(len(WEIGHTS))]
        k.gate_in = [ctx.enter_context(nc.semaphore(f"gate_in{i}")) for i in range(len(WEIGHTS))]
        stored = ctx.enter_context(nc.semaphore("stored"))
        prologue(nc, d, k, first)
        for f in phases:
            f(nc, d, k)
        with nc.Block() as block:

            @block.sync
            def _(sp):
                for g in range(4):
                    sp.dma_start(out.rearrange("b (t p) d -> p b t d", p=P)[:, 4 * g:4 * g + 4],
                                 k.norms.x[:, 4 * g:4 * g + 4]).then_inc(stored, 16)
                sp.wait_ge(stored, 64)


def start_norms(dve, n, s):
    var_of_rows(dve, n, s["chain"], s["var"])
    rstd_of_rows(dve, n, s["std"], s["rstd"])


def softmax_top(dve, s, spare, at, E, K, r, b, acc_each=1, transposed=True):
    k = at.item * 5

    def link(i, m):
        i.then_inc(s["top"], 1)
        dve.wait_ge(s["top"], k + m)

    wait(dve, s["rexp"], at, item=True)
    link(dve.reciprocal(b["rec"][:], b["sums"][:]), 1)
    for t in range(NT):
        i = dve.tensor_scalar(b["probs"][:, t, 0:E], b["e"][:, t, :], b["rec"][:, t:t + 1], None, ALU.mult)
    link(i, 2)
    hold(dve, spare)
    for t in range(NT):
        i = dve.max(b["max8"][:, t, :], b["probs"][:, t, :])
    link(i, 3)
    link(dve.tensor_copy(b["top"][:, :, 0:K], b["max8"][:, :, 0:K]), 4)
    hold(dve, spare)
    for t in range(NT):
        i = dve.match_replace(b["rest"][:, t, :], b["top"][:, t, :], b["probs"][:, t, :], 0.0)
    link(i, 5)
    before = at.shift(-at.per)
    wait(dve, s["acc"], before.shift(-before.p - 1), acc_each)
    if transposed:
        wait(dve, s["cwT_mm"], at.shift(-2 * at.per), item=True)
    dve.tensor_tensor(b["cw"][:, r, :, 0:E], b["probs"][:, :, 0:E], b["rest"][:, :, 0:E], ALU.subtract).then_inc(s["cw"], 1)


def router_tiles(nc, ctx, pre, E):
    b = {}

    def sb(name, *shape):
        b[name] = ctx.enter_context(nc.sbuf_tensor(pre + name, [P, *shape], F32))

    sb("logits", NT, E)
    sb("e", NT, E)
    sb("nmax", NT)
    sb("sums", NT)
    sb("rec", NT)
    sb("probs", NT, E + 8)
    sb("rest", NT, E + 8)
    sb("max8", NT, 8)
    sb("top", NT, 8)
    sb("cw", 2, NT, 16)
    return b


def ffn0(nc, d, k):
    phase, PER, E, K = 1, 16, 15, 3
    n = k.norms
    w = weights(k, phase)
    with ExitStack() as ctx:
        def sb(name, shape):
            return ctx.enter_context(nc.sbuf_tensor("f0_" + name, shape, F32))

        hidden = sb("hidden", [P, 2, T])
        acc = sb("acc", [P, NT, P])
        cwT = sb("cwT", [16, 2, T])
        b = router_tiles(nc, ctx, "f0_", E)
        h_ps, y_ps = k.banks[0:2], k.banks[2:4]
        ht_ps, rt_ps, cwT_ps = k.banks[4], k.banks[5], k.banks[6]
        names = ("chain", "var", "std", "rstd", "xn", "ht_mm", "ht", "rt_mm", "logits", "nmax", "rexp", "top", "cw",
                 "cwT_mm", "cwT", "h_mm", "hidden", "y_mm", "acc", "res", "pads")
        s = signals(nc, ctx, "f0_", names)
        LAST = PER - 1

        with nc.Block() as block:

            @block.sync
            def _(sp):
                prefetch(sp, nc, k, d, phase)

            @block.scalar
            def _(act):
                std_of_rows(act, n, s["var"], s["std"])
                act.wait_ge(k.weights_in[phase], 16 * len(WEIGHTS[phase]))

                def step(at):
                    nx, ni = at.shift(1), at.shift(PER)
                    if nx.real:
                        wait(act, s["h_mm"], nx)
                        wait(act, s["y_mm"], nx.shift(-2))
                        act.activation(hidden[:, nx.ring(2), :], h_ps[nx.ring(2)][:, 0:T], ACT.Relu,
                                       bias=w["e1b"][:, nx.p:nx.p + 1]).then_inc(s["hidden"], 1)
                    r = (at.s // PER + 1) % 2
                    if at.p == 6 and ni.real:
                        wait(act, s["ht_mm"], ni, item=True)
                        wait(act, s["h_mm"], at.shift(-7))
                        modulated(act, k, phase, ni, ht_ps[:, 0:T], n.hT[:, r, :], s["ht"])
                    if at.p == 9 and ni.real:
                        wait(act, s["nmax"], ni, item=True)
                        for t in range(NT):
                            i = act.activation(b["e"][:, t, :], b["logits"][:, t, :], ACT.Exp, bias=b["nmax"][:, t:t + 1],
                                               accum_out=b["sums"][:, t:t + 1])
                        i.then_inc(s["rexp"], 1)
                    if at.p == 13 and ni.real:
                        wait(act, s["cwT_mm"], ni, item=True)
                        wait(act, s["y_mm"], at.shift(-14))
                        act.copy(cwT[:, r, :], cwT_ps[0:16, 0:T]).then_inc(s["cwT"], 1)

                walk(act, PER, 2, 12, 1, step)

            @block.tensor
            def _(pe):
                pe.wait_ge(k.weights_in[phase], 16 * len(WEIGHTS[phase]))

                def step(at):
                    nx, ni = at.shift(1), at.shift(PER)
                    if nx.real:
                        if nx.p == 0:
                            wait(pe, s["ht"], nx, item=True)
                        wait(pe, s["hidden"], nx.shift(-2))
                        pe.matmul(h_ps[nx.ring(2)][:, 0:T], w["e1w"][:, nx.p, :], n.hT[:, nx.s // PER % 2, :],
                                  start=True, stop=True).then_inc(s["h_mm"], 1)
                    r = (at.s // PER + 1) % 2
                    if at.p == 6 and ni.real:
                        wait(pe, s["xn"], ni, item=True)
                        wait(pe, s["ht"], ni.shift(-PER), item=True)
                        for t in range(NT):
                            mm = pe.transpose(ht_ps[:, t * P:(t + 1) * P], n.xn[:, t, :], k.ident[:])
                        mm.then_inc(s["ht_mm"], 1)
                    if at.p == 8 and ni.real:
                        wait(pe, s["ht"], ni, item=True)
                        wait(pe, s["logits"], ni.shift(-PER), item=True)
                        for t in range(NT):
                            mm = pe.matmul(rt_ps[:, t * E:(t + 1) * E], n.hT[:, r, t * P:(t + 1) * P], w["rw"][:],
                                           start=True, stop=True)
                        mm.then_inc(s["rt_mm"], 1)
                    if at.p == 13 and ni.real:
                        wait(pe, s["cw"], ni, item=True)
                        wait(pe, s["cwT"], ni.shift(-PER), item=True)
                        for t in range(NT):
                            mm = pe.transpose(cwT_ps[0:16, t * P:(t + 1) * P], b["cw"][:, r, t, :], k.ident[:])
                        mm.then_inc(s["cwT_mm"], 1)
                    if at.real:
                        wait(pe, s["hidden"], at)
                        wait(pe, s["acc"], at.shift(-2))
                        last = at.p == LAST
                        if last:
                            wait(pe, s["cwT"], at, item=True)
                        for t in range(NT):
                            y = y_ps[at.ring(2)][:, t * P:(t + 1) * P]
                            mm = pe.matmul(y, hidden[:, at.ring(2), t * P:(t + 1) * P], w["e2w"][:, at.p, :],
                                           start=(t == 0), stop=not last, skip_group_check=True)
                            if last:
                                mm = pe.matmul(y, cwT[:, at.s // PER % 2, t * P:(t + 1) * P], w["e2b"][:],
                                               start=False, stop=True, skip_group_check=True)
                        mm.then_inc(s["y_mm"], 1)

                walk(pe, PER, 2, 12, 1, step)

            @block.vector
            def _(dve):
                start_norms(dve, n, s)
                dve.memset(b["probs"][:], -1.0)
                dve.memset(b["top"][:], -1.0)
                dve.memset(b["cw"][:], 1.0).then_inc(s["pads"], 1)
                dve.wait_ge(s["pads"], 1)
                dve.wait_ge(k.weights_in[phase], 16 * len(WEIGHTS[phase]))
                dve.wait_ge(k.gate_in[phase], 16)

                def step(at):
                    ni = at.shift(PER)
                    r = (at.s // PER + 1) % 2
                    if at.p == 4 and ni.real:
                        normalise(dve, n, ni, s["ht_mm"], s["xn"])
                    if at.p == 9 and ni.real:
                        wait(dve, s["rt_mm"], ni, item=True)
                        dve.tensor_tensor(b["logits"][:], rt_ps[:, 0:NT * E].rearrange("p (t e) -> p t e", t=NT),
                                          w["rb"][:].unsqueeze(1).to_broadcast([P, NT, E]), ALU.add).then_inc(s["logits"], 1)
                        wait(dve, s["logits"], ni, item=True)
                        dve.tensor_reduce(b["nmax"][:], b["logits"][:], AX_X, ALU.max, negate=True).then_inc(s["nmax"], 1)
                    if at.p == 11 and ni.real:
                        softmax_top(dve, s, k.spare, ni, E, K, r, b)
                    if at.real:
                        wait(dve, s["y_mm"], at)
                        wait(dve, s["acc"], at.shift(-1))
                        y, c = y_ps[at.ring(2)], b["cw"][:, at.s // PER % 2]
                        if at.p == 0:
                            wait(dve, s["cw"], at, item=True)
                            wait(dve, s["res"], at.shift(-PER), item=True)
                        if at.p == LAST:
                            dve.tensor_tensor(acc[:], acc[:], y[:, 0:T].rearrange("p (t d) -> p t d", t=NT),
                                              ALU.add).then_inc(s["acc"], 1)
                            wait(dve, s["acc"], at)
                            add_residual(dve, n, at, acc[:], k.gate[phase % 2], None, s["chain"], 2, None
                                         ).then_inc(s["res"], 1)
                            return
                        for t in range(NT):
                            a, z = acc[:, t, :], y[:, t * P:(t + 1) * P]
                            if at.p == 0:
                                i = dve.tensor_scalar(a, z, c[:, t, 0:1], None, ALU.mult)
                            else:
                                i = dve.scalar_tensor_tensor(out=a, in0=z, scalar=c[:, t, at.p:at.p + 1], in1=a,
                                                             op0=ALU.mult, op1=ALU.add)
                        i.then_inc(s["acc"], 1)

                walk(dve, PER, 2, 12, 1, step)


def attention1(nc, d, k):
    phase, PER = 2, 8
    n = k.norms
    w = weights(k, phase)
    SCALE = P ** -0.5
    SPAN = T + P - 1
    PITCH = SPAN + 1
    with ExitStack() as ctx:
        def sb(name, shape):
            return ctx.enter_context(nc.sbuf_tensor("a1_" + name, shape, F32))

        rel_k = sb("rel_k", [P, PER, 2 * T])
        q_c = sb("q_c", [P, 4, T])
        q_p = sb("q_p", [P, 2, T])
        kT = sb("kT", [P, 4, T])
        v = sb("v", [P, 4, NT, P])
        pos = sb("pos", [P, 2, NT, PITCH])
        shifted = sb("shifted", [P, 2, NT, T])
        sc = sb("sc", [P, 2, NT, T])
        p = sb("p", [P, 2, NT, T])
        pT = sb("pT", [P, 2, NT, T])
        oT = sb("oT", [P, 2, T])
        top = sb("top", [P, 2, NT])
        nmax = sb("nmax", [P, 2, NT])
        sums = sb("sums", [P, 2, NT])
        rec = sb("rec", [P, 2, NT])
        pos_dram = nc.dram_tensor("pos_dram", (4, NT, P, PITCH), F32, kind="Internal").ap()
        qh_ps, kv_ps, pos_ps = k.banks[0], k.banks[1], k.banks[2:4]
        s_ps, pT_ps, o_ps, y_ps = k.banks[4:8]
        names = ("chain", "var", "std", "rstd", "xn", "ht_mm", "ht", "rel_mm", "rel", "q_mm", "q", "kv_mm", "kv",
                 "pos_mm", "pos0", "pos1", "s_mm", "sc", "nmax", "exp", "rec", "p", "pT_mm",
                 "pT", "o_mm", "oT", "y_mm", "res")
        s = signals(nc, ctx, "a1_", names + tuple(f"{x}{i}" for x in ("written", "shifted") for i in range(4)))
        written, shifted_in = ([s[f"{x}{i}"] for i in range(4)] for x in ("written", "shifted"))
        LAST = PER - 1
        LEAD, LAG = 5, 3

        with nc.Block() as block:

            @block.sync
            def _(sp):
                prefetch(sp, nc, k, d, phase)

                def step(at):
                    n1, n2 = at.shift(1), at.shift(2)
                    if n1.real:
                        wait_ring(sp, written, n1)
                        start = n1.ring(4) * NT * P * PITCH + P - 1
                        skewed = bass.AP(pos_dram.tensor, start, [[PITCH - 1, P], [P * PITCH, NT], [1, T]])
                        sp.dma_start(shifted[:, n1.ring(2)], skewed).then_inc(shifted_in[n1.ring(4)], 16)
                    if n2.real:
                        wait(sp, s["pos0"], n2)
                        wait(sp, s["pos1"], n2)
                        sp.dma_start(pos_dram[n2.ring(4)].rearrange("t p c -> p t c")[:, :, 0:SPAN],
                                     pos[:, n2.ring(2), :, 0:SPAN]).then_inc(written[n2.ring(4)], 16)

                walk(sp, PER, 1, LEAD, LAG, step)

            @block.scalar
            def _(act):
                std_of_rows(act, n, s["var"], s["std"])
                for h in range(PER):
                    act.wait_ge(s["rel_mm"], h + 1)
                    act.copy(rel_k[:, h, 0:2 * T - 1], k.banks[h % 2][:, 0:2 * T - 1]).then_inc(s["rel"], 1)

                def step(at):
                    n2, b1, b2 = at.shift(2), at.shift(-1), at.shift(-2)
                    if b2.real:
                        wait(act, s["o_mm"], b2)
                        wait(act, s["y_mm"], b2.shift(-2))
                        act.copy(oT[:, b2.ring(2), :], o_ps[:, 0:T]).then_inc(s["oT"], 1)
                    if n2.real:
                        wait(act, s["kv_mm"], n2)
                        wait(act, s["o_mm"], n2.shift(-4))
                        act.copy(kT[:, n2.ring(4), :], kv_ps[:, 0:T])
                        act.copy(v[:, n2.ring(4)], kv_ps[:, T:2 * T].rearrange("p (t d) -> p t d", t=NT)
                                 ).then_inc(s["kv"], 1)
                    if at.p == 5:
                        ni = at.shift(3)
                        if ni.real:
                            wait(act, s["ht_mm"], ni, item=True)
                            modulated(act, k, phase, ni, qh_ps[:, T:2 * T], n.hT[:, 0, :], s["ht"])
                    if at.real:
                        r = at.ring(2)
                        wait(act, s["nmax"], at)
                        wait(act, s["pT_mm"], at.shift(-2))
                        for t in range(NT):
                            i = act.activation(p[:, r, t, :], sc[:, r, t, :], ACT.Exp, bias=nmax[:, r, t:t + 1],
                                               accum_out=sums[:, r, t:t + 1])
                        i.then_inc(s["exp"], 1)
                    if n2.real:
                        wait(act, s["pos_mm"], n2)
                        wait_ring(act, written, n2.shift(-2))
                        act.copy(pos[:, n2.ring(2), 0, 0:SPAN], pos_ps[0][:, 0:SPAN]).then_inc(s["pos0"], 1)

                walk(act, PER, 1, LEAD, LAG, step)

            @block.tensor
            def _(pe):
                pe.wait_ge(k.weights_in[phase], 16 * len(WEIGHTS[phase]))
                for h in range(PER):
                    if h >= 2:
                        pe.wait_ge(s["rel"], h - 1)
                    for c in range(2):
                        mm = pe.matmul(k.banks[h % 2][:, 0:2 * T - 1], w["w_rel"][:, c, h * P:(h + 1) * P],
                                       w["positions"][:, c, 0:2 * T - 1], start=(c == 0), stop=(c == 1))
                    mm.then_inc(s["rel_mm"], 1)
                pe.wait_ge(s["rel"], PER)

                def step(at):
                    n2, b1, b2 = at.shift(2), at.shift(-1), at.shift(-2)
                    if n2.real:
                        c = n2.p * P
                        if n2.p == 0:
                            wait(pe, s["ht"], n2, item=True)
                        wait(pe, s["q"], n2.shift(-1))
                        pe.matmul(qh_ps[:, 0:T], w["wqkv1"][:, 0, c:c + P], n.hT[:, 0, :], start=True,
                                  stop=True).then_inc(s["q_mm"], 1)
                        wait(pe, s["kv"], n2.shift(-1))
                        pe.matmul(kv_ps[:, 0:T], w["wqkv1"][:, 1, c:c + P], n.hT[:, 0, :], start=True, stop=True)
                        for t in range(NT):
                            mm = pe.matmul(kv_ps[:, T + t * P:T + (t + 1) * P], n.hT[:, 0, t * P:(t + 1) * P],
                                           w["wqkv1"][:, 2, c:c + P], start=True, stop=True)
                        mm.then_inc(s["kv_mm"], 1)
                    if at.real:
                        wait(pe, s["q"], at)
                        wait(pe, s["kv"], at)
                        wait(pe, s["sc"], at.shift(-1))
                        for t in range(NT):
                            mm = pe.matmul(s_ps[:, t * T:(t + 1) * T], q_c[:, at.ring(4), t * P:(t + 1) * P],
                                           kT[:, at.ring(4), :], start=True, stop=True)
                        mm.then_inc(s["s_mm"], 1)
                    ni = at.shift(3)
                    if at.p == 5 and ni.real:
                        wait(pe, s["xn"], ni, item=True)
                        wait(pe, s["q"], n2)
                        for t in range(NT):
                            mm = pe.transpose(qh_ps[:, T + t * P:T + (t + 1) * P], n.xn[:, t, :], k.ident[:])
                        mm.then_inc(s["ht_mm"], 1)
                    if b1.real:
                        wait(pe, s["p"], b1)
                        wait(pe, s["pT"], b1.shift(-1))
                        for j in range(NT):
                            for t in range(NT):
                                mm = pe.transpose(pT_ps[:, j * T + t * P:j * T + (t + 1) * P],
                                                  p[:, b1.ring(2), t, j * P:(j + 1) * P], k.ident[:])
                        mm.then_inc(s["pT_mm"], 1)
                    if b2.real:
                        wait(pe, s["oT"], b2)
                        if b2.p == 0:
                            wait(pe, s["res"], b2.shift(-PER), item=True)
                        for t in range(NT):
                            mm = pe.matmul(y_ps[:, t * P:(t + 1) * P], oT[:, b2.ring(2), t * P:(t + 1) * P],
                                           w["wo1"][:, b2.p, :], start=(b2.p == 0 and t == 0), stop=(b2.p == LAST),
                                           skip_group_check=True)
                        mm.then_inc(s["y_mm"], 1)
                    if n2.real:
                        wait(pe, s["q"], n2)
                        wait(pe, s["pos0"], n2.shift(-1))
                        wait(pe, s["pos1"], n2.shift(-1))
                        for t in range(NT):
                            first = P if t == 0 else 0
                            mm = pe.matmul(pos_ps[t][:, 0:SPAN], q_p[:, n2.ring(2), t * P:(t + 1) * P],
                                           rel_k[:, n2.p, first:first + SPAN], start=True, stop=True)
                        mm.then_inc(s["pos_mm"], 1)
                    if b1.real:
                        wait(pe, s["pT"], b1)
                        wait(pe, s["kv"], b1)
                        wait(pe, s["oT"], b1.shift(-1))
                        for j in range(NT):
                            mm = pe.matmul(o_ps[:, 0:T], v[:, b1.ring(4), j, :], pT[:, b1.ring(2), j, :],
                                           start=(j == 0), stop=(j == 1))
                        mm.then_inc(s["o_mm"], 1)

                walk(pe, PER, 1, LEAD, LAG, step)

            @block.vector
            def _(dve):
                start_norms(dve, n, s)
                dve.wait_ge(k.weights_in[phase], 16 * len(WEIGHTS[phase]))
                dve.wait_ge(k.gate_in[phase], 16)

                def step(at):
                    n2, b1, b2 = at.shift(2), at.shift(-1), at.shift(-2)
                    if at.p == 3 and at.shift(5).real:
                        normalise(dve, n, at.shift(5), s["ht_mm"], s["xn"])
                    if b1.real:
                        r = b1.ring(2)
                        wait(dve, s["exp"], b1)
                        dve.reciprocal(rec[:, r], sums[:, r]).then_inc(s["rec"], 1)
                        wait(dve, s["rec"], b1)
                        for t in range(NT):
                            i = dve.tensor_scalar(p[:, r, t, :], p[:, r, t, :], rec[:, r, t:t + 1], None, ALU.mult)
                        i.then_inc(s["p"], 1)
                    if n2.real:
                        wait(dve, s["q_mm"], n2)
                        wait(dve, s["s_mm"], n2.shift(-4))
                        wait(dve, s["pos_mm"], n2.shift(-2))
                        dve.tensor_scalar(q_c[:, n2.ring(4), :], qh_ps[:, 0:T], SCALE, w["qb1"][:, 0, n2.p:n2.p + 1],
                                          ALU.mult, ALU.add)
                        dve.tensor_scalar(q_p[:, n2.ring(2), :], qh_ps[:, 0:T], SCALE, w["qb1"][:, 1, n2.p:n2.p + 1],
                                          ALU.mult, ALU.add).then_inc(s["q"], 1)
                    if at.real:
                        r = at.ring(2)
                        wait(dve, s["s_mm"], at)
                        wait_ring(dve, shifted_in, at)
                        wait(dve, s["exp"], at.shift(-2))
                        hold(dve, k.spare)
                        for t in range(NT):
                            i = dve.tensor_tensor_reduce(sc[:, r, t, :], s_ps[:, t * T:(t + 1) * T],
                                                         shifted[:, r, t, :], 1.0, -3e38, ALU.add, ALU.max,
                                                         top[:, r, t:t + 1])
                        i.then_inc(s["sc"], 1)
                        wait(dve, s["sc"], at)
                        dve.tensor_scalar(nmax[:, r], top[:, r], -1.0, None, ALU.mult).then_inc(s["nmax"], 1)
                    if b1.real:
                        wait(dve, s["pT_mm"], b1)
                        wait(dve, s["o_mm"], b1.shift(-2))
                        dve.tensor_copy(pT[:, b1.ring(2)], pT_ps[:].rearrange("p (j q) -> p j q", j=NT)
                                        ).then_inc(s["pT"], 1)
                    if b2.real and b2.p == LAST:
                        wait(dve, s["y_mm"], b2)
                        add_residual(dve, n, b2, y_ps[:, 0:T].rearrange("p (t d) -> p t d", t=NT), k.gate[phase % 2],
                                     w["bo1"].unsqueeze(1).to_broadcast([P, NT, P]), s["chain"], 3, None
                                     ).then_inc(s["res"], 1)
                    if n2.real:
                        wait(dve, s["pos_mm"], n2)
                        wait_ring(dve, written, n2.shift(-2))
                        dve.tensor_copy(pos[:, n2.ring(2), 1, 0:SPAN], pos_ps[1][:, 0:SPAN]).then_inc(s["pos1"], 1)

                walk(dve, PER, 1, LEAD, LAG, step)


def ffn1(nc, d, k):
    phase, PER, E = 3, 8, 8
    n = k.norms
    w = weights(k, phase)
    LOWEST = -3e38
    with ExitStack() as ctx:
        def sb(name, shape):
            return ctx.enter_context(nc.sbuf_tensor("f1_" + name, shape, F32))

        silu = sb("silu", [P, 2, 2 * T])
        hidden = sb("hidden", [P, 2, 2 * T])
        acc = sb("acc", [P, NT, P])
        logits = sb("logits", [P, NT, 2 * E])
        max8 = sb("max8", [P, NT, 8])
        top = sb("top", [P, 2, NT, 8])
        rest = sb("rest", [P, 2, NT, 2 * E])
        is_top = sb("is_top", [P, 2, NT, E])
        gap = sb("gap", [P, NT])
        tilt = sb("tilt", [P, NT])
        second = sb("second", [P, NT])
        part = sb("part", [P, NT, E])
        cw = sb("cw", [P, 2, NT, E])
        h1_ps, h2_ps, y_ps = k.banks[0:2], k.banks[2:4], k.banks[4:6]
        ht_ps, rt_ps = k.banks[6:8]
        names = ("chain", "var", "std", "rstd", "xn", "ht_mm", "ht", "rt_mm", "logits", "gap", "tilt", "top", "cw",
                 "h1_mm", "h2_mm", "silu", "hidden", "y_mm", "acc", "res", "pads")
        s = signals(nc, ctx, "f1_", names)
        LAST, LEAD, LAG = PER - 1, 8, 1

        with nc.Block() as block:

            @block.sync
            def _(sp):
                prefetch(sp, nc, k, d, phase)

            @block.scalar
            def _(act):
                std_of_rows(act, n, s["var"], s["std"])

                def step(at):
                    nx, ni = at.shift(1), at.shift(PER)
                    if nx.real:
                        wait(act, s["h1_mm"], nx)
                        wait(act, s["hidden"], nx.shift(-2))
                        act.activation(silu[:, nx.ring(2), :], h1_ps[nx.ring(2)][:], ACT.Silu).then_inc(s["silu"], 1)
                    if at.p == 2 and ni.real:
                        wait(act, s["ht_mm"], ni, item=True)
                        wait(act, s["h2_mm"], at.shift(-3))
                        modulated(act, k, phase, ni, ht_ps[:, 0:T], n.hT[:, (at.s // PER + 1) % 2, :], s["ht"])
                    if at.p == 4 and ni.real:
                        wait(act, s["gap"], ni, item=True)
                        act.activation(tilt[:], gap[:], ACT.Tanh, scale=0.5).then_inc(s["tilt"], 1)

                walk(act, PER, 2, LEAD, LAG, step)

            @block.tensor
            def _(pe):
                pe.wait_ge(k.weights_in[phase], 16 * len(WEIGHTS[phase]))

                def step(at):
                    nx, ni = at.shift(1), at.shift(PER)
                    if nx.real:
                        if nx.p == 0:
                            wait(pe, s["ht"], nx, item=True)
                        hT = n.hT[:, nx.s // PER % 2, :]
                        wait(pe, s["silu"], nx.shift(-2))
                        for c in range(2):
                            mm = pe.matmul(h1_ps[nx.ring(2)][:, c * T:(c + 1) * T], w["w12"][:, nx.p, c * P:(c + 1) * P],
                                           hT, start=True, stop=True)
                        mm.then_inc(s["h1_mm"], 1)
                        wait(pe, s["hidden"], nx.shift(-2))
                        for c in range(2):
                            mm = pe.matmul(h2_ps[nx.ring(2)][:, c * T:(c + 1) * T],
                                           w["w12"][:, nx.p, T + c * P:T + (c + 1) * P], hT, start=True, stop=True)
                        mm.then_inc(s["h2_mm"], 1)
                    if at.p == 1 and ni.real:
                        wait(pe, s["xn"], ni, item=True)
                        wait(pe, s["ht"], ni.shift(-PER), item=True)
                        for t in range(NT):
                            mm = pe.transpose(ht_ps[:, t * P:(t + 1) * P], n.xn[:, t, :], k.ident[:])
                        mm.then_inc(s["ht_mm"], 1)
                    if at.p == 3 and ni.real:
                        wait(pe, s["ht"], ni, item=True)
                        wait(pe, s["logits"], ni.shift(-PER), item=True)
                        for t in range(NT):
                            mm = pe.matmul(rt_ps[:, t * E:(t + 1) * E],
                                           n.hT[:, (at.s // PER + 1) % 2, t * P:(t + 1) * P], w["gw1"][:],
                                           start=True, stop=True)
                        mm.then_inc(s["rt_mm"], 1)
                    if at.real:
                        wait(pe, s["hidden"], at)
                        wait(pe, s["acc"], at.shift(-2))
                        for t in range(NT):
                            for c in range(2):
                                mm = pe.matmul(y_ps[at.ring(2)][:, t * P:(t + 1) * P],
                                               hidden[:, at.ring(2), c * T + t * P:c * T + (t + 1) * P],
                                               w["w3"][:, at.p, c, :], start=(c == 0), stop=(c == 1))
                        mm.then_inc(s["y_mm"], 1)

                walk(pe, PER, 2, LEAD, LAG, step)

            @block.vector
            def _(dve):
                start_norms(dve, n, s)
                dve.memset(logits[:], LOWEST)
                dve.memset(top[:], LOWEST).then_inc(s["pads"], 1)
                dve.wait_ge(s["pads"], 1)
                dve.wait_ge(k.gate_in[phase], 16)

                def step(at):
                    nx, ni = at.shift(1), at.shift(PER)
                    if at.p == 0 and ni.real:
                        normalise(dve, n, ni, s["ht_mm"], s["xn"])
                    if nx.real:
                        wait(dve, s["silu"], nx)
                        wait(dve, s["h2_mm"], nx)
                        wait(dve, s["y_mm"], nx.shift(-2))
                        dve.tensor_tensor(hidden[:, nx.ring(2), :], silu[:, nx.ring(2), :], h2_ps[nx.ring(2)][:],
                                          ALU.mult).then_inc(s["hidden"], 1)
                    steps = ni.item * 4

                    def link(i, m):
                        i.then_inc(s["top"], 1)
                        dve.wait_ge(s["top"], steps + m)

                    if at.p == 3 and ni.real:
                        wait(dve, s["rt_mm"], ni, item=True)
                        dve.tensor_copy(logits[:, :, 0:E], rt_ps[:, 0:NT * E].rearrange("p (t e) -> p t e", t=NT)
                                        ).then_inc(s["logits"], 1)
                        wait(dve, s["logits"], ni, item=True)
                        hold(dve, k.spare)
                        for t in range(NT):
                            i = dve.max(max8[:, t, :], logits[:, t, :])
                        link(i, 1)
                        dve.tensor_tensor(gap[:], max8[:, :, 0], max8[:, :, 1], ALU.subtract).then_inc(s["gap"], 1)
                        dve.tensor_copy(top[:, 0, :, 0:1], max8[:, :, 0:1])
                        link(dve.tensor_copy(top[:, 1, :, 0:2], max8[:, :, 0:2]), 2)
                        hold(dve, k.spare)
                        for m in range(2):
                            for t in range(NT):
                                i = dve.match_replace(rest[:, m, t, :], top[:, m, t, :], logits[:, t, :], LOWEST)
                        link(i, 3)
                    if at.p == 5 and ni.real:
                        wait(dve, s["tilt"], ni, item=True)
                        for m in range(2):
                            dve.tensor_tensor(is_top[:, m], rest[:, m, :, 0:E], logits[:, :, 0:E], ALU.not_equal)
                        link(dve.tensor_scalar(second[:], tilt[:], -0.5, 0.5, ALU.mult, ALU.add), 4)
                        wait(dve, s["acc"], Step(at.base, at.s - at.p - 1, PER))
                        for t in range(NT):
                            i = dve.tensor_scalar(part[:, t, :], is_top[:, 1, t, :], second[:, t:t + 1], None, ALU.mult)
                        i.then_inc(s["cw"], 1)
                        dve.wait_ge(s["cw"], 2 * ni.item + 1)
                        for t in range(NT):
                            i = dve.scalar_tensor_tensor(out=cw[:, (at.s // PER + 1) % 2, t, :], in0=is_top[:, 0, t, :],
                                                         scalar=tilt[:, t:t + 1], in1=part[:, t, :], op0=ALU.mult,
                                                         op1=ALU.add)
                        i.then_inc(s["cw"], 1)
                    if at.real:
                        wait(dve, s["y_mm"], at)
                        wait(dve, s["acc"], at.shift(-1))
                        c = cw[:, at.s // PER % 2]
                        if at.p == 0:
                            wait(dve, s["cw"], at, 2, item=True)
                            wait(dve, s["res"], at.shift(-PER), item=True)
                        for t in range(NT):
                            a, z = acc[:, t, :], y_ps[at.ring(2)][:, t * P:(t + 1) * P]
                            if at.p == 0:
                                i = dve.tensor_scalar(a, z, c[:, t, 0:1], None, ALU.mult)
                            else:
                                i = dve.scalar_tensor_tensor(out=a, in0=z, scalar=c[:, t, at.p:at.p + 1], in1=a,
                                                             op0=ALU.mult, op1=ALU.add)
                        i.then_inc(s["acc"], 1)
                        if at.p == LAST:
                            wait(dve, s["acc"], at)
                            add_residual(dve, n, at, acc[:], k.gate[phase % 2], None, s["chain"], 2, None
                                         ).then_inc(s["res"], 1)

                walk(dve, PER, 2, LEAD, LAG, step)


def rope_attention(nc, d, k, phase):
    PER, H, DH, PARTS = 8, 16, 8, 3
    ROWS = DH * sum(PARTS - a for a in range(PARTS))
    n = k.norms
    w = weights(k, phase)
    for name in list(w):
        w[name[:-1]] = w[name]
    C = 3 * P
    with ExitStack() as ctx:
        def sb(name, shape):
            return ctx.enter_context(nc.sbuf_tensor(f"a{phase}_{name}", shape, F32))

        terms = sb("terms", [P, 2, 2, T])
        rotated = sb("rotated", [P, 2, T])
        rest = sb("rest", [P, 2, T])
        cut = ctx.enter_context(nc.sbuf_tensor(f"a{phase}_cut", [P, PARTS, 2, T], BF16))
        stack = ctx.enter_context(nc.sbuf_tensor(f"a{phase}_stack", [ROWS, 2, 2, H, T], BF16))
        v = sb("v", [P, 2, NT, H, 32])
        p = sb("p", [P, 2, 2, C])
        pT = sb("pT", [P, 2, 2, C])
        o = sb("o", [P, T])
        oT = sb("oT", [P, T])
        nmax = sb("nmax", [P, 2, 2, NT])
        sums = sb("sums", [P, 2, NT, H])
        rec = sb("rec", [P, NT, H])
        recT = sb("recT", [H, T])
        scale = sb("scale", [P, T])
        cut_dram = nc.dram_tensor(f"cut_dram{phase}", (2, PARTS, 2, DH * H, T), BF16, kind="Internal").ap()
        misc_ps, o_ps = k.banks[0:2]
        s_ps, pT_ps = (k.banks[2:4], k.banks[4:6]), k.banks[6:8]
        names = ("chain", "var", "std", "rstd", "xn", "ht_mm", "ht", "q_mm", "q_terms", "k_mm", "k_terms", "cut",
                 "written_q", "written_k", "stacked0", "stacked1", "v_mm", "v", "s_mm", "nmax", "exp", "pT_mm", "pT0", "pT1", "o_mm", "o",
                 "rec", "recT_mm", "recT", "scale_mm", "scale", "oT", "y_mm", "res", "v0")
        s = signals(nc, ctx, f"a{phase}_", names)
        stacked, written = [s["stacked0"], s["stacked1"]], [s["written_q"], s["written_k"]]
        LEAD, LAG = 2 * PER - 3, 5

        def place(at):
            return at.s // PER % 2

        def diagonal(at, t):
            whole = v[:, place(at), t]
            return bass.AP(whole.tensor, whole.offset, [list(whole.ap[0]), [4 * 32, 4], [32 + DH, 4], [1, DH]])

        with nc.Block() as block:

            @block.sync
            def _(sp):
                prefetch(sp, nc, k, d, phase)
                ROW = H * DH * T

                def step(at):
                    ni = at.shift(PER)
                    for which in range(2):
                        if at.p == 1 + 2 * which and ni.real:
                            wait(sp, s["cut"], ni, 10, 5 - 5 * which, item=True)
                            sp.dma_start(cut_dram[place(ni), :, which].rearrange("a r t -> r a t"), cut[:, :, which]
                                         ).then_inc(written[which], 16)
                        if at.p == 2 + 2 * which and ni.real:
                            wait(sp, written[which], ni, 16, item=True)
                            row = 0
                            for a in range(PARTS):
                                rows = (PARTS - a) * DH
                                start = (place(ni) * PARTS * 2 + (1 if which else 2 * a)) * ROW
                                src = bass.AP(cut_dram.tensor, start,
                                              [[2 * ROW if which else 0, PARTS - a], [H * T, DH], [1, H * T]])
                                sp.dma_start(stack[row:row + rows, place(ni), which].rearrange("r h t -> r (h t)"), src
                                             ).then_inc(stacked[place(ni)], 16)
                                row += rows

                walk(sp, PER, 2, LEAD, LAG, step)

            @block.gpsimd
            def _(pool):
                def cut_up(which, at, terms_ready):
                    def link(i, m):
                        i.then_inc(s["cut"], 1)
                        if m < 5:
                            pool.wait_ge(s["cut"], at.item * 10 + 5 * which + m)

                    wait(pool, terms_ready, at, item=True)
                    wait(pool, written[which], at.shift(-PER), 16, item=True)
                    x, y, c = terms[:, which, 0, :], terms[:, which, 1, :], cut[:, :, which, :]
                    link(pool.tensor_tensor(c[:, 0], x, y, ALU.add), 1)
                    link(pool.tensor_tensor(rotated[:, which], x, y, ALU.add), 2)
                    link(pool.tensor_tensor(rest[:, which], rotated[:, which], c[:, 0], ALU.subtract), 3)
                    link(pool.tensor_tensor(c[:, 1], rotated[:, which], c[:, 0], ALU.subtract), 4)
                    link(pool.tensor_tensor(c[:, 2], rest[:, which], c[:, 1], ALU.subtract), 5)

                def step(at):
                    ni, pi, ni2 = at.shift(PER), at.shift(-PER), at.shift(2 * PER)
                    if at.p == 7 and ni2.real:
                        cut_up(0, ni2, s["q_terms"])
                    if at.p == 0 and ni.real:
                        cut_up(1, ni, s["k_terms"])
                    if at.p == 2 and pi.real:
                        wait(pool, s["o"], pi, item=True)
                        wait(pool, s["scale"], pi, item=True)
                        wait(pool, s["y_mm"], pi.shift(-PER), item=True)
                        pool.tensor_tensor(oT[:], o[:], scale[:], ALU.mult).then_inc(s["oT"], 1)

                walk(pool, PER, 2, LEAD, LAG, step)

            @block.scalar
            def _(act):
                std_of_rows(act, n, s["var"], s["std"])
                act.wait_ge(s["v0"], 1)

                def step(at):
                    b1, ni, ni2, pi = at.shift(-1), at.shift(PER), at.shift(2 * PER), at.shift(-PER)
                    def exps(h):
                        r, head = at.ring(2), at.p + 8 * h
                        wait(act, s["nmax"], at, 2, 1 - h)
                        for t in range(NT):
                            c = slice(0, P) if t == 0 else slice(P, C)
                            i = act.activation(p[:, r, h, c], s_ps[at.ring(2)][h][:, c], ACT.Exp,
                                               bias=nmax[:, r, h, t:t + 1],
                                               accum_out=sums[:, place(at), t, head:head + 1])
                        i.then_inc(s["exp"], 1)

                    if at.real:
                        if at.p == 0:
                            wait(act, s["rec"], at.shift(-2 * PER), item=True)
                        wait(act, s["pT_mm"], at.shift(-2), 2)
                        exps(0)
                    if b1.real:
                        wait(act, s["pT_mm"], b1, 2)
                        wait(act, s["o_mm"], b1.shift(-2))
                        act.copy(pT[:, b1.ring(2), 1, :], pT_ps[1][:, 0:C]).then_inc(s["pT1"], 1)
                    if at.p == 1 and pi.real:
                        wait(act, s["recT_mm"], pi, item=True)
                        wait(act, s["scale_mm"], pi.shift(-PER), item=True)
                        act.copy(recT[:], misc_ps[0:H, 0:T]).then_inc(s["recT"], 1)
                    if at.p == 2 and pi.real:
                        wait(act, s["scale_mm"], pi, item=True)
                        wait(act, s["oT"], pi.shift(-PER), item=True)
                        act.copy(scale[:], misc_ps[:, T:2 * T]).then_inc(s["scale"], 1)
                    if at.p == 5 and ni.real:
                        wait(act, s["v_mm"], ni, item=True)
                        for t in range(NT):
                            i = act.copy(diagonal(ni, t),
                                         misc_ps[:, t * P:(t + 1) * P].rearrange("p (g r c) -> p g r c", g=4, r=4))
                        i.then_inc(s["v"], 1)
                    if at.p == 6 and ni2.real:
                        wait(act, s["ht_mm"], ni2, item=True)
                        wait(act, s["v_mm"], ni, item=True)
                        modulated(act, k, phase, ni2, misc_ps[:, T:2 * T], n.hT[:, 0, :], s["ht"])
                    if at.real:
                        exps(1)

                walk(act, PER, 2, LEAD, LAG, step)

            @block.tensor
            def _(pe):
                pe.wait_ge(k.weights_in[phase], 16 * len(WEIGHTS[phase]))

                def projections(at, which, sem):
                    for c in range(2):
                        mm = pe.matmul(misc_ps[:, c * T:(c + 1) * T], w["wqk"][:, 2 * which + c, :], n.hT[:, 0, :],
                                       start=True, stop=True)
                    mm.then_inc(sem, 1)

                def step(at):
                    b1, b2, ni, pi = at.shift(-1), at.shift(-2), at.shift(PER), at.shift(-PER)
                    ni2, n1 = at.shift(2 * PER), at.shift(1)
                    if n1.real and n1.p == 0:
                        i = n1.s // PER
                        pe.wait_ge(stacked[i % 2], at.base * (2 * PARTS * 16 // 2) + (i // 2 + 1) * (2 * PARTS * 16))
                    for h in range(2):
                        if b1.real:
                            wait(pe, s[("pT0", "pT1")[h]], b1.shift(-1))
                            wait(pe, s["exp"], b1, 2, 1 - h)
                            causal_transposes(pe, pT_ps[h], p[:, b1.ring(2), h, :], k.ident[:]).then_inc(s["pT_mm"], 1)
                        if n1.real:
                            q, keys = (stack[:, place(n1), which, n1.p + 8 * h, :] for which in range(2))
                            bank = s_ps[n1.ring(2)][h]
                            wait(pe, s["exp"], n1.shift(-2), 2, 1 - h)
                            pe.matmul(bank[:, 0:P], q[:, 0:P], keys[:, 0:P], start=True, stop=False,
                                      skip_group_check=True)
                            pe.matmul(bank[:, P:C], q[:, P:T], keys, start=False, stop=False,
                                      skip_group_check=True)
                            for c in (0, 2 * P):
                                mm = pe.matmul(bank[:, c:c + P], k.ident_bf[:], k.causal_bf[:], start=False,
                                               stop=True, skip_group_check=True)
                            mm.then_inc(s["s_mm"], 1)
                    if b2.real:
                        wait(pe, s["pT0"], b2)
                        wait(pe, s["pT1"], b2)
                        if b2.p == 0:
                            wait(pe, s["v"], b2, item=True)
                            wait(pe, s["o"], b2.shift(-PER), item=True)
                        for j in range(NT):
                            for h in range(2):
                                head = b2.p + 8 * h
                                g = head // 4 * 32
                                mm = pe.matmul(o_ps[g:g + 32, j * P:T], v[:, place(b2), j, head, :],
                                               pT[:, b2.ring(2), h, 0:T] if j == 0 else pT[:, b2.ring(2), h, T:C],
                                               start=(j == 0 and head % 4 == 0), stop=(j == 1 and head % 4 == 3),
                                               skip_group_check=True)
                        mm.then_inc(s["o_mm"], 1)
                    if at.p == 0 and pi.real:
                        wait(pe, s["rec"], pi, item=True)
                        wait(pe, s["k_terms"], ni, item=True)
                        wait(pe, s["v"], at, item=True)
                        wait(pe, s["res"], pi.shift(-PER), item=True)
                        for t in range(NT):
                            mm = pe.transpose(misc_ps[0:H, t * P:(t + 1) * P], rec[:, t, :], k.ident[:])
                        mm.then_inc(s["recT_mm"], 1)
                    if at.p == 1 and pi.real:
                        wait(pe, s["recT"], pi, item=True)
                        pe.matmul(misc_ps[:, T:2 * T], w["head_rows"][:], recT[:], start=True, stop=True
                                  ).then_inc(s["scale_mm"], 1)
                    if at.p == 3 and pi.real:
                        wait(pe, s["oT"], pi, item=True)
                        wait(pe, s["scale"], pi, item=True)
                        for t in range(NT):
                            mm = pe.matmul(misc_ps[:, t * P:(t + 1) * P], oT[:, t * P:(t + 1) * P], w["wproj"][:],
                                           start=True, stop=True)
                        mm.then_inc(s["y_mm"], 1)
                    if at.p == 4 and ni.real:
                        wait(pe, s["k_terms"], ni, item=True)
                        if pi.real:
                            pe.wait_ge(s["chain"], pi.item * 2 + 3)
                        for t in range(NT):
                            mm = pe.matmul(misc_ps[:, t * P:(t + 1) * P], n.hT[:, 0, t * P:(t + 1) * P], w["wv"][:],
                                           start=True, stop=True)
                        mm.then_inc(s["v_mm"], 1)
                    if at.p == 5 and ni2.real:
                        wait(pe, s["xn"], ni2, item=True)
                        wait(pe, s["v"], ni, item=True)
                        for t in range(NT):
                            mm = pe.transpose(misc_ps[:, T + t * P:T + (t + 1) * P], n.xn[:, t, :], k.ident[:])
                        mm.then_inc(s["ht_mm"], 1)
                    if at.p == 6 and ni2.real:
                        wait(pe, s["ht"], ni2, item=True)
                        projections(ni2, 0, s["q_mm"])
                    if at.p == 7 and ni2.real:
                        wait(pe, s["q_terms"], ni2, item=True)
                        projections(ni2, 1, s["k_mm"])

                walk(pe, PER, 2, LEAD, LAG, step)

            @block.vector
            def _(dve):
                start_norms(dve, n, s)
                dve.memset(v[:], 0.0).then_inc(s["v0"], 1)
                dve.wait_ge(k.weights_in[phase], 16 * len(WEIGHTS[phase]))
                dve.wait_ge(k.gate_in[phase], 16)

                def rotation_terms(which, at, mm, table, done):
                    wait(dve, mm, at, item=True)
                    wait(dve, s["cut"], at.shift(-PER), 10, 5 - 5 * which, item=True)
                    dve.tensor_tensor(terms[:, which], misc_ps[:].rearrange("p (c t) -> p c t", c=2), table, ALU.mult
                                      ).then_inc(done, 1)

                def step(at):
                    b1, ni, pi, ni2 = at.shift(-1), at.shift(PER), at.shift(-PER), at.shift(2 * PER)
                    if at.real:
                        for h in range(2):
                            wait(dve, s["s_mm"], at, 2, 1 - h)
                            wait(dve, s["exp"], at.shift(-2), 2)
                            for t in range(NT):
                                i = dve.tensor_reduce(nmax[:, at.ring(2), h, t:t + 1],
                                                      s_ps[at.ring(2)][h][:, 0:P] if t == 0 else s_ps[at.ring(2)][h][:, P:C], AX_X, ALU.max,
                                                      negate=True)
                            i.then_inc(s["nmax"], 1)
                    if at.p == 0 and pi.real:
                        wait(dve, s["exp"], at.shift(-1), 2)
                        wait(dve, s["recT_mm"], pi.shift(-PER), item=True)
                        dve.reciprocal(rec[:], sums[:, (at.s // PER + 1) % 2]).then_inc(s["rec"], 1)
                    if at.p == 2 and pi.real:
                        wait(dve, s["o_mm"], at.shift(-3))
                        wait(dve, s["oT"], pi.shift(-PER), item=True)
                        dve.tensor_copy(o[:], o_ps[:, 0:T]).then_inc(s["o"], 1)
                    if at.p == 4 and pi.real:
                        wait(dve, s["y_mm"], pi, item=True)
                        add_residual(dve, n, pi, misc_ps[:, 0:T].rearrange("p (t d) -> p t d", t=NT), k.gate[phase % 2],
                                     None, s["chain"], 2, None).then_inc(s["res"], 1)
                    if at.p == 3 and ni2.real:
                        normalise(dve, n, ni2, s["ht_mm"], s["xn"])
                    if at.p == 7 and ni2.real:
                        rotation_terms(0, ni2, s["q_mm"], w["rope_q"], s["q_terms"])
                    if at.p == 0 and ni.real:
                        rotation_terms(1, ni, s["k_mm"], w["rope_k"], s["k_terms"])
                    if b1.real:
                        wait(dve, s["pT_mm"], b1, 2, 1)
                        wait(dve, s["o_mm"], b1.shift(-2))
                        dve.tensor_copy(pT[:, b1.ring(2), 0, :], pT_ps[0][:, 0:C]).then_inc(s["pT0"], 1)

                walk(dve, PER, 2, LEAD, LAG, step)


def attention2(nc, d, k):
    rope_attention(nc, d, k, 4)


def attention3(nc, d, k):
    rope_attention(nc, d, k, 6)


CAT = 2 * 512 + 4 + P


def ffn2(nc, d, k):
    phase, PER, E = 5, 4, 8
    n = k.norms
    w = weights(k, phase)
    with ExitStack() as ctx:
        def sb(name, shape):
            return ctx.enter_context(nc.sbuf_tensor("f2_" + name, shape, F32))

        merged = sb("merged", [P, 2, CAT])
        hT = sb("hT", [P, 4, T])
        uT = sb("uT", [P, 2, T])
        gate_hidden = sb("gate_hidden", [P, T])
        hidden_sum = sb("hidden_sum", [P, 1])
        sum_cols = sb("sum_cols", [P, P])
        g = sb("g", [P, 2, E])
        ht_ps, gh_ps, g_ps, u_ps, y_ps = k.banks[0], k.banks[1], k.banks[2], k.banks[3:5], k.banks[5]
        names = ("chain", "var", "std", "rstd", "xn", "ht_mm", "ht", "gh_mm", "sum", "cols", "g_mm", "g", "merge",
                 "u_mm", "u", "y_mm", "res")
        s = signals(nc, ctx, "f2_", names)
        LEAD, LAG = 8, 1

        with nc.Block() as block:

            @block.sync
            def _(sp):
                prefetch(sp, nc, k, d, phase)

            @block.scalar
            def _(act):
                std_of_rows(act, n, s["var"], s["std"])
                act.wait_ge(k.weights_in[phase], 16 * len(WEIGHTS[phase]))

                def step(at):
                    i2 = at.shift(2 * PER)
                    if at.real:
                        wait(act, s["u_mm"], at)
                        wait(act, s["y_mm"], at.shift(-2))
                        c = 2 * 512 + at.p
                        act.activation(uT[:, at.ring(2), :], u_ps[at.ring(2)][:, 0:T], ACT.Gelu_apprx_tanh,
                                       bias=merged[:, at.s // PER % 2, c:c + 1]).then_inc(s["u"], 1)
                    if at.p == 1 and i2.real:
                        wait(act, s["ht_mm"], i2, item=True)
                        wait(act, s["u_mm"], at.shift(-6))
                        modulated(act, k, phase, i2, ht_ps[:, 0:T], hT[:, i2.s // PER % 4, :], s["ht"])
                    if at.p == 2 and i2.real:
                        wait(act, s["gh_mm"], i2, item=True)
                        act.activation(gate_hidden[:], gh_ps[:, 0:T], ACT.Relu, bias=w["gb1"][:, 0:1],
                                       accum_out=hidden_sum[:]).then_inc(s["sum"], 1)
                        wait(act, s["sum"], i2, item=True)
                        wait(act, s["g_mm"], i2.shift(-PER), item=True)
                        act.activation(sum_cols[:], k.ident[:], ACT.Identity, scale=0.0, bias=hidden_sum[:, 0:1]
                                       ).then_inc(s["cols"], 1)

                walk(act, PER, 4, LEAD, LAG, step)

            @block.tensor
            def _(pe):
                pe.wait_ge(k.weights_in[phase], 16 * len(WEIGHTS[phase]))

                def step(at):
                    b1, i2 = at.shift(-1), at.shift(2 * PER)
                    if b1.real:
                        wait(pe, s["u"], b1)
                        if b1.p == 0:
                            wait(pe, s["res"], b1.shift(-PER), item=True)
                        for t in range(NT):
                            mm = pe.matmul(y_ps[:, t * P:(t + 1) * P], uT[:, b1.ring(2), t * P:(t + 1) * P],
                                           merged[:, b1.s // PER % 2, 512 + b1.p * P:512 + (b1.p + 1) * P],
                                           start=(b1.p == 0 and t == 0), stop=(b1.p == PER - 1),
                                           skip_group_check=True)
                        mm.then_inc(s["y_mm"], 1)
                    if at.p == 1 and i2.real:
                        wait(pe, s["xn"], i2, item=True)
                        wait(pe, s["ht"], i2.shift(-PER), item=True)
                        for t in range(NT):
                            mm = pe.transpose(ht_ps[:, t * P:(t + 1) * P], n.xn[:, t, :], k.ident[:])
                        mm.then_inc(s["ht_mm"], 1)
                    if at.p == 2 and i2.real:
                        wait(pe, s["ht"], i2, item=True)
                        wait(pe, s["sum"], i2.shift(-PER), item=True)
                        pe.matmul(gh_ps[:, 0:T], w["gw1_2"][:], hT[:, i2.s // PER % 4, :], start=True, stop=True
                                  ).then_inc(s["gh_mm"], 1)
                    if at.p == 3 and i2.real:
                        wait(pe, s["cols"], i2, item=True)
                        wait(pe, s["g"], i2.shift(-PER), item=True)
                        pe.matmul(g_ps[:, 0:E], sum_cols[:], w["gw2"][:], start=True, stop=True).then_inc(s["g_mm"], 1)
                    if at.real:
                        wait(pe, s["merge"], at, E, item=True)
                        wait(pe, s["u"], at.shift(-2))
                        pe.matmul(u_ps[at.ring(2)][:, 0:T], merged[:, at.s // PER % 2, at.p * P:(at.p + 1) * P],
                                  hT[:, at.s // PER % 4, :], start=True, stop=True).then_inc(s["u_mm"], 1)

                walk(pe, PER, 4, LEAD, LAG, step)

            @block.vector
            def _(dve):
                start_norms(dve, n, s)
                dve.wait_ge(k.weights_in[phase], 16 * len(WEIGHTS[phase]))
                dve.wait_ge(k.gate_in[phase], 16)

                def step(at):
                    ni, i2 = at.shift(PER), at.shift(2 * PER)
                    if at.p == 0 and i2.real:
                        normalise(dve, n, i2, s["ht_mm"], s["xn"])
                    if ni.real:
                        if ni.p == 0:
                            wait(dve, s["g"], Step(ni.base, ni.s, PER), item=True)
                            wait(dve, s["y_mm"], at.shift(-PER + 3))
                        m = merged[:, ni.s // PER % 2, :]
                        for e in (2 * ni.p, 2 * ni.p + 1):
                            if e:
                                dve.wait_ge(s["merge"], ni.item * E + e)
                            dve.scalar_tensor_tensor(out=m, in0=w["task"][:, e, :], scalar=g[:, ni.s // PER % 2, e:e + 1],
                                                     in1=m if e else w["base"][:], op0=ALU.mult, op1=ALU.add
                                                     ).then_inc(s["merge"], 1)
                    if at.p == 3 and i2.real:
                        wait(dve, s["g_mm"], i2, item=True)
                        wait(dve, s["merge"], i2.shift(-2 * PER), E, item=True)
                        dve.scalar_tensor_tensor(out=g[:, i2.s // PER % 2, :], in0=g_ps[:, 0:E], scalar=1.0 / T,
                                                 in1=w["gb2"][:], op0=ALU.mult, op1=ALU.add).then_inc(s["g"], 1)
                    if at.p == 3 and at.real:
                        wait(dve, s["y_mm"], at)
                        add_residual(dve, n, at, y_ps[:, 0:T].rearrange("p (t d) -> p t d", t=NT), k.gate[phase % 2],
                                     merged[:, at.s // PER % 2, CAT - P:CAT].unsqueeze(1).to_broadcast([P, NT, P]),
                                     s["chain"], 3, None).then_inc(s["res"], 1)

                walk(dve, PER, 4, LEAD, LAG, step)


def ffn3(nc, d, k):
    phase, PER, E, K = 7, 5, 8, 6
    n = k.norms
    w = weights(k, phase)
    with ExitStack() as ctx:
        def sb(name, shape):
            return ctx.enter_context(nc.sbuf_tensor("f3_" + name, shape, F32))

        tanh = sb("tanh", [P, 2, T])
        gated = sb("gated", [P, 2, T])
        hidden = sb("hidden", [P, 2, T])
        acc = sb("acc", [P, NT, P])
        b = router_tiles(nc, ctx, "f3_", E)
        gu_ps, y_ps = k.banks[0:2], k.banks[2:4]
        ht_ps, rt_ps = k.banks[4], k.banks[5]
        names = ("chain", "var", "std", "rstd", "xn", "ht_mm", "ht", "rt_mm", "nmax", "rexp", "top", "cw", "cwT_mm",
                 "gu_mm", "tanh", "gated", "hidden", "y_mm", "acc", "res", "pads")
        s = signals(nc, ctx, "f3_", names)
        LAST, LEAD, LAG = PER - 1, 5, 2

        with nc.Block() as block:

            @block.scalar
            def _(act):
                std_of_rows(act, n, s["var"], s["std"])

                def step(at):
                    nx, ni = at.shift(1), at.shift(PER)
                    if nx.real:
                        wait(act, s["gu_mm"], nx)
                        wait(act, s["gated"], nx.shift(-2))
                        act.activation(tanh[:, nx.ring(2), :], gu_ps[nx.ring(2)][:, 0:T], ACT.Tanh, scale=0.5
                                       ).then_inc(s["tanh"], 1)
                    if at.p == 1 and ni.real:
                        wait(act, s["ht_mm"], ni, item=True)
                        wait(act, s["gu_mm"], at.shift(-2))
                        modulated(act, k, phase, ni, ht_ps[:, 0:T], n.hT[:, (at.s // PER + 1) % 2, :], s["ht"])
                    if at.p == 2 and ni.real:
                        wait(act, s["nmax"], ni, item=True)
                        wait(act, s["top"], ni.shift(-PER), 5, item=True)
                        for t in range(NT):
                            i = act.activation(b["e"][:, t, :], rt_ps[:, t * E:(t + 1) * E], ACT.Exp,
                                               bias=b["nmax"][:, t:t + 1], accum_out=b["sums"][:, t:t + 1])
                        i.then_inc(s["rexp"], 1)

                walk(act, PER, 2, LEAD, LAG, step)

            @block.tensor
            def _(pe):
                pe.wait_ge(k.weights_in[phase], 16 * len(WEIGHTS[phase]))

                def step(at):
                    nx, ni = at.shift(1), at.shift(PER)
                    if nx.real:
                        if nx.p == 0:
                            wait(pe, s["ht"], nx, item=True)
                        wait(pe, s["hidden"], nx.shift(-2))
                        for c in range(2):
                            mm = pe.matmul(gu_ps[nx.ring(2)][:, c * T:(c + 1) * T], w["gu"][:, nx.p, c, :],
                                           n.hT[:, nx.s // PER % 2, :], start=True, stop=True)
                        mm.then_inc(s["gu_mm"], 1)
                    if at.p == 1 and ni.real:
                        wait(pe, s["xn"], ni, item=True)
                        wait(pe, s["ht"], ni.shift(-PER), item=True)
                        for t in range(NT):
                            mm = pe.transpose(ht_ps[:, t * P:(t + 1) * P], n.xn[:, t, :], k.ident[:])
                        mm.then_inc(s["ht_mm"], 1)
                    if at.p == 2 and ni.real:
                        wait(pe, s["ht"], ni, item=True)
                        wait(pe, s["rexp"], ni.shift(-PER), item=True)
                        for t in range(NT):
                            mm = pe.matmul(rt_ps[:, t * E:(t + 1) * E],
                                           n.hT[:, (at.s // PER + 1) % 2, t * P:(t + 1) * P], w["rw3"][:],
                                           start=True, stop=True)
                        mm.then_inc(s["rt_mm"], 1)
                    if at.real:
                        wait(pe, s["hidden"], at)
                        wait(pe, s["acc"], at.shift(-2))
                        width = P if at.p == LAST else 2 * P
                        for t in range(NT):
                            mm = pe.matmul(y_ps[at.ring(2)][:, t * width:(t + 1) * width],
                                           hidden[:, at.ring(2), t * P:(t + 1) * P],
                                           w["shared"][:] if at.p == LAST else w["down"][:, at.p, :],
                                           start=True, stop=True)
                        mm.then_inc(s["y_mm"], 1)

                walk(pe, PER, 2, LEAD, LAG, step)

            @block.vector
            def _(dve):
                start_norms(dve, n, s)
                dve.memset(b["probs"][:], -1.0)
                dve.memset(b["top"][:], -1.0).then_inc(s["pads"], 1)
                dve.wait_ge(s["pads"], 1)
                dve.wait_ge(k.gate_in[phase], 16)

                def step(at):
                    nx, ni = at.shift(1), at.shift(PER)
                    if at.p == 0 and ni.real:
                        normalise(dve, n, ni, s["ht_mm"], s["xn"])
                    if nx.real:
                        r = nx.ring(2)
                        wait(dve, s["tanh"], nx)
                        dve.scalar_tensor_tensor(out=gated[:, r, :], in0=tanh[:, r, :], scalar=1.0,
                                                 in1=gu_ps[r][:, 0:T], op0=ALU.add, op1=ALU.mult
                                                 ).then_inc(s["gated"], 1)
                        wait(dve, s["gated"], nx)
                        wait(dve, s["y_mm"], nx.shift(-2))
                        dve.scalar_tensor_tensor(out=hidden[:, r, :], in0=gated[:, r, :], scalar=0.5,
                                                 in1=gu_ps[r][:, T:2 * T], op0=ALU.mult, op1=ALU.mult
                                                 ).then_inc(s["hidden"], 1)
                    if at.p == 2 and ni.real:
                        wait(dve, s["rt_mm"], ni, item=True)
                        dve.tensor_reduce(b["nmax"][:], rt_ps[:, 0:NT * E].rearrange("p (t e) -> p t e", t=NT), AX_X,
                                          ALU.max, negate=True).then_inc(s["nmax"], 1)
                    if at.real:
                        wait(dve, s["y_mm"], at)
                        wait(dve, s["acc"], at.shift(-1), 2)
                        y, c = y_ps[at.ring(2)], b["cw"][:, at.s // PER % 2]
                        if at.p == 0:
                            wait(dve, s["cw"], at, item=True)
                            wait(dve, s["res"], at.shift(-PER), item=True)
                        if at.p == LAST:
                            dve.tensor_tensor(acc[:], acc[:], y[:, 0:T].rearrange("p (t d) -> p t d", t=NT),
                                              ALU.add).then_inc(s["acc"], 2)
                            wait(dve, s["acc"], at, 2)
                            add_residual(dve, n, at, acc[:], k.gate[phase % 2], None, s["chain"], 2, None
                                         ).then_inc(s["res"], 1)
                        else:
                            for j in range(2):
                                if j:
                                    wait(dve, s["acc"], at, 2, 1)
                                for t in range(NT):
                                    a, z = acc[:, t, :], y[:, t * 2 * P + j * P:t * 2 * P + (j + 1) * P]
                                    e = 2 * at.p + j
                                    if e == 0:
                                        i = dve.tensor_scalar(a, z, c[:, t, 0:1], None, ALU.mult)
                                    else:
                                        i = dve.scalar_tensor_tensor(out=a, in0=z, scalar=c[:, t, e:e + 1], in1=a,
                                                                     op0=ALU.mult, op1=ALU.add)
                                i.then_inc(s["acc"], 1)
                    if at.p == 3 and ni.real:
                        softmax_top(dve, s, k.spare, ni, E, K, (at.s // PER + 1) % 2, b, acc_each=2, transposed=False)

                walk(dve, PER, 2, LEAD, LAG, step)


PHASES = [attention0, ffn0, attention1, ffn1, attention2, ffn2, attention3, ffn3]


def position_table(length, features):
    dist = np.arange(-length + 1, length, dtype=np.float64)
    n, a = features // 6, np.abs(dist)[:, None]
    decay = np.exp(-math.log(2.0) / 2.0 ** np.linspace(3.0, math.log2(length), n)[None] * a)
    central = (2.0 ** np.arange(1, n + 1)[None] - 1.0 > a).astype(np.float64)
    stddev = length / (2.0 * n)
    mean = np.linspace(length / n, float(length), n)[None]
    conc, rate = (mean / stddev) ** 2, mean / stddev ** 2
    log_a = np.log(np.maximum(a, 1e-300))
    log_norm = np.array([[math.lgamma(c) for c in conc[0]]]) - conc * np.log(rate)
    gamma = np.exp((conc - 1.0) * log_a - rate * a - log_norm) + 1e-8
    gamma = gamma / gamma.max(axis=-1, keepdims=True)
    emb = np.concatenate([decay, central, gamma], axis=-1)
    return np.concatenate([emb, np.sign(dist)[:, None] * emb], axis=-1).astype(np.float32)


def laid_out(i):
    f = {x: np.asarray(v) for x, v in i.items()}
    o = {}
    o["x"] = f["L0_attn_x"]
    o["cT"] = np.concatenate([f[f"L{n}_c"].T for n in range(4)], axis=1)
    o["wmod"] = np.stack([f[f"L{n}_wmod"] for n in range(4)], axis=1)
    o["ident"] = np.eye(P, dtype=np.float32)
    q = np.arange(P)
    o["causal"] = np.where(q[None, :] > q[:, None], MASKED, 0.0).astype(np.float32)

    def rows(a, k):
        return a.reshape(k, -1, a.shape[-1]).transpose(1, 0, 2)

    def bcast(a):
        return np.broadcast_to(a, (P, *a.shape))

    o["wqkv0"] = np.concatenate([f["L0_attn_Wq"], f["L0_attn_Wkv"]], axis=1)
    o["wo0"] = rows(f["L0_attn_Wo"], 8)
    o["bo0"] = bcast(f["L0_attn_bo"])
    o["e1w"] = np.concatenate([f["L0_ffn_eW1"], f["L0_ffn_sW1"][None]]).transpose(1, 0, 2)
    o["e2w"] = np.concatenate([f["L0_ffn_eW2"], f["L0_ffn_sW2"][None]]).transpose(1, 0, 2)
    o["e1b"] = np.concatenate([f["L0_ffn_eb1"], f["L0_ffn_sb1"][None]]).T
    o["e2b"] = np.concatenate([f["L0_ffn_eb2"], f["L0_ffn_sb2"][None]])
    o["rw"] = f["L0_ffn_router_W"]
    o["rb"] = bcast(f["L0_ffn_router_b"])
    o["wqkv1"] = np.concatenate([f["L1_attn_w_qs"], f["L1_attn_w_ks"], f["L1_attn_w_vs"]], axis=1)
    o["wo1"] = rows(f["L1_attn_w_out"], 8)
    o["bo1"] = bcast(f["L1_attn_b_out"])
    o["qb1"] = np.stack([f["L1_attn_rel_embed_bias"][0, :, 0].T, f["L1_attn_rel_pos_bias"][0, :, 0].T], axis=1)
    o["w_rel"] = rows(f["L1_attn_w_rel_pos_k"], 2)
    table = position_table(T, f["L1_attn_w_rel_pos_k"].shape[0])
    o["positions"] = rows(np.pad(table.T, ((0, 0), (0, 1))), 2)
    o["w12"] = f["L1_ffn_w12"].transpose(2, 0, 1)
    o["w3"] = f["L1_ffn_w3"].reshape(8, P, 2, P).transpose(3, 0, 2, 1)
    o["gw1"] = f["L1_ffn_gate_w"].T
    qkv = f["L2_attn_Wqkv"]
    swapped = np.arange(P) ^ 1
    angle = np.arange(T)[None, :] * (10000.0 ** (-(np.arange(P) % 8 // 2) / 4.0))[:, None]
    sign = np.where(np.arange(P) % 2 == 0, -1.0, 1.0)[:, None]
    by_feature = np.arange(P).reshape(16, 8).T.ravel()
    rope = np.stack([np.cos(angle), np.sin(angle) * sign], axis=1)[by_feature]
    for x, (wq, wk, wv), wo in ((2, [qkv[:, i * P:(i + 1) * P] for i in range(3)], f["L2_attn_Wproj"]),
                                (3, [f[f"L3_attn_W_{c}"].T for c in "qkv"], f["L3_attn_W_o"].T)):
        o[f"wqk{x}"] = np.stack([c[:, by_feature] for c in (wq, wq[:, swapped], wk, wk[:, swapped])], axis=1)
        o[f"wv{x}"], o[f"wproj{x}"] = wv, wo
        o[f"rope_q{x}"] = (rope / math.sqrt(8.0)).astype(np.float32)
        o[f"rope_k{x}"] = rope.astype(np.float32)
        o[f"head_rows{x}"] = (np.arange(16)[:, None] == np.arange(P)[None, :] // 8).astype(np.float32)

    def joined(w1, w2, b1, b2):
        return np.concatenate([w1.T, w2.T.reshape(4, P, P).transpose(1, 0, 2).reshape(P, -1), b1.reshape(4, P).T,
                               bcast(b2)], axis=1)

    o["base"] = joined(*(f[f"L2_ffn_{x}"] for x in ("W1", "W2", "b1", "b2")))
    o["task"] = np.stack([joined(*(f[f"L2_ffn_T{x}"][e] for x in ("W1", "W2", "b1", "b2"))) for e in range(8)], axis=1)
    o["gw1_2"], o["gb1"] = f["L2_ffn_gate_w1"].T, f["L2_ffn_gate_b1"][:, None]
    o["gw2"], o["gb2"] = f["L2_ffn_gate_w2"].T, bcast(f["L2_ffn_gate_b2"])
    pairs = [np.concatenate([f[f"L3_ffn_w_{x}"][e::2] for e in range(2)], axis=2) for x in ("gate", "up")]
    gu = np.stack([np.concatenate([pair, f[f"L3_ffn_ws_{x}"][None]]) for pair, x in zip(pairs, ("gate", "up"))], axis=1)
    o["gu"] = gu.transpose(2, 0, 1, 3)
    down = np.zeros((P, 4, 2, P), np.float32)
    down[0:64, :, 0], down[64:, :, 1] = (f["L3_ffn_w_down"][e::2].transpose(1, 0, 2) for e in range(2))
    o["down"], o["shared"], o["rw3"] = down, f["L3_ffn_ws_down"], f["L3_ffn_router_w"]
    for name, shape, parts in (w for ph in WEIGHTS for w in ph):
        o[name] = o[name].reshape(parts, -1)
    return o


def kernel(**inputs):
    import numpy as _np
    import concourse.bacc as _bacc
    from concourse import mybir as _mybir
    from concourse.bass_utils import run_bass_kernel_spmd as _run

    nc = _bacc.Bacc("TRN2", target_bir_lowering=False, num_devices=1)
    arrays, d = {}, {}
    for name, a in laid_out(inputs).items():
        a = _np.ascontiguousarray(a)
        arrays[f"in_{name}"] = a
        d[name] = nc.dram_tensor(f"in_{name}", a.shape, _mybir.dt.from_np(a.dtype), kind="ExternalInput").ap()
    out = nc.dram_tensor("out_0", (NB, T, P), _mybir.dt.float32, kind="ExternalOutput").ap()
    build(nc, d, out, PHASES)
    r = _run(nc, [arrays], core_ids=[0])
    return r.results[0]["out_0"]
```

```python
import math
from contextlib import ExitStack

import numpy as np

import concourse.bass as bass
from concourse import mybir

F32 = mybir.dt.float32
BF16 = mybir.dt.bfloat16
F32R = mybir.dt.float32r
ALU = mybir.AluOpType
ACT = mybir.ActivationFunctionType
AX_X = mybir.AxisListType.X

NB = 16
T = 256
P = 128
NT = T // P
LN_EPS = 1e-5
MASKED = -1e30
ARENA = 6912, 10624


class Step:

    def __init__(self, base, s, per):
        self.base, self.s, self.per = base, s, per
        self.item = base + s // per
        self.count = base * per + s
        self.p = s % per

    def shift(self, by):
        return Step(self.base, self.s + by, self.per)

    @property
    def real(self):
        return not isinstance(self.base, int) or 0 <= self.count < NB * self.per

    def ring(self, n):
        return self.s % n


def walk(eng, per, unroll, lead, lag, step):
    for s in range(-lead, unroll * per):
        step(Step(0, s, per))
    with eng.Fori(1, NB // unroll - 1) as lap:
        for s in range(unroll * per):
            step(Step(lap * unroll, s, per))
    for s in range((NB - unroll) * per, NB * per + lag):
        step(Step(0, s, per))


def wait(eng, sem, step, each=1, extra=0, item=False):
    if not step.real:
        return
    n = (step.item if item else step.count) * each + each - extra
    eng.wait_ge(sem, n)


def hold(dve, spare):
    dve.memset(spare, 0.0)


def wait_ring(eng, sems, step):
    if step.real:
        eng.wait_ge(sems[step.ring(len(sems))], (step.base * (step.per // len(sems)) + step.s // len(sems)) * 16 + 16)


def signals(nc, ctx, prefix, names):
    sems = {x: nc.alloc_semaphore(f"{prefix}{x}") for x in names}

    def give_back():
        nc.clear_and_free_semaphores(list(sems.values()))
        nc.all_engine_barrier(sem_only=True)

    ctx.callback(give_back)
    return sems


class Norms:

    def __init__(self, nc, ctx):
        def sb(name, shape):
            return ctx.enter_context(nc.sbuf_tensor(name, shape, F32))

        self.x = sb("x", [P, NB, NT, P])
        self.stats = sb("row_stats", [P, NB, NT, 6])
        self.mean = sb("row_mean", [P, NB, NT])
        self.half_gap = sb("row_half_gap", [P, NB, NT])
        self.m2 = sb("row_m2", [P, NB, NT])
        self.var = sb("row_var", [P, NB, NT])
        self.std = sb("row_std", [P, NB, NT])
        self.rstd = sb("row_rstd", [P, NB, NT])
        self.xn = sb("xn", [P, NT, P])
        self.delta = sb("delta", [P, NT, P])
        self.hT = sb("hT", [P, 2, T])
        self.hT2 = ctx.enter_context(nc.sbuf_tensor("hT2", [P, 2, 2, T], F32R))



def matmul3(pe, out, left, right, start=True, stop=True):
    pe.matmul(out, left[0], right[0], start=start, stop=False, skip_group_check=True)
    pe.matmul(out, left[0], right[1], start=False, stop=False, skip_group_check=True)
    return pe.matmul(out, left[1], right[0], start=False, stop=stop, skip_group_check=True)


def cut_hT(act, n, at, ready, rounded):
    wait(act, ready, at, item=True)
    r = at.s // at.per % 2
    act.copy(n.hT2[:, r, 0, :], n.hT[:, r, :]).then_inc(rounded, 1)


def cut_hT_rest(pool, n, at, rounded, rest_ready):
    wait(pool, rounded, at, item=True)
    r = at.s // at.per % 2
    pool.tensor_tensor(n.hT2[:, r, 1, :], n.hT[:, r, :], n.hT2[:, r, 0, :], ALU.subtract).then_inc(rest_ready, 1)


def var_of_rows(dve, n, chain, var_ready):
    s = n.stats
    dve.tensor_tensor(n.mean[:], s[:, :, :, 1], s[:, :, :, 4], ALU.add)
    dve.tensor_tensor(n.half_gap[:], s[:, :, :, 1], s[:, :, :, 4], ALU.subtract)
    dve.tensor_tensor(n.m2[:], s[:, :, :, 2], s[:, :, :, 5], ALU.add).then_inc(chain, 1)
    dve.wait_ge(chain, 1)
    dve.tensor_scalar(n.mean[:], n.mean[:], 0.5, None, ALU.mult)
    dve.tensor_scalar(n.m2[:], n.m2[:], 1.0 / P, LN_EPS, ALU.mult, ALU.add)
    dve.scalar_tensor_tensor(out=n.half_gap[:], in0=n.half_gap[:], scalar=0.25, in1=n.half_gap[:],
                             op0=ALU.mult, op1=ALU.mult).then_inc(chain, 1)
    dve.wait_ge(chain, 2)
    dve.tensor_tensor(n.var[:], n.m2[:], n.half_gap[:], ALU.add).then_inc(var_ready, 1)


def std_of_rows(act, n, var_ready, std_ready):
    act.wait_ge(var_ready, 1)
    act.activation(n.std[:], n.var[:], ACT.Sqrt).then_inc(std_ready, 1)


def rstd_of_rows(dve, n, std_ready, rstd_ready):
    dve.wait_ge(std_ready, 1)
    dve.reciprocal(n.rstd[:], n.std[:]).then_inc(rstd_ready, 1)
    dve.wait_ge(rstd_ready, 1)


def normalise(dve, n, at, xn_used, xn_ready):
    wait(dve, xn_used, at.shift(-at.per), item=True)
    for t in range(NT):
        k = dve.tensor_scalar(n.xn[:, t, :], n.x[:, at.item, t, :], n.mean[:, at.item, t:t + 1],
                              n.rstd[:, at.item, t:t + 1], ALU.subtract, ALU.mult)
    k.then_inc(xn_ready, 1)


def add_residual(dve, n, at, y, gate, bias, chain, per_item, parts, chain0=2):
    k = at.item * per_item + chain0
    biased = 0 if bias is None else 1
    if "bias" in parts and biased:
        dve.tensor_tensor(n.delta[:], y, bias, ALU.add).then_inc(chain, 1)
    if "gate" in parts:
        if biased:
            dve.wait_ge(chain, k + 1)
        g = gate[:, at.item, :].unsqueeze(1).to_broadcast([P, NT, P])
        dve.tensor_tensor(n.delta[:], n.delta[:] if biased else y, g, ALU.mult).then_inc(chain, 1)
    if "add" in parts:
        dve.wait_ge(chain, k + biased + 1)
        dve.tensor_tensor(n.x[:, at.item, :, :], n.x[:, at.item, :, :], n.delta[:], ALU.add).then_inc(chain, 1)
    if "stats" in parts:
        dve.wait_ge(chain, k + biased + 2)
        for t in range(NT):
            i = dve.bn_stats(n.stats[:, at.item, t, :], n.x[:, at.item, t, :])
        return i


ALL_PARTS = ("bias", "gate", "add", "stats")


def prologue(nc, d, k, first):
    with ExitStack() as ctx:
        n = k.norms
        cT = ctx.enter_context(nc.sbuf_tensor("cT", [P, 4 * NB], F32))
        silu_c = ctx.enter_context(nc.sbuf_tensor("silu_c", [P, 4 * NB], F32))
        wmod = ctx.enter_context(nc.sbuf_tensor("wmod", [P, 4, 6 * P], F32))
        mag = ctx.enter_context(nc.sbuf_tensor("gate_size", [NB, 8, P], F32))
        sign = ctx.enter_context(nc.sbuf_tensor("gate_sign", [NB, 8, P], F32))
        gates = ctx.enter_context(nc.sbuf_tensor("gates", [NB, 8, P], F32))
        maskf = ctx.enter_context(nc.sbuf_tensor("maskf", [P, P], F32))
        mod_ps, gate_ps = k.banks[0][:, 0:16 * NB], [k.banks[1 + h][0:NB, :] for h in range(2)]
        sems = signals(nc, ctx, "pro_", ("mod_in", "x_in", "consts_in", "silu", "mod_mm", "gates", "gate_abs",
                                         "gate_steps", "gates_out"))
        with nc.Block() as block:

            @block.sync
            def _(sp):
                sp.dma_start(cT[:], d["cT"]).then_inc(sems["mod_in"], 16)
                sp.dma_start(wmod[:], d["wmod"]).then_inc(sems["mod_in"], 16)
                for g in range(4):
                    sp.dma_start(n.x[:, 4 * g:4 * g + 4], d["x"].rearrange("b (t p) d -> p b t d", p=P)[:, 4 * g:4 * g + 4]
                                 ).then_inc(sems["x_in"], 16)
                sp.dma_start(k.ident[:], d["ident"]).then_inc(sems["consts_in"], 16)
                sp.dma_start(maskf[:], d["causal"]).then_inc(sems["consts_in"], 16)
                load_weights(sp, nc, k, d, first)
                sp.wait_ge(sems["gates"], 1)
                sp.dma_start(k.gates_dram, gates[:]).then_inc(sems["gates_out"], 16)
                sp.wait_ge(sems["gates_out"], 16)
                load_gate(sp, k, first)

            @block.scalar
            def _(act):
                act.wait_ge(sems["mod_in"], 32)
                act.activation(silu_c[:], cT[:], ACT.Silu).then_inc(sems["silu"], 1)
                act.wait_ge(sems["mod_mm"], 1)
                for h in range(2):
                    i = act.activation(mag[:, 4 * h:4 * h + 4, :], gate_ps[h].rearrange("b (s d) -> b s d", s=4), ACT.Abs)
                i.then_inc(sems["gate_abs"], 1)

            @block.tensor
            def _(pe):
                pe.wait_ge(sems["mod_in"], 32)
                pe.wait_ge(sems["silu"], 1)
                for layer in range(4):
                    c = silu_c[:, layer * NB:(layer + 1) * NB]
                    for j, kind in enumerate((0, 1, 3, 4)):
                        at = (layer * 4 + j) * NB
                        pe.matmul(mod_ps[:, at:at + NB], wmod[:, layer, kind * P:(kind + 1) * P], c,
                                  start=True, stop=True)
                    for j, kind in enumerate((2, 5)):
                        at = ((layer * 2 + j) % 4) * P
                        mm = pe.matmul(gate_ps[layer // 2][:, at:at + P], c,
                                       wmod[:, layer, kind * P:(kind + 1) * P], start=True, stop=True)
                mm.then_inc(sems["mod_mm"], 1)

            @block.vector
            def _(dve):
                dve.wait_ge(sems["mod_mm"], 1)
                m = mod_ps.rearrange("p (l j b) -> p l j b", l=8, j=2)
                dve.tensor_copy(k.mod[:, :, 0, :], m[:, :, 0, :])
                dve.tensor_scalar(k.mod[:, :, 1, :], m[:, :, 1, :], 1.0, None, ALU.add)
                dve.wait_ge(sems["gate_abs"], 1)
                for h in range(2):
                    g = gate_ps[h].rearrange("b (s d) -> b s d", s=4)
                    i = dve.tensor_scalar(sign[:, 4 * h:4 * h + 4, :], g, 0.0, 2.0, ALU.is_ge, ALU.mult)
                dve.tensor_scalar(mag[:], mag[:], 0.25, None, ALU.max).then_inc(sems["gate_steps"], 1)
                dve.wait_ge(sems["gate_steps"], 1)
                dve.scalar_tensor_tensor(out=gates[:], in0=sign[:], scalar=-1.0, in1=mag[:],
                                         op0=ALU.add, op1=ALU.mult).then_inc(sems["gates"], 1)
                dve.wait_ge(sems["consts_in"], 32)
                dve.tensor_copy(k.ident_bf[:], k.ident[:])
                dve.tensor_copy(k.causal_bf[:], maskf[:])
                for b in range(NB):
                    if b % 4 == 0:
                        dve.wait_ge(sems["x_in"], 4 * b + 16)
                    for t in range(NT):
                        dve.bn_stats(n.stats[:, b, t, :], n.x[:, b, t, :])


def load_gate(sp, k, phase):
    sp.dma_start(k.gate[phase % 2][:], k.gates_dram[:, phase, :].partition_broadcast(P)).then_inc(k.gate_in[phase], 16)


def load_weights(sp, nc, k, d, phase):
    at = 0
    for name, shape, parts in WEIGHTS[phase]:
        size = int(np.prod(shape))
        sp.dma_start(k.arena[phase % 2][0:parts, at:at + size], d[name]).then_inc(k.weights_in[phase], 16)
        at += size
    assert at <= ARENA[phase % 2]


def weights(k, phase):
    at, views = 0, {}
    for name, shape, parts in WEIGHTS[phase]:
        size = int(np.prod(shape))
        v = k.arena[phase % 2][0:parts, at:at + size]
        if len(shape) == 2:
            v = v.rearrange("p (a b) -> p a b", a=shape[0])
        elif len(shape) == 3:
            v = v.rearrange("p (a b c) -> p a b c", a=shape[0], b=shape[1])
        views[name] = v
        at += size
    return views


class Shared:
    pass


ROPE_WEIGHTS = [[(f"wqk{x}", (4, P), P), (f"wv{x}", (P,), P), (f"wproj{x}", (P,), P), (f"rope_q{x}", (2, T), P),
                 (f"rope_k{x}", (2, T), P), (f"head_rows{x}", (P,), 16)]
                for x in (2, 3)]
WEIGHTS = [
    [("wqT0", (16, P), 64), ("wkT0", (16, P), 64), ("wv0", (1024,), P), ("wo0", (8, P), P), ("bo0", (P,), P)],
    [("e1w", (16, P), P), ("e2w", (16, P), P), ("e1b", (16,), P), ("rw", (15,), P), ("rb", (15,), P),
     ("e2b", (P,), 16)],
    [("wkT", (8, P), P), ("qb1", (2, 8), P), ("w_relT", (8, 2, 96), P), ("wqT", (8, P), P), ("positions", (2, 512), 96),
     ("wv1", (1024,), P), ("wo1", (8, P), P), ("bo1", (P,), P)],
    [("w12", (8, 512), P), ("w3", (8, 2, P), P), ("gw1", (8,), P)],
    ROPE_WEIGHTS[0],
    [("base", (1156,), P), ("task", (8, 1156), P), ("gw1_2", (P,), P), ("gb1", (1,), P), ("gw2", (8,), P),
     ("gb2", (8,), P)],
    ROPE_WEIGHTS[1],
    [("gu", (5, 2, P), P), ("down", (4, 2 * P), P), ("shared", (P,), P), ("rw3", (8,), P)],
]


def causal_transposes(pe, pT, p, ident):
    for block in range(3):
        mm = pe.transpose(pT[:, block * P:(block + 1) * P], p[:, block * P:(block + 1) * P], ident)
    return mm


def modulated(act, k, phase, at, ps, hT, sem):
    act.activation(hT, ps, ACT.Identity, scale=k.mod[:, phase, 1, bass.ds(at.item, 1)],
                   bias=k.mod[:, phase, 0, bass.ds(at.item, 1)]).then_inc(sem, 1)


def attention0(nc, d, k):
    phase, PER = 0, 8
    n = k.norms
    w = weights(k, phase)
    EPS = 1e-8
    C = 3 * P
    with ExitStack() as ctx:
        def sb(name, shape):
            return ctx.enter_context(nc.sbuf_tensor("a0_" + name, shape, F32))

        A = ctx.enter_context(nc.sbuf_tensor("a0_A", [P, 2 * PER, 2, P], F32R))
        xA = ctx.enter_context(nc.sbuf_tensor("a0_xA", [P, 4, 2, T], F32R))
        v = sb("v", [P, 4, NT, P])
        p = sb("p", [P, 2, 2, C])
        pT = sb("pT", [P, 2, 2, C])
        oT = sb("oT", [P, 2, T])
        nmax = sb("nmax", [P, 2, 2, NT])
        sums = sb("sums", [P, 2, 2, NT])
        den = sb("den", [P, 2, 2, NT])
        rec = sb("rec", [P, 2, 2, NT])
        xA_ps = k.banks[0:2]
        s_ps, pT_ps = k.banks[2:4], k.banks[4:6]
        o_ps, y_ps = k.banks[6], k.banks[7]
        names = ("chain", "var", "std", "rstd", "xn", "ht_mm", "ht", "ht_rounded", "ht_cut", "A_mm", "A_rounded", "A_cut",
                 "xA_mm", "xA_rounded", "xA", "v", "s_mm",
                 "nmax", "masked", "exp", "den", "rec", "p", "pT_mm", "pT0", "pT1", "o_mm", "oT", "y_mm", "res")
        s = signals(nc, ctx, "a0_", names)
        LAST, LEAD, LAG = PER - 1, 6, 3

        def halves(x, i, first, end):
            return [x[:, i, part, first:end] for part in range(2)]

        with nc.Block() as block:

            @block.sync
            def _(sp):
                prefetch(sp, nc, k, d, phase)

            @block.gpsimd
            def _(pool):
                def step(at):
                    ni = at.shift(4)
                    if at.p == 4 and ni.real:
                        cut_hT_rest(pool, n, ni, s["ht_rounded"], s["ht_cut"])

                walk(pool, PER, 2, LEAD, LAG, step)

            @block.scalar
            def _(act):
                std_of_rows(act, n, s["var"], s["std"])
                for h in range(2 * PER):
                    act.wait_ge(s["A_mm"], h + 1)
                    act.activation(A[:, h, 0, :], k.banks[h % 4][:, 0:P], ACT.Identity, scale=64 ** -0.5
                                   ).then_inc(s["A_rounded"], 1)

                def step(at):
                    nx, b1, b2 = at.shift(1), at.shift(-1), at.shift(-2)
                    if b2.real:
                        wait(act, s["o_mm"], b2)
                        wait(act, s["y_mm"], b2.shift(-2))
                        act.copy(oT[:, b2.ring(2), :], o_ps[:, 0:T]).then_inc(s["oT"], 1)
                    if nx.real:
                        wait(act, s["s_mm"], nx.shift(-2), 2)
                        for h in range(2):
                            wait(act, s["xA_mm"], nx, 2, 1 - h)
                            act.copy(xA[:, 2 * nx.ring(2) + h, 0, :], xA_ps[h][:, 0:T]).then_inc(s["xA_rounded"], 1)
                        wait(act, s["o_mm"], nx.shift(-4))
                        act.copy(v[:, nx.ring(4)], xA_ps[1][:, T:2 * T].rearrange("p (t d) -> p t d", t=NT)).then_inc(s["v"], 1)
                    if at.p == 4:
                        ni = at.shift(4)
                        if ni.real:
                            wait(act, s["ht_mm"], ni, item=True)
                            modulated(act, k, phase, ni, xA_ps[0][:, T:2 * T], n.hT[:, ni.s // PER % 2, :], s["ht"])
                            cut_hT(act, n, ni, s["ht"], s["ht_rounded"])
                    if b1.real:
                        wait(act, s["pT_mm"], b1, 2)
                        wait(act, s["o_mm"], b1.shift(-2))
                        act.copy(pT[:, b1.ring(2), 1, :], pT_ps[1][:, 0:C]).then_inc(s["pT1"], 1)
                    if at.real:
                        r = at.ring(2)
                        for h in range(2):
                            wait(act, s["nmax"], at, 2, 1 - h)
                            wait(act, s["masked"], at, 2, 1 - h)
                            wait(act, s["pT_mm"], at.shift(-2), 2)
                            act.activation(p[:, r, h, 0:P], s_ps[h][:, 0:P], ACT.Exp,
                                           bias=nmax[:, r, h, 0:1], accum_out=sums[:, r, h, 0:1])
                            act.activation(p[:, r, h, P:C], s_ps[h][:, T:2 * T], ACT.Exp,
                                           bias=nmax[:, r, h, 1:2], accum_out=sums[:, r, h, 1:2]
                                           ).then_inc(s["exp"], 1)

                walk(act, PER, 2, LEAD, LAG, step)

            @block.tensor
            def _(pe):
                pe.wait_ge(k.weights_in[phase], 16 * len(WEIGHTS[phase]))
                for h in range(2 * PER):
                    if h >= 4:
                        pe.wait_ge(s["A_cut"], h - 3)
                    pe.matmul(k.banks[h % 4][:, 0:P], w["wqT0"][:, h, :], w["wkT0"][:, h, :], start=True, stop=True
                              ).then_inc(s["A_mm"], 1)
                pe.wait_ge(s["A_cut"], 2 * PER)

                def step(at):
                    nx, b1, b2 = at.shift(1), at.shift(-1), at.shift(-2)
                    if nx.real:
                        c, item = nx.p * P, nx.s // PER % 2
                        if nx.p == 0:
                            wait(pe, s["ht_cut"], nx, item=True)
                        if at.p == 5:
                            wait(pe, s["ht"], at.shift(3), item=True)
                        for h in range(2):
                            wait(pe, s["xA"], nx.shift(-1), 2, 1 - h)
                            for t in range(NT if h else 0):
                                pe.matmul(xA_ps[1][:, T + t * P:T + (t + 1) * P], n.hT[:, item, t * P:(t + 1) * P],
                                          w["wv0"][:, c:c + P], start=True, stop=True)
                            matmul3(pe, xA_ps[h][:, 0:T], halves(A, 2 * nx.p + h, 0, P), halves(n.hT2, item, 0, T)
                                    ).then_inc(s["xA_mm"], 1)
                    if at.real:
                        for h in range(2):
                            wait(pe, s["xA"], at, 2, 1 - h)
                            wait(pe, s["exp"], at.shift(-1), 2, 1 - h)
                            for t in range(NT):
                                mm = matmul3(pe, s_ps[h][:, t * T:(t + 1) * T],
                                             halves(xA, 2 * at.ring(2) + h, t * P, (t + 1) * P),
                                             halves(n.hT2, at.s // PER % 2, 0, T), start=(t == 0))
                            mm.then_inc(s["s_mm"], 1)
                    ni = at.shift(4)
                    if at.p == 4 and ni.real:
                        wait(pe, s["xn"], ni, item=True)
                        wait(pe, s["xA"], nx, 2, 1)
                        for t in range(NT):
                            mm = pe.transpose(xA_ps[0][:, T + t * P:T + (t + 1) * P], n.xn[:, t, :], k.ident[:])
                        mm.then_inc(s["ht_mm"], 1)
                    if b1.real:
                        wait(pe, s["p"], b1)
                        wait(pe, s["pT0"], b1.shift(-1))
                        wait(pe, s["pT1"], b1.shift(-1))
                        for h in range(2):
                            causal_transposes(pe, pT_ps[h], p[:, b1.ring(2), h, :], k.ident[:]).then_inc(s["pT_mm"], 1)
                    if b2.real:
                        wait(pe, s["oT"], b2)
                        before = b2.shift(-PER)
                        if b2.p == 0 and before.real:
                            pe.wait_ge(s["chain"], before.item * 3 + 3)
                        for t in range(NT):
                            mm = pe.matmul(y_ps[:, t * P:(t + 1) * P], oT[:, b2.ring(2), t * P:(t + 1) * P],
                                           w["wo0"][:, b2.p, :], start=(b2.p == 0 and t == 0),
                                           stop=(b2.p == LAST), skip_group_check=True)
                        mm.then_inc(s["y_mm"], 1)
                    if at.real:
                        for h in range(2):
                            wait(pe, s["nmax"], at, 2, 1 - h)
                            pe.matmul(s_ps[h][:, 0:P], k.ident_bf[:], k.causal_bf[:], start=False, stop=True,
                                      skip_group_check=True)
                            pe.matmul(s_ps[h][:, T + P:2 * T], k.ident_bf[:], k.causal_bf[:], start=False, stop=True,
                                      skip_group_check=True).then_inc(s["masked"], 1)
                    if b1.real:
                        wait(pe, s["pT0"], b1)
                        wait(pe, s["pT1"], b1)
                        wait(pe, s["v"], b1)
                        wait(pe, s["oT"], b1.shift(-1))
                        r = b1.ring(2)
                        for j in range(NT):
                            for h in range(2):
                                mm = pe.matmul(o_ps[64 * h:64 * h + 64, j * P:T],
                                               v[:, b1.ring(4), j, 64 * h:64 * h + 64],
                                               pT[:, r, h, 0:T] if j == 0 else pT[:, r, h, T:C],
                                               start=(j == 0), stop=(j == 1), skip_group_check=True)
                        mm.then_inc(s["o_mm"], 1)

                walk(pe, PER, 2, LEAD, LAG, step)

            @block.vector
            def _(dve):
                var_of_rows(dve, n, s["chain"], s["var"])
                rstd_of_rows(dve, n, s["std"], s["rstd"])
                dve.wait_ge(k.weights_in[phase], 16 * len(WEIGHTS[phase]))
                for h in range(2 * PER):
                    dve.wait_ge(s["A_rounded"], h + 1)
                    dve.scalar_tensor_tensor(out=A[:, h, 1, :], in0=k.banks[h % 4][:, 0:P], scalar=64 ** -0.5,
                                             in1=A[:, h, 0, :], op0=ALU.mult, op1=ALU.subtract).then_inc(s["A_cut"], 1)
                dve.wait_ge(k.gate_in[phase], 16)

                def residual(item, *parts):
                    return add_residual(dve, n, item, y_ps[:, 0:T].rearrange("p (t d) -> p t d", t=NT),
                                        k.gate[phase % 2], w["bo0"].unsqueeze(1).to_broadcast([P, NT, P]), s["chain"],
                                        3, parts)

                def step(at):
                    nx, b1, b2 = at.shift(1), at.shift(-1), at.shift(-2)
                    ended = b2.real and b2.p == LAST
                    after = at.shift(-3).real and at.p == 2
                    if after:
                        residual(at.shift(-3), "add")
                    if at.p == 2 and at.shift(6).real:
                        normalise(dve, n, at.shift(6), s["ht_mm"], s["xn"])
                    if b1.real:
                        r = b1.ring(2)
                        wait(dve, s["exp"], b1, 2)
                        dve.tensor_scalar(den[:, r], sums[:, r], EPS, None, ALU.add).then_inc(s["den"], 1)
                        wait(dve, s["den"], b1)
                        dve.reciprocal(rec[:, r], den[:, r]).then_inc(s["rec"], 1)
                        wait(dve, s["rec"], b1)
                        for h in range(2):
                            for t in range(NT):
                                c = p[:, r, h, 0:P] if t == 0 else p[:, r, h, P:C]
                                i = dve.tensor_scalar(c, c, rec[:, r, h, t:t + 1], None, ALU.mult)
                        i.then_inc(s["p"], 1)
                    if nx.real:
                        for h in range(2):
                            if h == 0:
                                wait(dve, s["xA_rounded"], nx, 2, 1)
                            else:
                                wait(dve, s["v"], nx)
                            dve.tensor_tensor(xA[:, 2 * nx.ring(2) + h, 1, :], xA_ps[h][:, 0:T],
                                              xA[:, 2 * nx.ring(2) + h, 0, :], ALU.subtract).then_inc(s["xA"], 1)
                    if after:
                        residual(at.shift(-3), "stats").then_inc(s["res"], 1)
                    if at.real:
                        for h in range(2):
                            wait(dve, s["s_mm"], at, 2, 1 - h)
                            wait(dve, s["exp"], at.shift(-2), 2)
                            dve.tensor_reduce(nmax[:, at.ring(2), h, :],
                                              s_ps[h][:].rearrange("p (t k) -> p t k", t=NT), AX_X, ALU.max,
                                              negate=True).then_inc(s["nmax"], 1)
                    if ended:
                        wait(dve, s["y_mm"], b2)
                        residual(b2, "bias")
                    if b1.real:
                        wait(dve, s["pT_mm"], b1, 2, 1)
                        wait(dve, s["o_mm"], b1.shift(-2))
                        dve.tensor_copy(pT[:, b1.ring(2), 0, :], pT_ps[0][:, 0:C]).then_inc(s["pT0"], 1)
                    if ended:
                        residual(b2, "gate")

                walk(dve, PER, 2, LEAD, LAG, step)


def prefetch(sp, nc, k, d, phase):
    if phase + 1 < len(WEIGHTS):
        load_weights(sp, nc, k, d, phase + 1)
        load_gate(sp, k, phase + 1)


def build(nc, d, out, phases, first=0):
    with ExitStack() as ctx:
        k = Shared()
        k.norms = Norms(nc, ctx)
        k.banks = [ctx.enter_context(nc.psum_tensor(f"bank{i}", [P, 512], F32)) for i in range(8)]
        k.ident = ctx.enter_context(nc.sbuf_tensor("ident", [P, P], F32))
        k.ident_bf = ctx.enter_context(nc.sbuf_tensor("ident_bf", [P, P], BF16))
        k.causal_bf = ctx.enter_context(nc.sbuf_tensor("causal_bf", [P, P], BF16))
        k.spare = ctx.enter_context(nc.sbuf_tensor("spare", [1, 1], F32))[:]
        k.mod = ctx.enter_context(nc.sbuf_tensor("mod", [P, 8, 2, NB], F32))
        k.gate = [ctx.enter_context(nc.sbuf_tensor(f"gate{i}", [P, NB, P], F32)) for i in range(2)]
        k.arena = [ctx.enter_context(nc.sbuf_tensor(f"arena{i}", [P, ARENA[i]], F32)) for i in range(2)]
        k.gates_dram = nc.dram_tensor("gates_dram", (NB, 8, P), F32, kind="Internal").ap()
        k.weights_in = [ctx.enter_context(nc.semaphore(f"weights_in{i}")) for i in range(len(WEIGHTS))]
        k.gate_in = [ctx.enter_context(nc.semaphore(f"gate_in{i}")) for i in range(len(WEIGHTS))]
        stored = ctx.enter_context(nc.semaphore("stored"))
        prologue(nc, d, k, first)
        for f in phases:
            f(nc, d, k)
        with nc.Block() as block:

            @block.sync
            def _(sp):
                for g in range(4):
                    sp.dma_start(out.rearrange("b (t p) d -> p b t d", p=P)[:, 4 * g:4 * g + 4],
                                 k.norms.x[:, 4 * g:4 * g + 4]).then_inc(stored, 16)
                sp.wait_ge(stored, 64)


def start_norms(dve, n, s):
    var_of_rows(dve, n, s["chain"], s["var"])
    rstd_of_rows(dve, n, s["std"], s["rstd"])


def softmax_top(dve, s, spare, at, E, K, r, b, acc_each=1, transposed=True):
    k = at.item * 5

    def link(i, m):
        i.then_inc(s["top"], 1)
        dve.wait_ge(s["top"], k + m)

    wait(dve, s["rexp"], at, item=True)
    link(dve.reciprocal(b["rec"][:], b["sums"][:]), 1)
    for t in range(NT):
        i = dve.tensor_scalar(b["probs"][:, t, 0:E], b["e"][:, t, :], b["rec"][:, t:t + 1], None, ALU.mult)
    link(i, 2)
    hold(dve, spare)
    for t in range(NT):
        i = dve.max(b["max8"][:, t, :], b["probs"][:, t, :])
    link(i, 3)
    link(dve.tensor_copy(b["top"][:, :, 0:K], b["max8"][:, :, 0:K]), 4)
    hold(dve, spare)
    for t in range(NT):
        i = dve.match_replace(b["rest"][:, t, :], b["top"][:, t, :], b["probs"][:, t, :], 0.0)
    link(i, 5)
    before = at.shift(-at.per)
    wait(dve, s["acc"], before.shift(-before.p - 1), acc_each)
    if transposed:
        wait(dve, s["cwT_mm"], at.shift(-2 * at.per), item=True)
    dve.tensor_tensor(b["cw"][:, r, :, 0:E], b["probs"][:, :, 0:E], b["rest"][:, :, 0:E], ALU.subtract).then_inc(s["cw"], 1)


def router_tiles(nc, ctx, pre, E):
    b = {}

    def sb(name, *shape):
        b[name] = ctx.enter_context(nc.sbuf_tensor(pre + name, [P, *shape], F32))

    sb("logits", NT, E)
    sb("e", NT, E)
    sb("nmax", NT)
    sb("sums", NT)
    sb("rec", NT)
    sb("probs", NT, E + 8)
    sb("rest", NT, E + 8)
    sb("max8", NT, 8)
    sb("top", NT, 8)
    sb("cw", 2, NT, 16)
    return b


def ffn0(nc, d, k):
    phase, PER, E, K = 1, 16, 15, 3
    n = k.norms
    w = weights(k, phase)
    with ExitStack() as ctx:
        def sb(name, shape):
            return ctx.enter_context(nc.sbuf_tensor("f0_" + name, shape, F32))

        hidden = sb("hidden", [P, 2, T])
        acc = sb("acc", [P, NT, P])
        cwT = sb("cwT", [16, 2, T])
        b = router_tiles(nc, ctx, "f0_", E)
        h_ps, y_ps = k.banks[0:2], k.banks[2:4]
        ht_ps, rt_ps, cwT_ps = k.banks[4], k.banks[5], k.banks[6]
        names = ("chain", "var", "std", "rstd", "xn", "ht_mm", "ht", "rt_mm", "logits", "nmax", "rexp", "top", "cw",
                 "cwT_mm", "cwT", "h_mm", "hidden", "y_mm", "acc", "res", "pads")
        s = signals(nc, ctx, "f0_", names)
        LAST = PER - 1

        with nc.Block() as block:

            @block.sync
            def _(sp):
                prefetch(sp, nc, k, d, phase)

            @block.scalar
            def _(act):
                std_of_rows(act, n, s["var"], s["std"])
                act.wait_ge(k.weights_in[phase], 16 * len(WEIGHTS[phase]))

                def step(at):
                    nx, ni = at.shift(1), at.shift(PER)
                    if nx.real:
                        wait(act, s["h_mm"], nx)
                        wait(act, s["y_mm"], nx.shift(-2))
                        act.activation(hidden[:, nx.ring(2), :], h_ps[nx.ring(2)][:, 0:T], ACT.Relu,
                                       bias=w["e1b"][:, nx.p:nx.p + 1]).then_inc(s["hidden"], 1)
                    r = (at.s // PER + 1) % 2
                    if at.p == 6 and ni.real:
                        wait(act, s["ht_mm"], ni, item=True)
                        wait(act, s["h_mm"], at.shift(-7))
                        modulated(act, k, phase, ni, ht_ps[:, 0:T], n.hT[:, r, :], s["ht"])
                    if at.p == 9 and ni.real:
                        wait(act, s["nmax"], ni, item=True)
                        for t in range(NT):
                            i = act.activation(b["e"][:, t, :], b["logits"][:, t, :], ACT.Exp, bias=b["nmax"][:, t:t + 1],
                                               accum_out=b["sums"][:, t:t + 1])
                        i.then_inc(s["rexp"], 1)
                    if at.p == 13 and ni.real:
                        wait(act, s["cwT_mm"], ni, item=True)
                        wait(act, s["y_mm"], at.shift(-14))
                        act.copy(cwT[:, r, :], cwT_ps[0:16, 0:T]).then_inc(s["cwT"], 1)

                walk(act, PER, 2, 12, 1, step)

            @block.tensor
            def _(pe):
                pe.wait_ge(k.weights_in[phase], 16 * len(WEIGHTS[phase]))

                def step(at):
                    nx, ni = at.shift(1), at.shift(PER)
                    if nx.real:
                        if nx.p == 0:
                            wait(pe, s["ht"], nx, item=True)
                        wait(pe, s["hidden"], nx.shift(-2))
                        pe.matmul(h_ps[nx.ring(2)][:, 0:T], w["e1w"][:, nx.p, :], n.hT[:, nx.s // PER % 2, :],
                                  start=True, stop=True).then_inc(s["h_mm"], 1)
                    r = (at.s // PER + 1) % 2
                    if at.p == 6 and ni.real:
                        wait(pe, s["xn"], ni, item=True)
                        wait(pe, s["ht"], ni.shift(-PER), item=True)
                        for t in range(NT):
                            mm = pe.transpose(ht_ps[:, t * P:(t + 1) * P], n.xn[:, t, :], k.ident[:])
                        mm.then_inc(s["ht_mm"], 1)
                    if at.p == 8 and ni.real:
                        wait(pe, s["ht"], ni, item=True)
                        wait(pe, s["logits"], ni.shift(-PER), item=True)
                        for t in range(NT):
                            mm = pe.matmul(rt_ps[:, t * E:(t + 1) * E], n.hT[:, r, t * P:(t + 1) * P], w["rw"][:],
                                           start=True, stop=True)
                        mm.then_inc(s["rt_mm"], 1)
                    if at.p == 13 and ni.real:
                        wait(pe, s["cw"], ni, item=True)
                        wait(pe, s["cwT"], ni.shift(-PER), item=True)
                        for t in range(NT):
                            mm = pe.transpose(cwT_ps[0:16, t * P:(t + 1) * P], b["cw"][:, r, t, :], k.ident[:])
                        mm.then_inc(s["cwT_mm"], 1)
                    if at.real:
                        wait(pe, s["hidden"], at)
                        wait(pe, s["acc"], at.shift(-2))
                        last = at.p == LAST
                        if last:
                            wait(pe, s["cwT"], at, item=True)
                        for t in range(NT):
                            y = y_ps[at.ring(2)][:, t * P:(t + 1) * P]
                            mm = pe.matmul(y, hidden[:, at.ring(2), t * P:(t + 1) * P], w["e2w"][:, at.p, :],
                                           start=(t == 0), stop=not last, skip_group_check=True)
                            if last:
                                mm = pe.matmul(y, cwT[:, at.s // PER % 2, t * P:(t + 1) * P], w["e2b"][:],
                                               start=False, stop=True, skip_group_check=True)
                        mm.then_inc(s["y_mm"], 1)

                walk(pe, PER, 2, 12, 1, step)

            @block.vector
            def _(dve):
                start_norms(dve, n, s)
                dve.memset(b["probs"][:], -1.0)
                dve.memset(b["top"][:], -1.0)
                dve.memset(b["cw"][:], 1.0).then_inc(s["pads"], 1)
                dve.wait_ge(s["pads"], 1)
                dve.wait_ge(k.weights_in[phase], 16 * len(WEIGHTS[phase]))
                dve.wait_ge(k.gate_in[phase], 16)

                def step(at):
                    ni = at.shift(PER)
                    r = (at.s // PER + 1) % 2
                    if at.p == 4 and ni.real:
                        normalise(dve, n, ni, s["ht_mm"], s["xn"])
                    if at.p == 9 and ni.real:
                        wait(dve, s["rt_mm"], ni, item=True)
                        dve.tensor_tensor(b["logits"][:], rt_ps[:, 0:NT * E].rearrange("p (t e) -> p t e", t=NT),
                                          w["rb"][:].unsqueeze(1).to_broadcast([P, NT, E]), ALU.add).then_inc(s["logits"], 1)
                        wait(dve, s["logits"], ni, item=True)
                        dve.tensor_reduce(b["nmax"][:], b["logits"][:], AX_X, ALU.max, negate=True).then_inc(s["nmax"], 1)
                    if at.p == 11 and ni.real:
                        softmax_top(dve, s, k.spare, ni, E, K, r, b)
                    if at.real:
                        wait(dve, s["y_mm"], at)
                        wait(dve, s["acc"], at.shift(-1))
                        y, c = y_ps[at.ring(2)], b["cw"][:, at.s // PER % 2]
                        if at.p == 0:
                            wait(dve, s["cw"], at, item=True)
                            wait(dve, s["res"], at.shift(-PER), item=True)
                        if at.p == LAST:
                            dve.tensor_tensor(acc[:], acc[:], y[:, 0:T].rearrange("p (t d) -> p t d", t=NT),
                                              ALU.add).then_inc(s["acc"], 1)
                            wait(dve, s["acc"], at)
                            add_residual(dve, n, at, acc[:], k.gate[phase % 2], None, s["chain"], 2, ALL_PARTS
                                         ).then_inc(s["res"], 1)
                            return
                        for t in range(NT):
                            a, z = acc[:, t, :], y[:, t * P:(t + 1) * P]
                            if at.p == 0:
                                i = dve.tensor_scalar(a, z, c[:, t, 0:1], None, ALU.mult)
                            else:
                                i = dve.scalar_tensor_tensor(out=a, in0=z, scalar=c[:, t, at.p:at.p + 1], in1=a,
                                                             op0=ALU.mult, op1=ALU.add)
                        i.then_inc(s["acc"], 1)

                walk(dve, PER, 2, 12, 1, step)


def attention1(nc, d, k):
    phase, PER = 2, 8
    n = k.norms
    w = weights(k, phase)
    SCALE = P ** -0.5
    SPAN = T + P - 1
    PITCH = SPAN + 1
    with ExitStack() as ctx:
        def sb(name, shape):
            return ctx.enter_context(nc.sbuf_tensor("a1_" + name, shape, F32))

        def cut_sb(name, shape):
            return ctx.enter_context(nc.sbuf_tensor("a1_" + name, shape, F32R))

        A = cut_sb("A", [P, PER, 2, P])
        R = cut_sb("R", [P, PER, 2, 2 * T])
        c_col = sb("c_col", [P, PER])
        r_rows = sb("r_rows", [P, PER, 2 * T])
        r_row = sb("r_row", [PER, 2 * T])
        WrelWq = sb("WrelWq", [96, 2, 2, P])
        Wrel_bias = sb("Wrel_bias", [96, 2, PER])
        xA = cut_sb("xA", [P, 2, 2, T])
        v = sb("v", [P, 4, NT, P])
        pos = sb("pos", [P, 2, NT, PITCH])
        shifted = sb("shifted", [P, 2, NT, T])
        p = sb("p", [P, 2, NT, T])
        pT = sb("pT", [P, 2, NT, T])
        oT = sb("oT", [P, 2, T])
        top = sb("top", [P, 2, NT])
        nmax = sb("nmax", [P, 2, NT])
        sums = sb("sums", [P, 2, NT])
        rec = sb("rec", [P, 2, NT])
        r_dram = nc.dram_tensor("r_dram", (PER, 2 * T), F32, kind="Internal").ap()
        pos_dram = nc.dram_tensor("pos_dram", (4, NT, P, PITCH), F32, kind="Internal").ap()
        qh_ps, v_ps, pos_ps = k.banks[0], k.banks[1], k.banks[2:4]
        s_ps, pT_ps, o_ps, y_ps = k.banks[4:8]
        names = ("chain", "var", "std", "rstd", "xn", "ht_mm", "ht", "ht_rounded", "ht_cut", "bias_mm", "bias", "r_mm",
                 "r_row", "r_out", "r_in", "A_mm", "A_rounded", "A_cut", "WW_mm", "WW", "R_mm", "R_rounded", "R_cut",
                 "xA_mm", "xA_rounded", "xA", "v_mm", "v", "pos_mm", "pos", "s_mm", "sc", "nmax", "exp", "rec", "p",
                 "pT_mm", "pT", "o_mm", "oT", "y_mm", "res")
        s = signals(nc, ctx, "a1_", names + tuple(f"{x}{i}" for x in ("written", "shifted") for i in range(4)))
        written, shifted_in = ([s[f"{x}{i}"] for i in range(4)] for x in ("written", "shifted"))
        LAST = PER - 1
        LEAD, LAG = 7, 3

        def halves(x, i, first, end):
            return [x[:, i, part, first:end] for part in range(2)]

        with nc.Block() as block:

            @block.sync
            def _(sp):
                prefetch(sp, nc, k, d, phase)
                sp.wait_ge(s["r_row"], 1)
                sp.dma_start(r_dram, r_row[:]).then_inc(s["r_out"], 16)
                sp.wait_ge(s["r_out"], 16)
                sp.dma_start(r_rows[:].rearrange("p h d -> p (h d)"), bass.AP(r_dram.tensor, 0, [[0, P], [1, PER * 2 * T]])
                             ).then_inc(s["r_in"], 16)

                def step(at):
                    n1, n2 = at.shift(1), at.shift(2)
                    if n1.real:
                        wait_ring(sp, written, n1)
                        start = n1.ring(4) * NT * P * PITCH + P - 1
                        skewed = bass.AP(pos_dram.tensor, start, [[PITCH - 1, P], [P * PITCH, NT], [1, T]])
                        sp.dma_start(shifted[:, n1.ring(2)], skewed).then_inc(shifted_in[n1.ring(4)], 16)
                    if n2.real:
                        wait(sp, s["pos"], n2)
                        sp.dma_start(pos_dram[n2.ring(4)].rearrange("t p c -> p t c")[:, :, 0:SPAN],
                                     pos[:, n2.ring(2), :, 0:SPAN]).then_inc(written[n2.ring(4)], 16)

                walk(sp, PER, 2, LEAD, LAG, step)

            @block.gpsimd
            def _(pool):
                def step(at):
                    ni = at.shift(5)
                    if at.p == 3 and ni.real:
                        cut_hT_rest(pool, n, ni, s["ht_rounded"], s["ht_cut"])

                walk(pool, PER, 2, LEAD, LAG, step)

            @block.scalar
            def _(act):
                std_of_rows(act, n, s["var"], s["std"])

                def round_R(h):
                    act.wait_ge(s["R_mm"], h + 1)
                    act.copy(R[:, h, 0, :], k.banks[4 + h % 2][:]).then_inc(s["R_rounded"], 1)

                for h in range(PER):
                    act.wait_ge(s["A_mm"], h + 1)
                    act.activation(A[:, h, 0, :], k.banks[h % 2][:, 0:P], ACT.Identity, scale=SCALE
                                   ).then_inc(s["A_rounded"], 1)
                    act.wait_ge(s["WW_mm"], h + 1)
                    if h >= 2:
                        act.wait_ge(s["R_mm"], h - 1)
                    act.activation(WrelWq[:, h % 2].rearrange("p c d -> p (c d)"), k.banks[2 + h % 2][0:96, 0:T],
                                   ACT.Identity, scale=SCALE).then_inc(s["WW"], 1)
                    if h:
                        round_R(h - 1)
                round_R(PER - 1)

                def step(at):
                    n2, b1, b2 = at.shift(2), at.shift(-1), at.shift(-2)
                    if b2.real:
                        wait(act, s["o_mm"], b2)
                        wait(act, s["y_mm"], b2.shift(-2))
                        act.copy(oT[:, b2.ring(2), :], o_ps[:, 0:T]).then_inc(s["oT"], 1)
                    if n2.real:
                        wait(act, s["xA_mm"], n2)
                        wait(act, s["s_mm"], n2.shift(-2))
                        act.activation(xA[:, n2.ring(2), 0, :], qh_ps[:, 0:T], ACT.Identity,
                                       bias=c_col[:, n2.p:n2.p + 1]).then_inc(s["xA_rounded"], 1)
                        wait(act, s["v_mm"], n2)
                        wait(act, s["o_mm"], n2.shift(-4))
                        act.copy(v[:, n2.ring(4)], v_ps[:, 0:T].rearrange("p (t d) -> p t d", t=NT)
                                 ).then_inc(s["v"], 1)
                    if at.p == 3:
                        ni = at.shift(5)
                        if ni.real:
                            wait(act, s["ht_mm"], ni, item=True)
                            modulated(act, k, phase, ni, qh_ps[:, T:2 * T], n.hT[:, ni.s // PER % 2, :], s["ht"])
                            cut_hT(act, n, ni, s["ht"], s["ht_rounded"])
                    if b1.real:
                        wait(act, s["pT_mm"], b1)
                        wait(act, s["o_mm"], b1.shift(-2))
                        act.copy(pT[:, b1.ring(2)], pT_ps[:].rearrange("p (j q) -> p j q", j=NT)
                                 ).then_inc(s["pT"], 1)
                    if at.real:
                        r = at.ring(2)
                        wait(act, s["nmax"], at)
                        wait(act, s["pT_mm"], at.shift(-2))
                        for t in range(NT):
                            i = act.activation(p[:, r, t, :], p[:, r, t, :], ACT.Exp, bias=nmax[:, r, t:t + 1],
                                               accum_out=sums[:, r, t:t + 1])
                        i.then_inc(s["exp"], 1)

                walk(act, PER, 2, LEAD, LAG, step)

            @block.tensor
            def _(pe):
                pe.wait_ge(k.weights_in[phase], 16 * len(WEIGHTS[phase]))
                for h in range(PER):
                    pe.matmul(k.banks[6][:, h:h + 1], w["wkT"][:, h, :], w["qb1"][:, 0, h:h + 1], start=True, stop=True)
                    for c in range(2):
                        col = (1 + c) * PER + h
                        mm = pe.matmul(k.banks[6][0:96, col:col + 1], w["w_relT"][:, h, c, :], w["qb1"][:, 1, h:h + 1],
                                       start=True, stop=True)
                mm.then_inc(s["bias_mm"], 1)

                def make_R(h):
                    pe.wait_ge(s["WW"], h + 1)
                    if h >= 2:
                        pe.wait_ge(s["R_cut"], h - 1)
                    for c in range(2):
                        mm = pe.matmul(k.banks[4 + h % 2][:], WrelWq[:, h % 2, c, :], w["positions"][:, c, :],
                                       start=(c == 0), stop=(c == 1))
                    mm.then_inc(s["R_mm"], 1)

                for h in range(PER):
                    if h >= 2:
                        pe.wait_ge(s["A_cut"], h - 1)
                    pe.matmul(k.banks[h % 2][:, 0:P], w["wqT"][:, h, :], w["wkT"][:, h, :], start=True, stop=True
                              ).then_inc(s["A_mm"], 1)
                    if h >= 2:
                        pe.wait_ge(s["WW"], h - 1)
                    for c in range(2):
                        mm = pe.matmul(k.banks[2 + h % 2][0:96, c * P:(c + 1) * P], w["w_relT"][:, h, c, :],
                                       w["wqT"][:, h, :], start=True, stop=True)
                    mm.then_inc(s["WW_mm"], 1)
                    if h == 1:
                        pe.wait_ge(s["bias"], 1)
                        for c in range(2):
                            mm = pe.matmul(k.banks[7][0:PER, :], Wrel_bias[:, c, :], w["positions"][:, c, :],
                                           start=(c == 0), stop=(c == 1))
                        mm.then_inc(s["r_mm"], 1)
                    if h:
                        make_R(h - 1)
                make_R(PER - 1)
                pe.wait_ge(s["A_cut"], PER)
                pe.wait_ge(s["R_cut"], PER)
                pe.wait_ge(s["r_row"], 1)

                def step(at):
                    n2, b1, b2 = at.shift(2), at.shift(-1), at.shift(-2)
                    if n2.real:
                        c, item = n2.p * P, n2.s // PER % 2
                        if n2.p == 0:
                            wait(pe, s["ht_cut"], n2, item=True)
                        wait(pe, s["xA"], n2.shift(-1))
                        matmul3(pe, qh_ps[:, 0:T], halves(A, n2.p, 0, P), halves(n.hT2, item, 0, T)
                                ).then_inc(s["xA_mm"], 1)
                        wait(pe, s["v"], n2.shift(-1))
                        for t in range(NT):
                            mm = pe.matmul(v_ps[:, t * P:(t + 1) * P], n.hT[:, item, t * P:(t + 1) * P],
                                           w["wv1"][:, c:c + P], start=True, stop=True)
                        mm.then_inc(s["v_mm"], 1)
                    if at.real:
                        wait(pe, s["xA"], at)
                        wait(pe, s["sc"], at.shift(-1))
                        for t in range(NT):
                            mm = matmul3(pe, s_ps[:, t * T:(t + 1) * T], halves(xA, at.ring(2), t * P, (t + 1) * P),
                                         halves(n.hT2, at.s // PER % 2, 0, T))
                        mm.then_inc(s["s_mm"], 1)
                    ni = at.shift(5)
                    if at.p == 3 and ni.real:
                        wait(pe, s["xn"], ni, item=True)
                        wait(pe, s["xA"], n2)
                        for t in range(NT):
                            mm = pe.transpose(qh_ps[:, T + t * P:T + (t + 1) * P], n.xn[:, t, :], k.ident[:])
                        mm.then_inc(s["ht_mm"], 1)
                    if b1.real:
                        wait(pe, s["p"], b1)
                        wait(pe, s["pT"], b1.shift(-1))
                        for j in range(NT):
                            for t in range(NT):
                                mm = pe.transpose(pT_ps[:, j * T + t * P:j * T + (t + 1) * P],
                                                  p[:, b1.ring(2), t, j * P:(j + 1) * P], k.ident[:])
                        mm.then_inc(s["pT_mm"], 1)
                    if b2.real:
                        wait(pe, s["oT"], b2)
                        before = b2.shift(-PER)
                        if b2.p == 0 and before.real:
                            pe.wait_ge(s["chain"], before.item * 3 + 3)
                        for t in range(NT):
                            mm = pe.matmul(y_ps[:, t * P:(t + 1) * P], oT[:, b2.ring(2), t * P:(t + 1) * P],
                                           w["wo1"][:, b2.p, :], start=(b2.p == 0 and t == 0), stop=(b2.p == LAST),
                                           skip_group_check=True)
                        mm.then_inc(s["y_mm"], 1)
                    if n2.real:
                        wait(pe, s["pos"], n2.shift(-1))
                        for t in range(NT):
                            first = P if t == 0 else 0
                            mm = matmul3(pe, pos_ps[t][:, 0:PITCH], halves(n.hT2, n2.s // PER % 2, t * P, (t + 1) * P),
                                         halves(R, n2.p, first, first + PITCH))
                        mm.then_inc(s["pos_mm"], 1)
                    if b1.real:
                        wait(pe, s["pT"], b1)
                        wait(pe, s["v"], b1)
                        wait(pe, s["oT"], b1.shift(-1))
                        for j in range(NT):
                            mm = pe.matmul(o_ps[:, 0:T], v[:, b1.ring(4), j, :], pT[:, b1.ring(2), j, :],
                                           start=(j == 0), stop=(j == 1))
                        mm.then_inc(s["o_mm"], 1)

                walk(pe, PER, 2, LEAD, LAG, step)

            @block.vector
            def _(dve):
                start_norms(dve, n, s)
                dve.wait_ge(s["bias_mm"], 1)
                dve.tensor_copy(c_col[:], k.banks[6][:, 0:PER])
                dve.tensor_copy(Wrel_bias[:].rearrange("p c h -> p (c h)"), k.banks[6][0:96, PER:3 * PER]
                                ).then_inc(s["bias"], 1)

                def cut_R(h):
                    dve.wait_ge(s["R_rounded"], h + 1)
                    dve.tensor_tensor(R[:, h, 1, :], k.banks[4 + h % 2][:], R[:, h, 0, :], ALU.subtract
                                      ).then_inc(s["R_cut"], 1)

                for h in range(PER):
                    dve.wait_ge(s["A_rounded"], h + 1)
                    dve.scalar_tensor_tensor(out=A[:, h, 1, :], in0=k.banks[h % 2][:, 0:P], scalar=SCALE,
                                             in1=A[:, h, 0, :], op0=ALU.mult, op1=ALU.subtract).then_inc(s["A_cut"], 1)
                    if h == 1:
                        dve.wait_ge(s["r_mm"], 1)
                        dve.tensor_copy(r_row[:], k.banks[7][0:PER, :]).then_inc(s["r_row"], 1)
                    if h:
                        cut_R(h - 1)
                cut_R(PER - 1)
                dve.wait_ge(s["r_in"], 16)
                dve.wait_ge(k.gate_in[phase], 16)

                def residual(item, *parts):
                    return add_residual(dve, n, item, y_ps[:, 0:T].rearrange("p (t d) -> p t d", t=NT),
                                        k.gate[phase % 2], w["bo1"].unsqueeze(1).to_broadcast([P, NT, P]), s["chain"],
                                        3, parts)

                def step(at):
                    n2, b1, b2 = at.shift(2), at.shift(-1), at.shift(-2)
                    ended = b2.real and b2.p == LAST
                    after = at.shift(-3).real and at.p == 2
                    if after:
                        residual(at.shift(-3), "add")
                    if at.p == 1 and at.shift(7).real:
                        normalise(dve, n, at.shift(7), s["ht_mm"], s["xn"])
                    if b1.real:
                        r = b1.ring(2)
                        wait(dve, s["exp"], b1)
                        dve.reciprocal(rec[:, r], sums[:, r]).then_inc(s["rec"], 1)
                        wait(dve, s["rec"], b1)
                        for t in range(NT):
                            i = dve.tensor_scalar(p[:, r, t, :], p[:, r, t, :], rec[:, r, t:t + 1], None, ALU.mult)
                        i.then_inc(s["p"], 1)
                    if after:
                        residual(at.shift(-3), "stats").then_inc(s["res"], 1)
                    if n2.real:
                        wait(dve, s["xA_rounded"], n2)
                        dve.scalar_tensor_tensor(out=xA[:, n2.ring(2), 1, :], in0=qh_ps[:, 0:T],
                                                 scalar=c_col[:, n2.p:n2.p + 1], in1=xA[:, n2.ring(2), 0, :],
                                                 op0=ALU.add, op1=ALU.subtract).then_inc(s["xA"], 1)
                    if at.real:
                        r = at.ring(2)
                        wait(dve, s["s_mm"], at)
                        wait_ring(dve, shifted_in, at)
                        wait(dve, s["pT_mm"], at.shift(-2))
                        hold(dve, k.spare)
                        for t in range(NT):
                            i = dve.tensor_tensor_reduce(p[:, r, t, :], s_ps[:, t * T:(t + 1) * T],
                                                         shifted[:, r, t, :], 1.0, -3e38, ALU.add, ALU.max,
                                                         top[:, r, t:t + 1])
                        i.then_inc(s["sc"], 1)
                        wait(dve, s["sc"], at)
                        dve.tensor_scalar(nmax[:, r], top[:, r], -1.0, None, ALU.mult).then_inc(s["nmax"], 1)
                    if ended:
                        wait(dve, s["y_mm"], b2)
                        residual(b2, "bias")
                    if n2.real:
                        wait(dve, s["pos_mm"], n2)
                        wait_ring(dve, written, n2.shift(-2))
                        for t in range(NT):
                            first = P if t == 0 else 0
                            i = dve.tensor_tensor(pos[:, n2.ring(2), t, :], pos_ps[t][:, 0:PITCH],
                                                  r_rows[:, n2.p, first:first + PITCH], ALU.add)
                        i.then_inc(s["pos"], 1)
                    if ended:
                        residual(b2, "gate")

                walk(dve, PER, 2, LEAD, LAG, step)


def ffn1(nc, d, k):
    phase, PER, E = 3, 8, 8
    n = k.norms
    w = weights(k, phase)
    LOWEST = -3e38
    with ExitStack() as ctx:
        def sb(name, shape):
            return ctx.enter_context(nc.sbuf_tensor("f1_" + name, shape, F32))

        silu = sb("silu", [P, 2, 2 * T])
        hidden = sb("hidden", [P, 2, 2 * T])
        acc = sb("acc", [P, NT, P])
        logits = sb("logits", [P, NT, 2 * E])
        max8 = sb("max8", [P, NT, 8])
        top = sb("top", [P, 2, NT, 8])
        rest = sb("rest", [P, 2, NT, 2 * E])
        is_top = sb("is_top", [P, 2, NT, E])
        gap = sb("gap", [P, NT])
        tilt = sb("tilt", [P, NT])
        second = sb("second", [P, NT])
        part = sb("part", [P, NT, E])
        cw = sb("cw", [P, 2, NT, E])
        w12 = ctx.enter_context(nc.sbuf_tensor("f1_w12", [P, E, 2, 2 * T], F32R))
        h1_ps, h2_ps, y_ps = k.banks[0:2], k.banks[2:4], k.banks[4:6]
        ht_ps, rt_ps = k.banks[6:8]
        names = ("chain", "var", "std", "rstd", "xn", "ht_mm", "ht", "ht_rounded", "ht_cut", "w_rounded", "w_cut", "rt_mm", "logits", "gap", "tilt", "top", "cw",
                 "h1_mm", "h2_mm", "silu", "hidden", "y_mm", "acc", "res", "pads")
        s = signals(nc, ctx, "f1_", names)
        LAST, LEAD, LAG = PER - 1, 8, 1

        with nc.Block() as block:

            @block.sync
            def _(sp):
                prefetch(sp, nc, k, d, phase)

            @block.gpsimd
            def _(pool):
                def step(at):
                    ni = at.shift(PER)
                    if at.p == 2 and ni.real:
                        cut_hT_rest(pool, n, ni, s["ht_rounded"], s["ht_cut"])

                walk(pool, PER, 2, LEAD, LAG, step)

            @block.scalar
            def _(act):
                std_of_rows(act, n, s["var"], s["std"])
                act.wait_ge(k.weights_in[phase], 16 * len(WEIGHTS[phase]))
                for e in range(E):
                    act.copy(w12[:, e, 0, :], w["w12"][:, e, :]).then_inc(s["w_rounded"], 1)

                def step(at):
                    nx, ni = at.shift(1), at.shift(PER)
                    if nx.real:
                        wait(act, s["h1_mm"], nx)
                        wait(act, s["hidden"], nx.shift(-2))
                        act.activation(silu[:, nx.ring(2), :], h1_ps[nx.ring(2)][:], ACT.Silu).then_inc(s["silu"], 1)
                    if at.p == 2 and ni.real:
                        wait(act, s["ht_mm"], ni, item=True)
                        wait(act, s["h2_mm"], at.shift(-3))
                        modulated(act, k, phase, ni, ht_ps[:, 0:T], n.hT[:, (at.s // PER + 1) % 2, :], s["ht"])
                        cut_hT(act, n, ni, s["ht"], s["ht_rounded"])
                    if at.p == 4 and ni.real:
                        wait(act, s["gap"], ni, item=True)
                        act.activation(tilt[:], gap[:], ACT.Tanh, scale=0.5).then_inc(s["tilt"], 1)

                walk(act, PER, 2, LEAD, LAG, step)

            @block.tensor
            def _(pe):
                pe.wait_ge(k.weights_in[phase], 16 * len(WEIGHTS[phase]))

                def step(at):
                    nx, ni = at.shift(1), at.shift(PER)
                    if nx.real:
                        if nx.p == 0:
                            wait(pe, s["ht_cut"], nx, item=True)
                        if isinstance(at.base, int) and nx.s < E:
                            pe.wait_ge(s["w_cut"], nx.s + 1)
                        hT = [n.hT2[:, nx.s // PER % 2, part, :] for part in range(2)]

                        def cols(c):
                            return [w12[:, nx.p, part, c * P:(c + 1) * P] for part in range(2)]

                        wait(pe, s["silu"], nx.shift(-2))
                        for c in range(2):
                            mm = matmul3(pe, h1_ps[nx.ring(2)][:, c * T:(c + 1) * T], cols(c), hT)
                        mm.then_inc(s["h1_mm"], 1)
                        wait(pe, s["hidden"], nx.shift(-2))
                        for c in range(2):
                            mm = matmul3(pe, h2_ps[nx.ring(2)][:, c * T:(c + 1) * T], cols(2 + c), hT)
                        mm.then_inc(s["h2_mm"], 1)
                    if at.p == 1 and ni.real:
                        wait(pe, s["xn"], ni, item=True)
                        wait(pe, s["ht"], ni.shift(-PER), item=True)
                        for t in range(NT):
                            mm = pe.transpose(ht_ps[:, t * P:(t + 1) * P], n.xn[:, t, :], k.ident[:])
                        mm.then_inc(s["ht_mm"], 1)
                    if at.p == 3 and ni.real:
                        wait(pe, s["ht"], ni, item=True)
                        wait(pe, s["logits"], ni.shift(-PER), item=True)
                        for t in range(NT):
                            mm = pe.matmul(rt_ps[:, t * E:(t + 1) * E],
                                           n.hT[:, (at.s // PER + 1) % 2, t * P:(t + 1) * P], w["gw1"][:],
                                           start=True, stop=True)
                        mm.then_inc(s["rt_mm"], 1)
                    if at.real:
                        wait(pe, s["hidden"], at)
                        wait(pe, s["acc"], at.shift(-2))
                        for t in range(NT):
                            for c in range(2):
                                mm = pe.matmul(y_ps[at.ring(2)][:, t * P:(t + 1) * P],
                                               hidden[:, at.ring(2), c * T + t * P:c * T + (t + 1) * P],
                                               w["w3"][:, at.p, c, :], start=(c == 0), stop=(c == 1))
                        mm.then_inc(s["y_mm"], 1)

                walk(pe, PER, 2, LEAD, LAG, step)

            @block.vector
            def _(dve):
                start_norms(dve, n, s)
                dve.memset(logits[:], LOWEST)
                dve.memset(top[:], LOWEST).then_inc(s["pads"], 1)
                dve.wait_ge(s["pads"], 1)
                for e in range(E):
                    dve.wait_ge(s["w_rounded"], e + 1)
                    dve.tensor_tensor(w12[:, e, 1, :], w["w12"][:, e, :], w12[:, e, 0, :], ALU.subtract
                                      ).then_inc(s["w_cut"], 1)
                dve.wait_ge(k.gate_in[phase], 16)

                def step(at):
                    nx, ni = at.shift(1), at.shift(PER)
                    if at.p == 0 and ni.real:
                        normalise(dve, n, ni, s["ht_mm"], s["xn"])
                    if nx.real:
                        wait(dve, s["silu"], nx)
                        wait(dve, s["h2_mm"], nx)
                        wait(dve, s["y_mm"], nx.shift(-2))
                        dve.tensor_tensor(hidden[:, nx.ring(2), :], silu[:, nx.ring(2), :], h2_ps[nx.ring(2)][:],
                                          ALU.mult).then_inc(s["hidden"], 1)
                    steps = ni.item * 4

                    def link(i, m):
                        i.then_inc(s["top"], 1)
                        dve.wait_ge(s["top"], steps + m)

                    if at.p == 3 and ni.real:
                        wait(dve, s["rt_mm"], ni, item=True)
                        dve.tensor_copy(logits[:, :, 0:E], rt_ps[:, 0:NT * E].rearrange("p (t e) -> p t e", t=NT)
                                        ).then_inc(s["logits"], 1)
                        wait(dve, s["logits"], ni, item=True)
                        hold(dve, k.spare)
                        for t in range(NT):
                            i = dve.max(max8[:, t, :], logits[:, t, :])
                        link(i, 1)
                        dve.tensor_tensor(gap[:], max8[:, :, 0], max8[:, :, 1], ALU.subtract).then_inc(s["gap"], 1)
                        dve.tensor_copy(top[:, 0, :, 0:1], max8[:, :, 0:1])
                        link(dve.tensor_copy(top[:, 1, :, 0:2], max8[:, :, 0:2]), 2)
                        hold(dve, k.spare)
                        for m in range(2):
                            for t in range(NT):
                                i = dve.match_replace(rest[:, m, t, :], top[:, m, t, :], logits[:, t, :], LOWEST)
                        link(i, 3)
                    if at.p == 5 and ni.real:
                        wait(dve, s["tilt"], ni, item=True)
                        for m in range(2):
                            dve.tensor_tensor(is_top[:, m], rest[:, m, :, 0:E], logits[:, :, 0:E], ALU.not_equal)
                        link(dve.tensor_scalar(second[:], tilt[:], -0.5, 0.5, ALU.mult, ALU.add), 4)
                        wait(dve, s["acc"], Step(at.base, at.s - at.p - 1, PER))
                        for t in range(NT):
                            i = dve.tensor_scalar(part[:, t, :], is_top[:, 1, t, :], second[:, t:t + 1], None, ALU.mult)
                        i.then_inc(s["cw"], 1)
                        dve.wait_ge(s["cw"], 2 * ni.item + 1)
                        for t in range(NT):
                            i = dve.scalar_tensor_tensor(out=cw[:, (at.s // PER + 1) % 2, t, :], in0=is_top[:, 0, t, :],
                                                         scalar=tilt[:, t:t + 1], in1=part[:, t, :], op0=ALU.mult,
                                                         op1=ALU.add)
                        i.then_inc(s["cw"], 1)
                    if at.real:
                        wait(dve, s["y_mm"], at)
                        wait(dve, s["acc"], at.shift(-1))
                        c = cw[:, at.s // PER % 2]
                        if at.p == 0:
                            wait(dve, s["cw"], at, 2, item=True)
                            wait(dve, s["res"], at.shift(-PER), item=True)
                        for t in range(NT):
                            a, z = acc[:, t, :], y_ps[at.ring(2)][:, t * P:(t + 1) * P]
                            if at.p == 0:
                                i = dve.tensor_scalar(a, z, c[:, t, 0:1], None, ALU.mult)
                            else:
                                i = dve.scalar_tensor_tensor(out=a, in0=z, scalar=c[:, t, at.p:at.p + 1], in1=a,
                                                             op0=ALU.mult, op1=ALU.add)
                        i.then_inc(s["acc"], 1)
                        if at.p == LAST:
                            wait(dve, s["acc"], at)
                            add_residual(dve, n, at, acc[:], k.gate[phase % 2], None, s["chain"], 2, ALL_PARTS
                                         ).then_inc(s["res"], 1)

                walk(dve, PER, 2, LEAD, LAG, step)


def rope_attention(nc, d, k, phase):
    PER, H, DH, PARTS = 8, 16, 8, 3
    ROWS = DH * sum(PARTS - a for a in range(PARTS))
    n = k.norms
    w = weights(k, phase)
    for name in list(w):
        w[name[:-1]] = w[name]
    C = 3 * P
    with ExitStack() as ctx:
        def sb(name, shape):
            return ctx.enter_context(nc.sbuf_tensor(f"a{phase}_{name}", shape, F32))

        terms = sb("terms", [P, 2, 2, T])
        rotated = sb("rotated", [P, 2, T])
        rest = sb("rest", [P, 2, T])
        cut = ctx.enter_context(nc.sbuf_tensor(f"a{phase}_cut", [P, PARTS, 2, T], BF16))
        stack = ctx.enter_context(nc.sbuf_tensor(f"a{phase}_stack", [ROWS, 2, 2, H, T], BF16))
        v = sb("v", [P, 2, NT, H, 32])
        p = sb("p", [P, 2, 2, C])
        pT = sb("pT", [P, 2, 2, C])
        o = sb("o", [P, T])
        oT = sb("oT", [P, T])
        nmax = sb("nmax", [P, 2, 2, NT])
        sums = sb("sums", [P, 2, NT, H])
        rec = sb("rec", [P, NT, H])
        recT = sb("recT", [H, T])
        scale = sb("scale", [P, T])
        cut_dram = nc.dram_tensor(f"cut_dram{phase}", (2, PARTS, 2, DH * H, T), BF16, kind="Internal").ap()
        misc_ps, o_ps = k.banks[0:2]
        s_ps, pT_ps = (k.banks[2:4], k.banks[4:6]), k.banks[6:8]
        names = ("chain", "var", "std", "rstd", "xn", "ht_mm", "ht", "q_mm", "q_terms", "k_mm", "k_terms", "cut",
                 "written_q", "written_k", "stacked0", "stacked1", "v_mm", "v", "s_mm", "nmax", "exp", "pT_mm", "pT0", "pT1", "o_mm", "o",
                 "rec", "recT_mm", "recT", "scale_mm", "scale", "oT", "y_mm", "res", "v0")
        s = signals(nc, ctx, f"a{phase}_", names)
        stacked, written = [s["stacked0"], s["stacked1"]], [s["written_q"], s["written_k"]]
        LEAD, LAG = 2 * PER - 3, 5

        def place(at):
            return at.s // PER % 2

        def diagonal(at, t):
            whole = v[:, place(at), t]
            return bass.AP(whole.tensor, whole.offset, [list(whole.ap[0]), [4 * 32, 4], [32 + DH, 4], [1, DH]])

        with nc.Block() as block:

            @block.sync
            def _(sp):
                prefetch(sp, nc, k, d, phase)
                ROW = H * DH * T

                def step(at):
                    ni = at.shift(PER)
                    for which in range(2):
                        if at.p == 1 + 2 * which and ni.real:
                            wait(sp, s["cut"], ni, 10, 5 - 5 * which, item=True)
                            sp.dma_start(cut_dram[place(ni), :, which].rearrange("a r t -> r a t"), cut[:, :, which]
                                         ).then_inc(written[which], 16)
                        if at.p == 2 + 2 * which and ni.real:
                            wait(sp, written[which], ni, 16, item=True)
                            row = 0
                            for a in range(PARTS):
                                rows = (PARTS - a) * DH
                                start = (place(ni) * PARTS * 2 + (1 if which else 2 * a)) * ROW
                                src = bass.AP(cut_dram.tensor, start,
                                              [[2 * ROW if which else 0, PARTS - a], [H * T, DH], [1, H * T]])
                                sp.dma_start(stack[row:row + rows, place(ni), which].rearrange("r h t -> r (h t)"), src
                                             ).then_inc(stacked[place(ni)], 16)
                                row += rows

                walk(sp, PER, 2, LEAD, LAG, step)

            @block.gpsimd
            def _(pool):
                def cut_up(which, at, terms_ready):
                    def link(i, m):
                        i.then_inc(s["cut"], 1)
                        if m < 5:
                            pool.wait_ge(s["cut"], at.item * 10 + 5 * which + m)

                    wait(pool, terms_ready, at, item=True)
                    wait(pool, written[which], at.shift(-PER), 16, item=True)
                    x, y, c = terms[:, which, 0, :], terms[:, which, 1, :], cut[:, :, which, :]
                    link(pool.tensor_tensor(c[:, 0], x, y, ALU.add), 1)
                    link(pool.tensor_tensor(rotated[:, which], x, y, ALU.add), 2)
                    link(pool.tensor_tensor(rest[:, which], rotated[:, which], c[:, 0], ALU.subtract), 3)
                    link(pool.tensor_tensor(c[:, 1], rotated[:, which], c[:, 0], ALU.subtract), 4)
                    link(pool.tensor_tensor(c[:, 2], rest[:, which], c[:, 1], ALU.subtract), 5)

                def step(at):
                    ni, pi, ni2 = at.shift(PER), at.shift(-PER), at.shift(2 * PER)
                    if at.p == 7 and ni2.real:
                        cut_up(0, ni2, s["q_terms"])
                    if at.p == 0 and ni.real:
                        cut_up(1, ni, s["k_terms"])
                    if at.p == 2 and pi.real:
                        wait(pool, s["o"], pi, item=True)
                        wait(pool, s["scale"], pi, item=True)
                        wait(pool, s["y_mm"], pi.shift(-PER), item=True)
                        pool.tensor_tensor(oT[:], o[:], scale[:], ALU.mult).then_inc(s["oT"], 1)

                walk(pool, PER, 2, LEAD, LAG, step)

            @block.scalar
            def _(act):
                std_of_rows(act, n, s["var"], s["std"])
                act.wait_ge(s["v0"], 1)

                def step(at):
                    b1, ni, ni2, pi = at.shift(-1), at.shift(PER), at.shift(2 * PER), at.shift(-PER)
                    def exps(h):
                        r, head = at.ring(2), at.p + 8 * h
                        wait(act, s["nmax"], at, 2, 1 - h)
                        for t in range(NT):
                            c = slice(0, P) if t == 0 else slice(P, C)
                            i = act.activation(p[:, r, h, c], s_ps[at.ring(2)][h][:, c], ACT.Exp,
                                               bias=nmax[:, r, h, t:t + 1],
                                               accum_out=sums[:, place(at), t, head:head + 1])
                        i.then_inc(s["exp"], 1)

                    if at.real:
                        if at.p == 0:
                            wait(act, s["rec"], at.shift(-2 * PER), item=True)
                        wait(act, s["pT_mm"], at.shift(-2), 2)
                        exps(0)
                    if b1.real:
                        wait(act, s["pT_mm"], b1, 2)
                        wait(act, s["o_mm"], b1.shift(-2))
                        act.copy(pT[:, b1.ring(2), 1, :], pT_ps[1][:, 0:C]).then_inc(s["pT1"], 1)
                    if at.p == 1 and pi.real:
                        wait(act, s["recT_mm"], pi, item=True)
                        wait(act, s["scale_mm"], pi.shift(-PER), item=True)
                        act.copy(recT[:], misc_ps[0:H, 0:T]).then_inc(s["recT"], 1)
                    if at.p == 2 and pi.real:
                        wait(act, s["scale_mm"], pi, item=True)
                        wait(act, s["oT"], pi.shift(-PER), item=True)
                        act.copy(scale[:], misc_ps[:, T:2 * T]).then_inc(s["scale"], 1)
                    if at.p == 5 and ni.real:
                        wait(act, s["v_mm"], ni, item=True)
                        for t in range(NT):
                            i = act.copy(diagonal(ni, t),
                                         misc_ps[:, t * P:(t + 1) * P].rearrange("p (g r c) -> p g r c", g=4, r=4))
                        i.then_inc(s["v"], 1)
                    if at.p == 6 and ni2.real:
                        wait(act, s["ht_mm"], ni2, item=True)
                        wait(act, s["v_mm"], ni, item=True)
                        modulated(act, k, phase, ni2, misc_ps[:, T:2 * T], n.hT[:, 0, :], s["ht"])
                    if at.real:
                        exps(1)

                walk(act, PER, 2, LEAD, LAG, step)

            @block.tensor
            def _(pe):
                pe.wait_ge(k.weights_in[phase], 16 * len(WEIGHTS[phase]))

                def projections(at, which, sem):
                    for c in range(2):
                        mm = pe.matmul(misc_ps[:, c * T:(c + 1) * T], w["wqk"][:, 2 * which + c, :], n.hT[:, 0, :],
                                       start=True, stop=True)
                    mm.then_inc(sem, 1)

                def step(at):
                    b1, b2, ni, pi = at.shift(-1), at.shift(-2), at.shift(PER), at.shift(-PER)
                    ni2, n1 = at.shift(2 * PER), at.shift(1)
                    if n1.real and n1.p == 0:
                        i = n1.s // PER
                        pe.wait_ge(stacked[i % 2], at.base * (2 * PARTS * 16 // 2) + (i // 2 + 1) * (2 * PARTS * 16))
                    for h in range(2):
                        if b1.real:
                            wait(pe, s[("pT0", "pT1")[h]], b1.shift(-1))
                            wait(pe, s["exp"], b1, 2, 1 - h)
                            causal_transposes(pe, pT_ps[h], p[:, b1.ring(2), h, :], k.ident[:]).then_inc(s["pT_mm"], 1)
                        if n1.real:
                            q, keys = (stack[:, place(n1), which, n1.p + 8 * h, :] for which in range(2))
                            bank = s_ps[n1.ring(2)][h]
                            wait(pe, s["exp"], n1.shift(-2), 2, 1 - h)
                            pe.matmul(bank[:, 0:P], q[:, 0:P], keys[:, 0:P], start=True, stop=False,
                                      skip_group_check=True)
                            pe.matmul(bank[:, P:C], q[:, P:T], keys, start=False, stop=False,
                                      skip_group_check=True)
                            for c in (0, 2 * P):
                                mm = pe.matmul(bank[:, c:c + P], k.ident_bf[:], k.causal_bf[:], start=False,
                                               stop=True, skip_group_check=True)
                            mm.then_inc(s["s_mm"], 1)
                    if b2.real:
                        wait(pe, s["pT0"], b2)
                        wait(pe, s["pT1"], b2)
                        if b2.p == 0:
                            wait(pe, s["v"], b2, item=True)
                            wait(pe, s["o"], b2.shift(-PER), item=True)
                        for j in range(NT):
                            for h in range(2):
                                head = b2.p + 8 * h
                                g = head // 4 * 32
                                mm = pe.matmul(o_ps[g:g + 32, j * P:T], v[:, place(b2), j, head, :],
                                               pT[:, b2.ring(2), h, 0:T] if j == 0 else pT[:, b2.ring(2), h, T:C],
                                               start=(j == 0 and head % 4 == 0), stop=(j == 1 and head % 4 == 3),
                                               skip_group_check=True)
                        mm.then_inc(s["o_mm"], 1)
                    if at.p == 0 and pi.real:
                        wait(pe, s["rec"], pi, item=True)
                        wait(pe, s["k_terms"], ni, item=True)
                        wait(pe, s["v"], at, item=True)
                        wait(pe, s["res"], pi.shift(-PER), item=True)
                        for t in range(NT):
                            mm = pe.transpose(misc_ps[0:H, t * P:(t + 1) * P], rec[:, t, :], k.ident[:])
                        mm.then_inc(s["recT_mm"], 1)
                    if at.p == 1 and pi.real:
                        wait(pe, s["recT"], pi, item=True)
                        pe.matmul(misc_ps[:, T:2 * T], w["head_rows"][:], recT[:], start=True, stop=True
                                  ).then_inc(s["scale_mm"], 1)
                    if at.p == 3 and pi.real:
                        wait(pe, s["oT"], pi, item=True)
                        wait(pe, s["scale"], pi, item=True)
                        for t in range(NT):
                            mm = pe.matmul(misc_ps[:, t * P:(t + 1) * P], oT[:, t * P:(t + 1) * P], w["wproj"][:],
                                           start=True, stop=True)
                        mm.then_inc(s["y_mm"], 1)
                    if at.p == 4 and ni.real:
                        wait(pe, s["k_terms"], ni, item=True)
                        if pi.real:
                            pe.wait_ge(s["chain"], pi.item * 2 + 3)
                        for t in range(NT):
                            mm = pe.matmul(misc_ps[:, t * P:(t + 1) * P], n.hT[:, 0, t * P:(t + 1) * P], w["wv"][:],
                                           start=True, stop=True)
                        mm.then_inc(s["v_mm"], 1)
                    if at.p == 5 and ni2.real:
                        wait(pe, s["xn"], ni2, item=True)
                        wait(pe, s["v"], ni, item=True)
                        for t in range(NT):
                            mm = pe.transpose(misc_ps[:, T + t * P:T + (t + 1) * P], n.xn[:, t, :], k.ident[:])
                        mm.then_inc(s["ht_mm"], 1)
                    if at.p == 6 and ni2.real:
                        wait(pe, s["ht"], ni2, item=True)
                        projections(ni2, 0, s["q_mm"])
                    if at.p == 7 and ni2.real:
                        wait(pe, s["q_terms"], ni2, item=True)
                        projections(ni2, 1, s["k_mm"])

                walk(pe, PER, 2, LEAD, LAG, step)

            @block.vector
            def _(dve):
                start_norms(dve, n, s)
                dve.memset(v[:], 0.0).then_inc(s["v0"], 1)
                dve.wait_ge(k.weights_in[phase], 16 * len(WEIGHTS[phase]))
                dve.wait_ge(k.gate_in[phase], 16)

                def rotation_terms(which, at, mm, table, done):
                    wait(dve, mm, at, item=True)
                    wait(dve, s["cut"], at.shift(-PER), 10, 5 - 5 * which, item=True)
                    dve.tensor_tensor(terms[:, which], misc_ps[:].rearrange("p (c t) -> p c t", c=2), table, ALU.mult
                                      ).then_inc(done, 1)

                def step(at):
                    b1, ni, pi, ni2 = at.shift(-1), at.shift(PER), at.shift(-PER), at.shift(2 * PER)
                    if at.real:
                        for h in range(2):
                            wait(dve, s["s_mm"], at, 2, 1 - h)
                            wait(dve, s["exp"], at.shift(-2), 2)
                            for t in range(NT):
                                i = dve.tensor_reduce(nmax[:, at.ring(2), h, t:t + 1],
                                                      s_ps[at.ring(2)][h][:, 0:P] if t == 0 else s_ps[at.ring(2)][h][:, P:C], AX_X, ALU.max,
                                                      negate=True)
                            i.then_inc(s["nmax"], 1)
                    if at.p == 0 and pi.real:
                        wait(dve, s["exp"], at.shift(-1), 2)
                        wait(dve, s["recT_mm"], pi.shift(-PER), item=True)
                        dve.reciprocal(rec[:], sums[:, (at.s // PER + 1) % 2]).then_inc(s["rec"], 1)
                    if at.p == 2 and pi.real:
                        wait(dve, s["o_mm"], at.shift(-3))
                        wait(dve, s["oT"], pi.shift(-PER), item=True)
                        dve.tensor_copy(o[:], o_ps[:, 0:T]).then_inc(s["o"], 1)
                    if at.p == 4 and pi.real:
                        wait(dve, s["y_mm"], pi, item=True)
                        add_residual(dve, n, pi, misc_ps[:, 0:T].rearrange("p (t d) -> p t d", t=NT), k.gate[phase % 2],
                                     None, s["chain"], 2, ALL_PARTS).then_inc(s["res"], 1)
                    if at.p == 3 and ni2.real:
                        normalise(dve, n, ni2, s["ht_mm"], s["xn"])
                    if at.p == 7 and ni2.real:
                        rotation_terms(0, ni2, s["q_mm"], w["rope_q"], s["q_terms"])
                    if at.p == 0 and ni.real:
                        rotation_terms(1, ni, s["k_mm"], w["rope_k"], s["k_terms"])
                    if b1.real:
                        wait(dve, s["pT_mm"], b1, 2, 1)
                        wait(dve, s["o_mm"], b1.shift(-2))
                        dve.tensor_copy(pT[:, b1.ring(2), 0, :], pT_ps[0][:, 0:C]).then_inc(s["pT0"], 1)

                walk(dve, PER, 2, LEAD, LAG, step)


def attention2(nc, d, k):
    rope_attention(nc, d, k, 4)


def attention3(nc, d, k):
    rope_attention(nc, d, k, 6)


CAT = 2 * 512 + 4 + P


def ffn2(nc, d, k):
    phase, PER, E = 5, 4, 8
    n = k.norms
    w = weights(k, phase)
    with ExitStack() as ctx:
        def sb(name, shape):
            return ctx.enter_context(nc.sbuf_tensor("f2_" + name, shape, F32))

        merged = sb("merged", [P, 2, CAT])
        hT = sb("hT", [P, 4, T])
        uT = sb("uT", [P, 2, T])
        gate_hidden = sb("gate_hidden", [P, T])
        hidden_sum = sb("hidden_sum", [P, 1])
        sum_cols = sb("sum_cols", [P, P])
        g = sb("g", [P, 2, E])
        ht_ps, gh_ps, g_ps, u_ps, y_ps = k.banks[0], k.banks[1], k.banks[2], k.banks[3:5], k.banks[5]
        names = ("chain", "var", "std", "rstd", "xn", "ht_mm", "ht", "gh_mm", "sum", "cols", "g_mm", "g", "merge",
                 "u_mm", "u", "y_mm", "res")
        s = signals(nc, ctx, "f2_", names)
        LEAD, LAG = 8, 1

        with nc.Block() as block:

            @block.sync
            def _(sp):
                prefetch(sp, nc, k, d, phase)

            @block.scalar
            def _(act):
                std_of_rows(act, n, s["var"], s["std"])
                act.wait_ge(k.weights_in[phase], 16 * len(WEIGHTS[phase]))

                def step(at):
                    i2 = at.shift(2 * PER)
                    if at.real:
                        wait(act, s["u_mm"], at)
                        wait(act, s["y_mm"], at.shift(-2))
                        c = 2 * 512 + at.p
                        act.activation(uT[:, at.ring(2), :], u_ps[at.ring(2)][:, 0:T], ACT.Gelu_apprx_tanh,
                                       bias=merged[:, at.s // PER % 2, c:c + 1]).then_inc(s["u"], 1)
                    if at.p == 1 and i2.real:
                        wait(act, s["ht_mm"], i2, item=True)
                        wait(act, s["u_mm"], at.shift(-6))
                        modulated(act, k, phase, i2, ht_ps[:, 0:T], hT[:, i2.s // PER % 4, :], s["ht"])
                    if at.p == 2 and i2.real:
                        wait(act, s["gh_mm"], i2, item=True)
                        act.activation(gate_hidden[:], gh_ps[:, 0:T], ACT.Relu, bias=w["gb1"][:, 0:1],
                                       accum_out=hidden_sum[:]).then_inc(s["sum"], 1)
                        wait(act, s["sum"], i2, item=True)
                        wait(act, s["g_mm"], i2.shift(-PER), item=True)
                        act.activation(sum_cols[:], k.ident[:], ACT.Identity, scale=0.0, bias=hidden_sum[:, 0:1]
                                       ).then_inc(s["cols"], 1)

                walk(act, PER, 4, LEAD, LAG, step)

            @block.tensor
            def _(pe):
                pe.wait_ge(k.weights_in[phase], 16 * len(WEIGHTS[phase]))

                def step(at):
                    b1, i2 = at.shift(-1), at.shift(2 * PER)
                    if b1.real:
                        wait(pe, s["u"], b1)
                        if b1.p == 0:
                            wait(pe, s["res"], b1.shift(-PER), item=True)
                        for t in range(NT):
                            mm = pe.matmul(y_ps[:, t * P:(t + 1) * P], uT[:, b1.ring(2), t * P:(t + 1) * P],
                                           merged[:, b1.s // PER % 2, 512 + b1.p * P:512 + (b1.p + 1) * P],
                                           start=(b1.p == 0 and t == 0), stop=(b1.p == PER - 1),
                                           skip_group_check=True)
                        mm.then_inc(s["y_mm"], 1)
                    if at.p == 1 and i2.real:
                        wait(pe, s["xn"], i2, item=True)
                        wait(pe, s["ht"], i2.shift(-PER), item=True)
                        for t in range(NT):
                            mm = pe.transpose(ht_ps[:, t * P:(t + 1) * P], n.xn[:, t, :], k.ident[:])
                        mm.then_inc(s["ht_mm"], 1)
                    if at.p == 2 and i2.real:
                        wait(pe, s["ht"], i2, item=True)
                        wait(pe, s["sum"], i2.shift(-PER), item=True)
                        pe.matmul(gh_ps[:, 0:T], w["gw1_2"][:], hT[:, i2.s // PER % 4, :], start=True, stop=True
                                  ).then_inc(s["gh_mm"], 1)
                    if at.p == 3 and i2.real:
                        wait(pe, s["cols"], i2, item=True)
                        wait(pe, s["g"], i2.shift(-PER), item=True)
                        pe.matmul(g_ps[:, 0:E], sum_cols[:], w["gw2"][:], start=True, stop=True).then_inc(s["g_mm"], 1)
                    if at.real:
                        wait(pe, s["merge"], at, E, item=True)
                        wait(pe, s["u"], at.shift(-2))
                        pe.matmul(u_ps[at.ring(2)][:, 0:T], merged[:, at.s // PER % 2, at.p * P:(at.p + 1) * P],
                                  hT[:, at.s // PER % 4, :], start=True, stop=True).then_inc(s["u_mm"], 1)

                walk(pe, PER, 4, LEAD, LAG, step)

            @block.vector
            def _(dve):
                start_norms(dve, n, s)
                dve.wait_ge(k.weights_in[phase], 16 * len(WEIGHTS[phase]))
                dve.wait_ge(k.gate_in[phase], 16)

                def step(at):
                    ni, i2 = at.shift(PER), at.shift(2 * PER)
                    if at.p == 0 and i2.real:
                        normalise(dve, n, i2, s["ht_mm"], s["xn"])
                    if ni.real:
                        if ni.p == 0:
                            wait(dve, s["g"], Step(ni.base, ni.s, PER), item=True)
                            wait(dve, s["y_mm"], at.shift(-PER + 3))
                        m = merged[:, ni.s // PER % 2, :]
                        for e in (2 * ni.p, 2 * ni.p + 1):
                            if e:
                                dve.wait_ge(s["merge"], ni.item * E + e)
                            dve.scalar_tensor_tensor(out=m, in0=w["task"][:, e, :], scalar=g[:, ni.s // PER % 2, e:e + 1],
                                                     in1=m if e else w["base"][:], op0=ALU.mult, op1=ALU.add
                                                     ).then_inc(s["merge"], 1)
                    if at.p == 3 and i2.real:
                        wait(dve, s["g_mm"], i2, item=True)
                        wait(dve, s["merge"], i2.shift(-2 * PER), E, item=True)
                        dve.scalar_tensor_tensor(out=g[:, i2.s // PER % 2, :], in0=g_ps[:, 0:E], scalar=1.0 / T,
                                                 in1=w["gb2"][:], op0=ALU.mult, op1=ALU.add).then_inc(s["g"], 1)
                    if at.p == 3 and at.real:
                        wait(dve, s["y_mm"], at)
                        add_residual(dve, n, at, y_ps[:, 0:T].rearrange("p (t d) -> p t d", t=NT), k.gate[phase % 2],
                                     merged[:, at.s // PER % 2, CAT - P:CAT].unsqueeze(1).to_broadcast([P, NT, P]),
                                     s["chain"], 3, ALL_PARTS).then_inc(s["res"], 1)

                walk(dve, PER, 4, LEAD, LAG, step)


def ffn3(nc, d, k):
    phase, PER, E, K = 7, 5, 8, 6
    n = k.norms
    w = weights(k, phase)
    with ExitStack() as ctx:
        def sb(name, shape):
            return ctx.enter_context(nc.sbuf_tensor("f3_" + name, shape, F32))

        tanh = sb("tanh", [P, 2, T])
        gated = sb("gated", [P, 2, T])
        hidden = sb("hidden", [P, 2, T])
        acc = sb("acc", [P, NT, P])
        b = router_tiles(nc, ctx, "f3_", E)
        gu_ps, y_ps = k.banks[0:2], k.banks[2:4]
        ht_ps, rt_ps = k.banks[4], k.banks[5]
        names = ("chain", "var", "std", "rstd", "xn", "ht_mm", "ht", "rt_mm", "nmax", "rexp", "top", "cw", "cwT_mm",
                 "gu_mm", "tanh", "gated", "hidden", "y_mm", "acc", "res", "pads")
        s = signals(nc, ctx, "f3_", names)
        LAST, LEAD, LAG = PER - 1, 5, 2

        with nc.Block() as block:

            @block.scalar
            def _(act):
                std_of_rows(act, n, s["var"], s["std"])

                def step(at):
                    nx, ni = at.shift(1), at.shift(PER)
                    if nx.real:
                        wait(act, s["gu_mm"], nx)
                        wait(act, s["gated"], nx.shift(-2))
                        act.activation(tanh[:, nx.ring(2), :], gu_ps[nx.ring(2)][:, 0:T], ACT.Tanh, scale=0.5
                                       ).then_inc(s["tanh"], 1)
                    if at.p == 1 and ni.real:
                        wait(act, s["ht_mm"], ni, item=True)
                        wait(act, s["gu_mm"], at.shift(-2))
                        modulated(act, k, phase, ni, ht_ps[:, 0:T], n.hT[:, (at.s // PER + 1) % 2, :], s["ht"])
                    if at.p == 2 and ni.real:
                        wait(act, s["nmax"], ni, item=True)
                        wait(act, s["top"], ni.shift(-PER), 5, item=True)
                        for t in range(NT):
                            i = act.activation(b["e"][:, t, :], rt_ps[:, t * E:(t + 1) * E], ACT.Exp,
                                               bias=b["nmax"][:, t:t + 1], accum_out=b["sums"][:, t:t + 1])
                        i.then_inc(s["rexp"], 1)

                walk(act, PER, 2, LEAD, LAG, step)

            @block.tensor
            def _(pe):
                pe.wait_ge(k.weights_in[phase], 16 * len(WEIGHTS[phase]))

                def step(at):
                    nx, ni = at.shift(1), at.shift(PER)
                    if nx.real:
                        if nx.p == 0:
                            wait(pe, s["ht"], nx, item=True)
                        wait(pe, s["hidden"], nx.shift(-2))
                        for c in range(2):
                            mm = pe.matmul(gu_ps[nx.ring(2)][:, c * T:(c + 1) * T], w["gu"][:, nx.p, c, :],
                                           n.hT[:, nx.s // PER % 2, :], start=True, stop=True)
                        mm.then_inc(s["gu_mm"], 1)
                    if at.p == 1 and ni.real:
                        wait(pe, s["xn"], ni, item=True)
                        wait(pe, s["ht"], ni.shift(-PER), item=True)
                        for t in range(NT):
                            mm = pe.transpose(ht_ps[:, t * P:(t + 1) * P], n.xn[:, t, :], k.ident[:])
                        mm.then_inc(s["ht_mm"], 1)
                    if at.p == 2 and ni.real:
                        wait(pe, s["ht"], ni, item=True)
                        wait(pe, s["rexp"], ni.shift(-PER), item=True)
                        for t in range(NT):
                            mm = pe.matmul(rt_ps[:, t * E:(t + 1) * E],
                                           n.hT[:, (at.s // PER + 1) % 2, t * P:(t + 1) * P], w["rw3"][:],
                                           start=True, stop=True)
                        mm.then_inc(s["rt_mm"], 1)
                    if at.real:
                        wait(pe, s["hidden"], at)
                        wait(pe, s["acc"], at.shift(-2))
                        width = P if at.p == LAST else 2 * P
                        for t in range(NT):
                            mm = pe.matmul(y_ps[at.ring(2)][:, t * width:(t + 1) * width],
                                           hidden[:, at.ring(2), t * P:(t + 1) * P],
                                           w["shared"][:] if at.p == LAST else w["down"][:, at.p, :],
                                           start=True, stop=True)
                        mm.then_inc(s["y_mm"], 1)

                walk(pe, PER, 2, LEAD, LAG, step)

            @block.vector
            def _(dve):
                start_norms(dve, n, s)
                dve.memset(b["probs"][:], -1.0)
                dve.memset(b["top"][:], -1.0).then_inc(s["pads"], 1)
                dve.wait_ge(s["pads"], 1)
                dve.wait_ge(k.gate_in[phase], 16)

                def step(at):
                    nx, ni = at.shift(1), at.shift(PER)
                    if at.p == 0 and ni.real:
                        normalise(dve, n, ni, s["ht_mm"], s["xn"])
                    if nx.real:
                        r = nx.ring(2)
                        wait(dve, s["tanh"], nx)
                        dve.scalar_tensor_tensor(out=gated[:, r, :], in0=tanh[:, r, :], scalar=1.0,
                                                 in1=gu_ps[r][:, 0:T], op0=ALU.add, op1=ALU.mult
                                                 ).then_inc(s["gated"], 1)
                        wait(dve, s["gated"], nx)
                        wait(dve, s["y_mm"], nx.shift(-2))
                        dve.scalar_tensor_tensor(out=hidden[:, r, :], in0=gated[:, r, :], scalar=0.5,
                                                 in1=gu_ps[r][:, T:2 * T], op0=ALU.mult, op1=ALU.mult
                                                 ).then_inc(s["hidden"], 1)
                    if at.p == 2 and ni.real:
                        wait(dve, s["rt_mm"], ni, item=True)
                        dve.tensor_reduce(b["nmax"][:], rt_ps[:, 0:NT * E].rearrange("p (t e) -> p t e", t=NT), AX_X,
                                          ALU.max, negate=True).then_inc(s["nmax"], 1)
                    if at.real:
                        wait(dve, s["y_mm"], at)
                        wait(dve, s["acc"], at.shift(-1), 2)
                        y, c = y_ps[at.ring(2)], b["cw"][:, at.s // PER % 2]
                        if at.p == 0:
                            wait(dve, s["cw"], at, item=True)
                            wait(dve, s["res"], at.shift(-PER), item=True)
                        if at.p == LAST:
                            dve.tensor_tensor(acc[:], acc[:], y[:, 0:T].rearrange("p (t d) -> p t d", t=NT),
                                              ALU.add).then_inc(s["acc"], 2)
                            wait(dve, s["acc"], at, 2)
                            add_residual(dve, n, at, acc[:], k.gate[phase % 2], None, s["chain"], 2, ALL_PARTS
                                         ).then_inc(s["res"], 1)
                        else:
                            for j in range(2):
                                if j:
                                    wait(dve, s["acc"], at, 2, 1)
                                for t in range(NT):
                                    a, z = acc[:, t, :], y[:, t * 2 * P + j * P:t * 2 * P + (j + 1) * P]
                                    e = 2 * at.p + j
                                    if e == 0:
                                        i = dve.tensor_scalar(a, z, c[:, t, 0:1], None, ALU.mult)
                                    else:
                                        i = dve.scalar_tensor_tensor(out=a, in0=z, scalar=c[:, t, e:e + 1], in1=a,
                                                                     op0=ALU.mult, op1=ALU.add)
                                i.then_inc(s["acc"], 1)
                    if at.p == 3 and ni.real:
                        softmax_top(dve, s, k.spare, ni, E, K, (at.s // PER + 1) % 2, b, acc_each=2, transposed=False)

                walk(dve, PER, 2, LEAD, LAG, step)


PHASES = [attention0, ffn0, attention1, ffn1, attention2, ffn2, attention3, ffn3]


def position_table(length, features):
    dist = np.arange(-length + 1, length, dtype=np.float64)
    n, a = features // 6, np.abs(dist)[:, None]
    decay = np.exp(-math.log(2.0) / 2.0 ** np.linspace(3.0, math.log2(length), n)[None] * a)
    central = (2.0 ** np.arange(1, n + 1)[None] - 1.0 > a).astype(np.float64)
    stddev = length / (2.0 * n)
    mean = np.linspace(length / n, float(length), n)[None]
    conc, rate = (mean / stddev) ** 2, mean / stddev ** 2
    log_a = np.log(np.maximum(a, 1e-300))
    log_norm = np.array([[math.lgamma(c) for c in conc[0]]]) - conc * np.log(rate)
    gamma = np.exp((conc - 1.0) * log_a - rate * a - log_norm) + 1e-8
    gamma = gamma / gamma.max(axis=-1, keepdims=True)
    emb = np.concatenate([decay, central, gamma], axis=-1)
    return np.concatenate([emb, np.sign(dist)[:, None] * emb], axis=-1).astype(np.float32)


def laid_out(i):
    f = {x: np.asarray(v) for x, v in i.items()}
    o = {}
    o["x"] = f["L0_attn_x"]
    o["cT"] = np.concatenate([f[f"L{n}_c"].T for n in range(4)], axis=1)
    o["wmod"] = np.stack([f[f"L{n}_wmod"] for n in range(4)], axis=1)
    o["ident"] = np.eye(P, dtype=np.float32)
    q = np.arange(P)
    o["causal"] = np.where(q[None, :] > q[:, None], MASKED, 0.0).astype(np.float32)

    def rows(a, k):
        return a.reshape(k, -1, a.shape[-1]).transpose(1, 0, 2)

    def bcast(a):
        return np.broadcast_to(a, (P, *a.shape))

    o["wqT0"], o["wkT0"] = (x.reshape(P, 16, 64).transpose(2, 1, 0) for x in (f["L0_attn_Wq"], f["L0_attn_Wkv"][:, :1024]))
    o["wv0"] = f["L0_attn_Wkv"][:, 1024:]
    o["wo0"] = rows(f["L0_attn_Wo"], 8)
    o["bo0"] = bcast(f["L0_attn_bo"])
    o["e1w"] = np.concatenate([f["L0_ffn_eW1"], f["L0_ffn_sW1"][None]]).transpose(1, 0, 2)
    o["e2w"] = np.concatenate([f["L0_ffn_eW2"], f["L0_ffn_sW2"][None]]).transpose(1, 0, 2)
    o["e1b"] = np.concatenate([f["L0_ffn_eb1"], f["L0_ffn_sb1"][None]]).T
    o["e2b"] = np.concatenate([f["L0_ffn_eb2"], f["L0_ffn_sb2"][None]])
    o["rw"] = f["L0_ffn_router_W"]
    o["rb"] = bcast(f["L0_ffn_router_b"])
    o["wqT"], o["wkT"] = (f[f"L1_attn_{x}"].reshape(P, 8, P).transpose(2, 1, 0) for x in ("w_qs", "w_ks"))
    o["wv1"] = f["L1_attn_w_vs"]
    o["wo1"] = rows(f["L1_attn_w_out"], 8)
    o["bo1"] = bcast(f["L1_attn_b_out"])
    o["qb1"] = np.stack([f["L1_attn_rel_embed_bias"][0, :, 0].T, f["L1_attn_rel_pos_bias"][0, :, 0].T], axis=1)
    o["w_relT"] = f["L1_attn_w_rel_pos_k"].reshape(2, 96, 8, P).transpose(3, 2, 0, 1)
    table = position_table(T, f["L1_attn_w_rel_pos_k"].shape[0])
    o["positions"] = rows(np.pad(table.T, ((0, 0), (0, 1))), 2)
    o["w12"] = f["L1_ffn_w12"].transpose(2, 0, 1)
    o["w3"] = f["L1_ffn_w3"].reshape(8, P, 2, P).transpose(3, 0, 2, 1)
    o["gw1"] = f["L1_ffn_gate_w"].T
    qkv = f["L2_attn_Wqkv"]
    swapped = np.arange(P) ^ 1
    angle = np.arange(T)[None, :] * (10000.0 ** (-(np.arange(P) % 8 // 2) / 4.0))[:, None]
    sign = np.where(np.arange(P) % 2 == 0, -1.0, 1.0)[:, None]
    by_feature = np.arange(P).reshape(16, 8).T.ravel()
    rope = np.stack([np.cos(angle), np.sin(angle) * sign], axis=1)[by_feature]
    for x, (wq, wk, wv), wo in ((2, [qkv[:, i * P:(i + 1) * P] for i in range(3)], f["L2_attn_Wproj"]),
                                (3, [f[f"L3_attn_W_{c}"].T for c in "qkv"], f["L3_attn_W_o"].T)):
        o[f"wqk{x}"] = np.stack([c[:, by_feature] for c in (wq, wq[:, swapped], wk, wk[:, swapped])], axis=1)
        o[f"wv{x}"], o[f"wproj{x}"] = wv, wo
        o[f"rope_q{x}"] = (rope / math.sqrt(8.0)).astype(np.float32)
        o[f"rope_k{x}"] = rope.astype(np.float32)
        o[f"head_rows{x}"] = (np.arange(16)[:, None] == np.arange(P)[None, :] // 8).astype(np.float32)

    def joined(w1, w2, b1, b2):
        return np.concatenate([w1.T, w2.T.reshape(4, P, P).transpose(1, 0, 2).reshape(P, -1), b1.reshape(4, P).T,
                               bcast(b2)], axis=1)

    o["base"] = joined(*(f[f"L2_ffn_{x}"] for x in ("W1", "W2", "b1", "b2")))
    o["task"] = np.stack([joined(*(f[f"L2_ffn_T{x}"][e] for x in ("W1", "W2", "b1", "b2"))) for e in range(8)], axis=1)
    o["gw1_2"], o["gb1"] = f["L2_ffn_gate_w1"].T, f["L2_ffn_gate_b1"][:, None]
    o["gw2"], o["gb2"] = f["L2_ffn_gate_w2"].T, bcast(f["L2_ffn_gate_b2"])
    pairs = [np.concatenate([f[f"L3_ffn_w_{x}"][e::2] for e in range(2)], axis=2) for x in ("gate", "up")]
    gu = np.stack([np.concatenate([pair, f[f"L3_ffn_ws_{x}"][None]]) for pair, x in zip(pairs, ("gate", "up"))], axis=1)
    o["gu"] = gu.transpose(2, 0, 1, 3)
    down = np.zeros((P, 4, 2, P), np.float32)
    down[0:64, :, 0], down[64:, :, 1] = (f["L3_ffn_w_down"][e::2].transpose(1, 0, 2) for e in range(2))
    o["down"], o["shared"], o["rw3"] = down, f["L3_ffn_ws_down"], f["L3_ffn_router_w"]
    for name, shape, parts in (w for ph in WEIGHTS for w in ph):
        o[name] = o[name].reshape(parts, -1)
    return o


def kernel(**inputs):
    import numpy as _np
    import concourse.bacc as _bacc
    from concourse import mybir as _mybir
    from concourse.bass_utils import run_bass_kernel_spmd as _run

    nc = _bacc.Bacc("TRN2", target_bir_lowering=False, num_devices=1)
    arrays, d = {}, {}
    for name, a in laid_out(inputs).items():
        a = _np.ascontiguousarray(a)
        arrays[f"in_{name}"] = a
        d[name] = nc.dram_tensor(f"in_{name}", a.shape, _mybir.dt.from_np(a.dtype), kind="ExternalInput").ap()
    out = nc.dram_tensor("out_0", (NB, T, P), _mybir.dt.float32, kind="ExternalOutput").ap()
    build(nc, d, out, PHASES)
    r = _run(nc, [arrays], core_ids=[0])
    return r.results[0]["out_0"]
```

```python
import math
from contextlib import ExitStack

import numpy as np

import concourse.bass as bass
from concourse import mybir

F32 = mybir.dt.float32
BF16 = mybir.dt.bfloat16
F32R = mybir.dt.float32r
ALU = mybir.AluOpType
ACT = mybir.ActivationFunctionType
AX_X = mybir.AxisListType.X

NB = 16
T = 256
P = 128
NT = T // P
LN_EPS = 1e-5
MASKED = -1e30
ARENA = 6912, 10624


class Step:

    def __init__(self, base, s, per):
        self.base, self.s, self.per = base, s, per
        self.item = base + s // per
        self.count = base * per + s
        self.p = s % per

    def shift(self, by):
        return Step(self.base, self.s + by, self.per)

    @property
    def real(self):
        return not isinstance(self.base, int) or 0 <= self.count < NB * self.per

    def ring(self, n):
        return self.s % n


def walk(eng, per, unroll, lead, lag, step):
    for s in range(-lead, unroll * per):
        step(Step(0, s, per))
    with eng.Fori(1, NB // unroll - 1) as lap:
        for s in range(unroll * per):
            step(Step(lap * unroll, s, per))
    for s in range((NB - unroll) * per, NB * per + lag):
        step(Step(0, s, per))


def wait(eng, sem, step, each=1, extra=0, item=False):
    if not step.real:
        return
    n = (step.item if item else step.count) * each + each - extra
    eng.wait_ge(sem, n)


def hold(dve, spare):
    dve.memset(spare, 0.0)


def wait_ring(eng, sems, step):
    if step.real:
        eng.wait_ge(sems[step.ring(len(sems))], (step.base * (step.per // len(sems)) + step.s // len(sems)) * 16 + 16)


def signals(nc, ctx, prefix, names):
    sems = {x: nc.alloc_semaphore(f"{prefix}{x}") for x in names}

    def give_back():
        nc.clear_and_free_semaphores(list(sems.values()))
        nc.all_engine_barrier(sem_only=True)

    ctx.callback(give_back)
    return sems


class Norms:

    def __init__(self, nc, ctx):
        def sb(name, shape):
            return ctx.enter_context(nc.sbuf_tensor(name, shape, F32))

        self.x = sb("x", [P, NB, NT, P])
        self.stats = sb("row_stats", [P, NB, NT, 6])
        self.mean = sb("row_mean", [P, NB, NT])
        self.half_gap = sb("row_half_gap", [P, NB, NT])
        self.m2 = sb("row_m2", [P, NB, NT])
        self.var = sb("row_var", [P, NB, NT])
        self.std = sb("row_std", [P, NB, NT])
        self.rstd = sb("row_rstd", [P, NB, NT])
        self.xn = sb("xn", [P, NT, P])
        self.delta = sb("delta", [P, NT, P])
        self.hT = sb("hT", [P, 2, T])
        self.hT2 = ctx.enter_context(nc.sbuf_tensor("hT2", [P, 2, 2, T], F32R))



def matmul3(pe, out, left, right, start=True, stop=True):
    pe.matmul(out, left[0], right[0], start=start, stop=False, skip_group_check=True)
    pe.matmul(out, left[0], right[1], start=False, stop=False, skip_group_check=True)
    return pe.matmul(out, left[1], right[0], start=False, stop=stop, skip_group_check=True)


def cut_hT(act, n, at, ready, rounded):
    wait(act, ready, at, item=True)
    r = at.s // at.per % 2
    act.copy(n.hT2[:, r, 0, :], n.hT[:, r, :]).then_inc(rounded, 1)


def cut_hT_rest(pool, n, at, rounded, rest_ready):
    wait(pool, rounded, at, item=True)
    r = at.s // at.per % 2
    pool.tensor_tensor(n.hT2[:, r, 1, :], n.hT[:, r, :], n.hT2[:, r, 0, :], ALU.subtract).then_inc(rest_ready, 1)


def var_of_rows(dve, n, chain, var_ready):
    s = n.stats
    dve.tensor_tensor(n.mean[:], s[:, :, :, 1], s[:, :, :, 4], ALU.add)
    dve.tensor_tensor(n.half_gap[:], s[:, :, :, 1], s[:, :, :, 4], ALU.subtract)
    dve.tensor_tensor(n.m2[:], s[:, :, :, 2], s[:, :, :, 5], ALU.add).then_inc(chain, 1)
    dve.wait_ge(chain, 1)
    dve.tensor_scalar(n.mean[:], n.mean[:], 0.5, None, ALU.mult)
    dve.tensor_scalar(n.m2[:], n.m2[:], 1.0 / P, LN_EPS, ALU.mult, ALU.add)
    dve.scalar_tensor_tensor(out=n.half_gap[:], in0=n.half_gap[:], scalar=0.25, in1=n.half_gap[:],
                             op0=ALU.mult, op1=ALU.mult).then_inc(chain, 1)
    dve.wait_ge(chain, 2)
    dve.tensor_tensor(n.var[:], n.m2[:], n.half_gap[:], ALU.add).then_inc(var_ready, 1)


def std_of_rows(act, n, var_ready, std_ready):
    act.wait_ge(var_ready, 1)
    act.activation(n.std[:], n.var[:], ACT.Sqrt).then_inc(std_ready, 1)


def rstd_of_rows(dve, n, std_ready, rstd_ready):
    dve.wait_ge(std_ready, 1)
    dve.reciprocal(n.rstd[:], n.std[:]).then_inc(rstd_ready, 1)
    dve.wait_ge(rstd_ready, 1)


def normalise(dve, n, at, xn_used, xn_ready):
    wait(dve, xn_used, at.shift(-at.per), item=True)
    for t in range(NT):
        k = dve.tensor_scalar(n.xn[:, t, :], n.x[:, at.item, t, :], n.mean[:, at.item, t:t + 1],
                              n.rstd[:, at.item, t:t + 1], ALU.subtract, ALU.mult)
    k.then_inc(xn_ready, 1)


def add_residual(dve, n, at, y, gate, bias, chain, per_item, parts, chain0=2):
    k = at.item * per_item + chain0
    biased = 0 if bias is None else 1
    if "bias" in parts and biased:
        dve.tensor_tensor(n.delta[:], y, bias, ALU.add).then_inc(chain, 1)
    if "gate" in parts:
        if biased:
            dve.wait_ge(chain, k + 1)
        g = gate[:, at.item, :].unsqueeze(1).to_broadcast([P, NT, P])
        dve.tensor_tensor(n.delta[:], n.delta[:] if biased else y, g, ALU.mult).then_inc(chain, 1)
    if "add" in parts:
        dve.wait_ge(chain, k + biased + 1)
        dve.tensor_tensor(n.x[:, at.item, :, :], n.x[:, at.item, :, :], n.delta[:], ALU.add).then_inc(chain, 1)
    if "stats" in parts:
        dve.wait_ge(chain, k + biased + 2)
        for t in range(NT):
            i = dve.bn_stats(n.stats[:, at.item, t, :], n.x[:, at.item, t, :])
        return i


def residual_by_pool(pool, n, at, y, gate, y_ready, each, weighted, added, item=False):
    wait(pool, added, at.shift(-at.per), item=True)
    wait(pool, y_ready, at, each, item=item)
    g = gate[:, at.item, :].unsqueeze(1).to_broadcast([P, NT, P])
    pool.tensor_tensor(n.delta[:], y, g, ALU.mult).then_inc(weighted, 1)
    wait(pool, weighted, at, item=True)
    pool.tensor_tensor(n.x[:, at.item, :, :], n.x[:, at.item, :, :], n.delta[:], ALU.add).then_inc(added, 1)


def row_stats(dve, n, at, added):
    wait(dve, added, at, item=True)
    for t in range(NT):
        dve.bn_stats(n.stats[:, at.item, t, :], n.x[:, at.item, t, :])


ALL_PARTS = ("bias", "gate", "add", "stats")


def prologue(nc, d, k, first):
    with ExitStack() as ctx:
        n = k.norms
        cT = ctx.enter_context(nc.sbuf_tensor("cT", [P, 4 * NB], F32))
        silu_c = ctx.enter_context(nc.sbuf_tensor("silu_c", [P, 4 * NB], F32))
        wmod = ctx.enter_context(nc.sbuf_tensor("wmod", [P, 4, 6 * P], F32))
        mag = ctx.enter_context(nc.sbuf_tensor("gate_size", [NB, 8, P], F32))
        sign = ctx.enter_context(nc.sbuf_tensor("gate_sign", [NB, 8, P], F32))
        gates = ctx.enter_context(nc.sbuf_tensor("gates", [NB, 8, P], F32))
        maskf = ctx.enter_context(nc.sbuf_tensor("maskf", [P, P], F32))
        mod_ps, gate_ps = k.banks[0][:, 0:16 * NB], [k.banks[1 + h][0:NB, :] for h in range(2)]
        sems = signals(nc, ctx, "pro_", ("mod_in", "x_in", "consts_in", "silu", "mod_mm", "gates", "gate_abs",
                                         "gate_steps", "gates_out"))
        with nc.Block() as block:

            @block.sync
            def _(sp):
                sp.dma_start(cT[:], d["cT"]).then_inc(sems["mod_in"], 16)
                sp.dma_start(wmod[:], d["wmod"]).then_inc(sems["mod_in"], 16)
                for g in range(4):
                    sp.dma_start(n.x[:, 4 * g:4 * g + 4], d["x"].rearrange("b (t p) d -> p b t d", p=P)[:, 4 * g:4 * g + 4]
                                 ).then_inc(sems["x_in"], 16)
                sp.dma_start(k.ident[:], d["ident"]).then_inc(sems["consts_in"], 16)
                sp.dma_start(maskf[:], d["causal"]).then_inc(sems["consts_in"], 16)
                load_weights(sp, nc, k, d, first)
                sp.wait_ge(sems["gates"], 1)
                sp.dma_start(k.gates_dram, gates[:]).then_inc(sems["gates_out"], 16)
                sp.wait_ge(sems["gates_out"], 16)
                load_gate(sp, k, first)

            @block.scalar
            def _(act):
                act.wait_ge(sems["mod_in"], 32)
                act.activation(silu_c[:], cT[:], ACT.Silu).then_inc(sems["silu"], 1)
                act.wait_ge(sems["mod_mm"], 1)
                for h in range(2):
                    i = act.activation(mag[:, 4 * h:4 * h + 4, :], gate_ps[h].rearrange("b (s d) -> b s d", s=4), ACT.Abs)
                i.then_inc(sems["gate_abs"], 1)

            @block.tensor
            def _(pe):
                pe.wait_ge(sems["mod_in"], 32)
                pe.wait_ge(sems["silu"], 1)
                for layer in range(4):
                    c = silu_c[:, layer * NB:(layer + 1) * NB]
                    for j, kind in enumerate((0, 1, 3, 4)):
                        at = (layer * 4 + j) * NB
                        pe.matmul(mod_ps[:, at:at + NB], wmod[:, layer, kind * P:(kind + 1) * P], c,
                                  start=True, stop=True)
                    for j, kind in enumerate((2, 5)):
                        at = ((layer * 2 + j) % 4) * P
                        mm = pe.matmul(gate_ps[layer // 2][:, at:at + P], c,
                                       wmod[:, layer, kind * P:(kind + 1) * P], start=True, stop=True)
                mm.then_inc(sems["mod_mm"], 1)

            @block.vector
            def _(dve):
                dve.wait_ge(sems["mod_mm"], 1)
                m = mod_ps.rearrange("p (l j b) -> p l j b", l=8, j=2)
                dve.tensor_copy(k.mod[:, :, 0, :], m[:, :, 0, :])
                dve.tensor_scalar(k.mod[:, :, 1, :], m[:, :, 1, :], 1.0, None, ALU.add)
                dve.wait_ge(sems["gate_abs"], 1)
                for h in range(2):
                    g = gate_ps[h].rearrange("b (s d) -> b s d", s=4)
                    i = dve.tensor_scalar(sign[:, 4 * h:4 * h + 4, :], g, 0.0, 2.0, ALU.is_ge, ALU.mult)
                dve.tensor_scalar(mag[:], mag[:], 0.25, None, ALU.max).then_inc(sems["gate_steps"], 1)
                dve.wait_ge(sems["gate_steps"], 1)
                dve.scalar_tensor_tensor(out=gates[:], in0=sign[:], scalar=-1.0, in1=mag[:],
                                         op0=ALU.add, op1=ALU.mult).then_inc(sems["gates"], 1)
                dve.wait_ge(sems["consts_in"], 32)
                dve.tensor_copy(k.ident_bf[:], k.ident[:])
                dve.tensor_copy(k.causal_bf[:], maskf[:])
                for b in range(NB):
                    if b % 4 == 0:
                        dve.wait_ge(sems["x_in"], 4 * b + 16)
                    for t in range(NT):
                        dve.bn_stats(n.stats[:, b, t, :], n.x[:, b, t, :])


def load_gate(sp, k, phase):
    sp.dma_start(k.gate[phase % 2][:], k.gates_dram[:, phase, :].partition_broadcast(P)).then_inc(k.gate_in[phase], 16)


def load_weights(sp, nc, k, d, phase):
    at = 0
    for name, shape, parts in WEIGHTS[phase]:
        size = int(np.prod(shape))
        sp.dma_start(k.arena[phase % 2][0:parts, at:at + size], d[name]).then_inc(k.weights_in[phase], 16)
        at += size
    assert at <= ARENA[phase % 2]


def weights(k, phase):
    at, views = 0, {}
    for name, shape, parts in WEIGHTS[phase]:
        size = int(np.prod(shape))
        v = k.arena[phase % 2][0:parts, at:at + size]
        if len(shape) == 2:
            v = v.rearrange("p (a b) -> p a b", a=shape[0])
        elif len(shape) == 3:
            v = v.rearrange("p (a b c) -> p a b c", a=shape[0], b=shape[1])
        views[name] = v
        at += size
    return views


class Shared:
    pass


ROPE_WEIGHTS = [[(f"wqk{x}", (4, P), P), (f"wv{x}", (P,), P), (f"wproj{x}", (P,), P), (f"rope_q{x}", (2, T), P),
                 (f"rope_k{x}", (2, T), P), (f"head_rows{x}", (P,), 16)]
                for x in (2, 3)]
WEIGHTS = [
    [("wqT0", (16, P), 64), ("wkT0", (16, P), 64), ("wv0", (1024,), P), ("wo0", (8, P), P), ("bo0", (P,), P)],
    [("e1w", (16, P), P), ("e2w", (16, P), P), ("e1b", (16,), P), ("rw", (15,), P), ("rb", (15,), P),
     ("e2b", (P,), 16)],
    [("wkT", (8, P), P), ("qb1", (2, 8), P), ("w_relT", (8, 2, 96), P), ("wqT", (8, P), P), ("positions", (2, 512), 96),
     ("wv1", (1024,), P), ("wo1", (8, P), P), ("bo1", (P,), P)],
    [("w12", (8, 512), P), ("w3", (8, 2, P), P), ("gw1", (8,), P)],
    ROPE_WEIGHTS[0],
    [("base", (1156,), P), ("task", (8, 1156), P), ("gw1_2", (P,), P), ("gb1", (1,), P), ("gw2", (8,), P),
     ("gb2", (8,), P)],
    ROPE_WEIGHTS[1],
    [("gu", (5, 2, P), P), ("down", (4, 2 * P), P), ("shared", (P,), P), ("rw3", (8,), P)],
]


def causal_transposes(pe, pT, p, ident):
    for block in range(3):
        mm = pe.transpose(pT[:, block * P:(block + 1) * P], p[:, block * P:(block + 1) * P], ident)
    return mm


def modulated(act, k, phase, at, ps, hT, sem):
    act.activation(hT, ps, ACT.Identity, scale=k.mod[:, phase, 1, bass.ds(at.item, 1)],
                   bias=k.mod[:, phase, 0, bass.ds(at.item, 1)]).then_inc(sem, 1)


def attention0(nc, d, k):
    phase, PER = 0, 8
    n = k.norms
    w = weights(k, phase)
    EPS = 1e-8
    C = 3 * P
    with ExitStack() as ctx:
        def sb(name, shape):
            return ctx.enter_context(nc.sbuf_tensor("a0_" + name, shape, F32))

        A = ctx.enter_context(nc.sbuf_tensor("a0_A", [P, 2 * PER, 2, P], F32R))
        xA = ctx.enter_context(nc.sbuf_tensor("a0_xA", [P, 4, 2, T], F32R))
        v = sb("v", [P, 4, NT, P])
        p = sb("p", [P, 4, 2, C])
        pT = sb("pT", [P, 2, 2, C])
        oT = sb("oT", [P, 2, T])
        nmax = sb("nmax", [P, 2, 2, NT])
        sums = sb("sums", [P, 2, 2, NT])
        den = sb("den", [P, 2, 2, NT])
        rec = sb("rec", [P, 2, 2, NT])
        xA_ps = k.banks[0:2]
        s_ps, pT_ps = k.banks[2:4], k.banks[4:6]
        o_ps, y_ps = k.banks[6], k.banks[7]
        names = ("chain", "var", "std", "rstd", "xn", "ht_mm", "ht", "ht_rounded", "ht_cut", "A_mm", "A_rounded", "A_cut",
                 "xA_mm", "xA_rounded", "xA", "v", "s_mm",
                 "nmax", "masked", "exp", "den", "rec", "p", "pT_mm", "pT0", "pT1", "o_mm", "oT", "y_mm", "res")
        s = signals(nc, ctx, "a0_", names)
        LAST, LEAD, LAG = PER - 1, 6, 4

        def halves(x, i, first, end):
            return [x[:, i, part, first:end] for part in range(2)]

        with nc.Block() as block:

            @block.sync
            def _(sp):
                prefetch(sp, nc, k, d, phase)

            @block.gpsimd
            def _(pool):
                def step(at):
                    ni = at.shift(3)
                    if at.p == 5 and ni.real:
                        cut_hT_rest(pool, n, ni, s["ht_rounded"], s["ht_cut"])

                walk(pool, PER, 2, LEAD, LAG, step)

            @block.scalar
            def _(act):
                std_of_rows(act, n, s["var"], s["std"])
                for h in range(2 * PER):
                    act.wait_ge(s["A_mm"], h + 1)
                    act.activation(A[:, h, 0, :], k.banks[h % 4][:, 0:P], ACT.Identity, scale=64 ** -0.5
                                   ).then_inc(s["A_rounded"], 1)

                def step(at):
                    nx, b1, b2, b3 = at.shift(1), at.shift(-1), at.shift(-2), at.shift(-3)
                    def exps(h):
                        r = at.ring(2)
                        wait(act, s["nmax"], at, 2, 1 - h)
                        wait(act, s["masked"], at, 2, 1 - h)
                        wait(act, s["pT_mm"], at.shift(-4), 2)
                        act.activation(p[:, at.ring(4), h, 0:P], s_ps[h][:, 0:P], ACT.Exp,
                                       bias=nmax[:, r, h, 0:1], accum_out=sums[:, r, h, 0:1])
                        act.activation(p[:, at.ring(4), h, P:C], s_ps[h][:, T:2 * T], ACT.Exp,
                                       bias=nmax[:, r, h, 1:2], accum_out=sums[:, r, h, 1:2]).then_inc(s["exp"], 1)

                    if b3.real:
                        wait(act, s["o_mm"], b3)
                        wait(act, s["y_mm"], b3.shift(-2))
                        act.copy(oT[:, b3.ring(2), :], o_ps[:, 0:T]).then_inc(s["oT"], 1)
                    if b2.real:
                        wait(act, s["pT_mm"], b2, 2)
                        wait(act, s["o_mm"], b2.shift(-2))
                        act.copy(pT[:, b2.ring(2), 1, :], pT_ps[1][:, 0:C]).then_inc(s["pT1"], 1)
                    if at.p == 5:
                        ni = at.shift(3)
                        if ni.real:
                            wait(act, s["ht_mm"], ni, item=True)
                            modulated(act, k, phase, ni, xA_ps[0][:, T:2 * T], n.hT[:, ni.s // PER % 2, :], s["ht"])
                            cut_hT(act, n, ni, s["ht"], s["ht_rounded"])
                    if nx.real:
                        wait(act, s["s_mm"], nx.shift(-2), 2)
                        for h in range(2):
                            wait(act, s["xA_mm"], nx, 2, 1 - h)
                            act.copy(xA[:, 2 * nx.ring(2) + h, 0, :], xA_ps[h][:, 0:T]).then_inc(s["xA_rounded"], 1)
                        wait(act, s["o_mm"], nx.shift(-4))
                        act.copy(v[:, nx.ring(4)], xA_ps[1][:, T:2 * T].rearrange("p (t d) -> p t d", t=NT)).then_inc(s["v"], 1)
                    if at.real:
                        exps(0)
                    if at.real:
                        exps(1)

                walk(act, PER, 2, LEAD, LAG, step)

            @block.tensor
            def _(pe):
                pe.wait_ge(k.weights_in[phase], 16 * len(WEIGHTS[phase]))
                for h in range(2 * PER):
                    if h >= 4:
                        pe.wait_ge(s["A_cut"], h - 3)
                    pe.matmul(k.banks[h % 4][:, 0:P], w["wqT0"][:, h, :], w["wkT0"][:, h, :], start=True, stop=True
                              ).then_inc(s["A_mm"], 1)
                pe.wait_ge(s["A_cut"], 2 * PER)

                def step(at):
                    nx, b1, b2, b3 = at.shift(1), at.shift(-1), at.shift(-2), at.shift(-3)
                    ni = at.shift(3)
                    if at.p == 5 and ni.real:
                        wait(pe, s["xn"], ni, item=True)
                        wait(pe, s["xA"], at, 2, 1)
                        for t in range(NT):
                            mm = pe.transpose(xA_ps[0][:, T + t * P:T + (t + 1) * P], n.xn[:, t, :], k.ident[:])
                        mm.then_inc(s["ht_mm"], 1)
                    if b2.real:
                        wait(pe, s["p"], b2)
                        wait(pe, s["pT0"], b2.shift(-1))
                        wait(pe, s["pT1"], b2.shift(-1))
                        for h in range(2):
                            causal_transposes(pe, pT_ps[h], p[:, b2.ring(4), h, :], k.ident[:]).then_inc(s["pT_mm"], 1)
                    if at.real:
                        for h in range(2):
                            wait(pe, s["xA"], at, 2, 1 - h)
                            wait(pe, s["exp"], at.shift(-1), 2, 1 - h)
                            for t in range(NT):
                                mm = matmul3(pe, s_ps[h][:, t * T:(t + 1) * T],
                                             halves(xA, 2 * at.ring(2) + h, t * P, (t + 1) * P),
                                             halves(n.hT2, at.s // PER % 2, 0, T), start=(t == 0))
                            mm.then_inc(s["s_mm"], 1)
                    if nx.real:
                        c, item = nx.p * P, nx.s // PER % 2
                        if nx.p == 0:
                            wait(pe, s["ht_cut"], nx, item=True)
                        if at.p == 5:
                            wait(pe, s["ht"], at.shift(3), item=True)
                        for h in range(2):
                            wait(pe, s["xA"], nx.shift(-1), 2, 1 - h)
                            for t in range(NT if h else 0):
                                pe.matmul(xA_ps[1][:, T + t * P:T + (t + 1) * P], n.hT[:, item, t * P:(t + 1) * P],
                                          w["wv0"][:, c:c + P], start=True, stop=True)
                            matmul3(pe, xA_ps[h][:, 0:T], halves(A, 2 * nx.p + h, 0, P), halves(n.hT2, item, 0, T)
                                    ).then_inc(s["xA_mm"], 1)
                    if at.real:
                        for h in range(2):
                            wait(pe, s["nmax"], at, 2, 1 - h)
                            pe.matmul(s_ps[h][:, 0:P], k.ident_bf[:], k.causal_bf[:], start=False, stop=True,
                                      skip_group_check=True)
                            pe.matmul(s_ps[h][:, T + P:2 * T], k.ident_bf[:], k.causal_bf[:], start=False, stop=True,
                                      skip_group_check=True).then_inc(s["masked"], 1)
                    if b2.real:
                        wait(pe, s["pT0"], b2)
                        wait(pe, s["pT1"], b2)
                        wait(pe, s["v"], b2)
                        wait(pe, s["oT"], b2.shift(-1))
                        r = b2.ring(2)
                        for j in range(NT):
                            for h in range(2):
                                mm = pe.matmul(o_ps[64 * h:64 * h + 64, j * P:T],
                                               v[:, b2.ring(4), j, 64 * h:64 * h + 64],
                                               pT[:, r, h, 0:T] if j == 0 else pT[:, r, h, T:C],
                                               start=(j == 0), stop=(j == 1), skip_group_check=True)
                        mm.then_inc(s["o_mm"], 1)
                    if b3.real:
                        wait(pe, s["oT"], b3)
                        before = b3.shift(-PER)
                        if b3.p == 0 and before.real:
                            pe.wait_ge(s["chain"], before.item * 3 + 3)
                        for t in range(NT):
                            mm = pe.matmul(y_ps[:, t * P:(t + 1) * P], oT[:, b3.ring(2), t * P:(t + 1) * P],
                                           w["wo0"][:, b3.p, :], start=(b3.p == 0 and t == 0),
                                           stop=(b3.p == LAST), skip_group_check=True)
                        mm.then_inc(s["y_mm"], 1)

                walk(pe, PER, 2, LEAD, LAG, step)

            @block.vector
            def _(dve):
                var_of_rows(dve, n, s["chain"], s["var"])
                rstd_of_rows(dve, n, s["std"], s["rstd"])
                dve.wait_ge(k.weights_in[phase], 16 * len(WEIGHTS[phase]))
                for h in range(2 * PER):
                    dve.wait_ge(s["A_rounded"], h + 1)
                    dve.scalar_tensor_tensor(out=A[:, h, 1, :], in0=k.banks[h % 4][:, 0:P], scalar=64 ** -0.5,
                                             in1=A[:, h, 0, :], op0=ALU.mult, op1=ALU.subtract).then_inc(s["A_cut"], 1)
                dve.wait_ge(k.gate_in[phase], 16)

                def residual(item, *parts):
                    return add_residual(dve, n, item, y_ps[:, 0:T].rearrange("p (t d) -> p t d", t=NT),
                                        k.gate[phase % 2], w["bo0"].unsqueeze(1).to_broadcast([P, NT, P]), s["chain"],
                                        3, parts)

                def step(at):
                    nx, b1, b2, b3 = at.shift(1), at.shift(-1), at.shift(-2), at.shift(-3)
                    ended = b3.real and b3.p == LAST
                    after = at.shift(-4).real and at.p == 3
                    if after:
                        residual(at.shift(-4), "add")
                    if at.p == 2 and at.shift(6).real:
                        normalise(dve, n, at.shift(6), s["ht_mm"], s["xn"])
                    if b2.real:
                        wait(dve, s["pT_mm"], b2, 2, 1)
                        wait(dve, s["o_mm"], b2.shift(-2))
                        dve.tensor_copy(pT[:, b2.ring(2), 0, :], pT_ps[0][:, 0:C]).then_inc(s["pT0"], 1)
                    if at.real:
                        for h in range(2):
                            wait(dve, s["s_mm"], at, 2, 1 - h)
                            wait(dve, s["exp"], at.shift(-2), 2)
                            dve.tensor_reduce(nmax[:, at.ring(2), h, :],
                                              s_ps[h][:].rearrange("p (t k) -> p t k", t=NT), AX_X, ALU.max,
                                              negate=True).then_inc(s["nmax"], 1)
                    if after:
                        residual(at.shift(-4), "stats").then_inc(s["res"], 1)
                    if b1.real:
                        r = b1.ring(2)
                        wait(dve, s["exp"], b1, 2)
                        dve.tensor_scalar(den[:, r], sums[:, r], EPS, None, ALU.add).then_inc(s["den"], 1)
                        wait(dve, s["den"], b1)
                        dve.reciprocal(rec[:, r], den[:, r]).then_inc(s["rec"], 1)
                        wait(dve, s["rec"], b1)
                        for h in range(2):
                            for t in range(NT):
                                c = p[:, b1.ring(4), h, 0:P] if t == 0 else p[:, b1.ring(4), h, P:C]
                                i = dve.tensor_scalar(c, c, rec[:, r, h, t:t + 1], None, ALU.mult)
                        i.then_inc(s["p"], 1)
                    if nx.real:
                        for h in range(2):
                            if h == 0:
                                wait(dve, s["xA_rounded"], nx, 2, 1)
                            else:
                                wait(dve, s["v"], nx)
                            dve.tensor_tensor(xA[:, 2 * nx.ring(2) + h, 1, :], xA_ps[h][:, 0:T],
                                              xA[:, 2 * nx.ring(2) + h, 0, :], ALU.subtract).then_inc(s["xA"], 1)
                    if ended:
                        wait(dve, s["y_mm"], b3)
                        residual(b3, "bias")
                    if ended:
                        residual(b3, "gate")

                walk(dve, PER, 2, LEAD, LAG, step)


def prefetch(sp, nc, k, d, phase):
    if phase + 1 < len(WEIGHTS):
        load_weights(sp, nc, k, d, phase + 1)
        load_gate(sp, k, phase + 1)


def build(nc, d, out, phases, first=0):
    with ExitStack() as ctx:
        k = Shared()
        k.norms = Norms(nc, ctx)
        k.banks = [ctx.enter_context(nc.psum_tensor(f"bank{i}", [P, 512], F32)) for i in range(8)]
        k.ident = ctx.enter_context(nc.sbuf_tensor("ident", [P, P], F32))
        k.ident_bf = ctx.enter_context(nc.sbuf_tensor("ident_bf", [P, P], BF16))
        k.causal_bf = ctx.enter_context(nc.sbuf_tensor("causal_bf", [P, P], BF16))
        k.spare = ctx.enter_context(nc.sbuf_tensor("spare", [1, 1], F32))[:]
        k.mod = ctx.enter_context(nc.sbuf_tensor("mod", [P, 8, 2, NB], F32))
        k.gate = [ctx.enter_context(nc.sbuf_tensor(f"gate{i}", [P, NB, P], F32)) for i in range(2)]
        k.arena = [ctx.enter_context(nc.sbuf_tensor(f"arena{i}", [P, ARENA[i]], F32)) for i in range(2)]
        k.gates_dram = nc.dram_tensor("gates_dram", (NB, 8, P), F32, kind="Internal").ap()
        k.weights_in = [ctx.enter_context(nc.semaphore(f"weights_in{i}")) for i in range(len(WEIGHTS))]
        k.gate_in = [ctx.enter_context(nc.semaphore(f"gate_in{i}")) for i in range(len(WEIGHTS))]
        stored = ctx.enter_context(nc.semaphore("stored"))
        prologue(nc, d, k, first)
        for f in phases:
            f(nc, d, k)
        with nc.Block() as block:

            @block.sync
            def _(sp):
                for g in range(4):
                    sp.dma_start(out.rearrange("b (t p) d -> p b t d", p=P)[:, 4 * g:4 * g + 4],
                                 k.norms.x[:, 4 * g:4 * g + 4]).then_inc(stored, 16)
                sp.wait_ge(stored, 64)


def start_norms(dve, n, s):
    var_of_rows(dve, n, s["chain"], s["var"])
    rstd_of_rows(dve, n, s["std"], s["rstd"])


def softmax_top(dve, s, spare, at, E, K, r, b, acc_each=1, transposed=True):
    k = at.item * 5

    def link(i, m):
        i.then_inc(s["top"], 1)
        dve.wait_ge(s["top"], k + m)

    wait(dve, s["rexp"], at, item=True)
    link(dve.reciprocal(b["rec"][:], b["sums"][:]), 1)
    for t in range(NT):
        i = dve.tensor_scalar(b["probs"][:, t, 0:E], b["e"][:, t, :], b["rec"][:, t:t + 1], None, ALU.mult)
    link(i, 2)
    hold(dve, spare)
    for t in range(NT):
        i = dve.max(b["max8"][:, t, :], b["probs"][:, t, :])
    link(i, 3)
    link(dve.tensor_copy(b["top"][:, :, 0:K], b["max8"][:, :, 0:K]), 4)
    hold(dve, spare)
    for t in range(NT):
        i = dve.match_replace(b["rest"][:, t, :], b["top"][:, t, :], b["probs"][:, t, :], 0.0)
    link(i, 5)
    before = at.shift(-at.per)
    wait(dve, s["acc"], before.shift(-before.p - 1), acc_each)
    if transposed:
        wait(dve, s["cwT_mm"], at.shift(-2 * at.per), item=True)
    dve.tensor_tensor(b["cw"][:, r, :, 0:E], b["probs"][:, :, 0:E], b["rest"][:, :, 0:E], ALU.subtract).then_inc(s["cw"], 1)


def router_tiles(nc, ctx, pre, E):
    b = {}

    def sb(name, *shape):
        b[name] = ctx.enter_context(nc.sbuf_tensor(pre + name, [P, *shape], F32))

    sb("logits", NT, E)
    sb("e", NT, E)
    sb("nmax", NT)
    sb("sums", NT)
    sb("rec", NT)
    sb("probs", NT, E + 8)
    sb("rest", NT, E + 8)
    sb("max8", NT, 8)
    sb("top", NT, 8)
    sb("cw", 2, NT, 16)
    return b


def ffn0(nc, d, k):
    phase, PER, E, K = 1, 16, 15, 3
    n = k.norms
    w = weights(k, phase)
    with ExitStack() as ctx:
        def sb(name, shape):
            return ctx.enter_context(nc.sbuf_tensor("f0_" + name, shape, F32))

        hidden = sb("hidden", [P, 2, T])
        acc = sb("acc", [P, 2, NT, P])
        e1w = ctx.enter_context(nc.sbuf_tensor("f0_e1w", [P, PER, 2, P], F32R))
        cwT = sb("cwT", [16, 2, T])
        b = router_tiles(nc, ctx, "f0_", E)
        h_ps, y_ps = k.banks[0:2], k.banks[2:4]
        ht_ps, rt_ps, cwT_ps = k.banks[4], k.banks[5], k.banks[6]
        names = ("chain", "var", "std", "rstd", "xn", "ht_mm", "ht", "ht_rounded", "ht_cut", "w_rounded", "w_cut", "rt_mm", "logits", "nmax", "rexp", "top", "cw",
                 "cwT_mm", "cwT", "h_mm", "hidden", "y_mm", "acc", "weighted", "added", "pads")
        s = signals(nc, ctx, "f0_", names)
        LAST = PER - 1

        with nc.Block() as block:

            @block.sync
            def _(sp):
                prefetch(sp, nc, k, d, phase)

            @block.gpsimd
            def _(pool):
                pool.wait_ge(k.gate_in[phase], 16)

                def step(at):
                    if at.real and at.p == LAST:
                        residual_by_pool(pool, n, at, acc[:, at.s // PER % 2], k.gate[phase % 2], s["acc"], 2,
                                         s["weighted"], s["added"])
                    if at.p == 6 and at.shift(PER).real:
                        cut_hT_rest(pool, n, at.shift(PER), s["ht_rounded"], s["ht_cut"])

                walk(pool, PER, 2, 12, 2, step)

            @block.scalar
            def _(act):
                std_of_rows(act, n, s["var"], s["std"])
                act.wait_ge(k.weights_in[phase], 16 * len(WEIGHTS[phase]))
                for e in range(0, PER, 4):
                    act.copy(e1w[:, e:e + 4, 0, :], w["e1w"][:, e:e + 4, :]).then_inc(s["w_rounded"], 1)

                def step(at):
                    nx, ni = at.shift(1), at.shift(PER)
                    if nx.real:
                        wait(act, s["h_mm"], nx)
                        wait(act, s["y_mm"], nx.shift(-2))
                        act.activation(hidden[:, nx.ring(2), :], h_ps[nx.ring(2)][:, 0:T], ACT.Relu,
                                       bias=w["e1b"][:, nx.p:nx.p + 1]).then_inc(s["hidden"], 1)
                    r = (at.s // PER + 1) % 2
                    if at.p == 6 and ni.real:
                        wait(act, s["ht_mm"], ni, item=True)
                        wait(act, s["h_mm"], at.shift(-7))
                        modulated(act, k, phase, ni, ht_ps[:, 0:T], n.hT[:, r, :], s["ht"])
                        cut_hT(act, n, ni, s["ht"], s["ht_rounded"])
                    if at.p == 9 and ni.real:
                        wait(act, s["nmax"], ni, item=True)
                        for t in range(NT):
                            i = act.activation(b["e"][:, t, :], b["logits"][:, t, :], ACT.Exp, bias=b["nmax"][:, t:t + 1],
                                               accum_out=b["sums"][:, t:t + 1])
                        i.then_inc(s["rexp"], 1)
                    if at.p == 13 and ni.real:
                        wait(act, s["cwT_mm"], ni, item=True)
                        wait(act, s["y_mm"], at.shift(-14))
                        act.copy(cwT[:, r, :], cwT_ps[0:16, 0:T]).then_inc(s["cwT"], 1)

                walk(act, PER, 2, 12, 2, step)

            @block.tensor
            def _(pe):
                pe.wait_ge(k.weights_in[phase], 16 * len(WEIGHTS[phase]))

                def step(at):
                    nx, ni = at.shift(1), at.shift(PER)
                    if nx.real:
                        if nx.p == 0:
                            wait(pe, s["ht_cut"], nx, item=True)
                        if isinstance(at.base, int) and nx.s < PER:
                            pe.wait_ge(s["w_cut"], nx.s // 4 + 1)
                        wait(pe, s["hidden"], nx.shift(-2))
                        matmul3(pe, h_ps[nx.ring(2)][:, 0:T], [e1w[:, nx.p, part, :] for part in range(2)],
                                [n.hT2[:, nx.s // PER % 2, part, :] for part in range(2)]).then_inc(s["h_mm"], 1)
                    r = (at.s // PER + 1) % 2
                    if at.p == 6 and ni.real:
                        wait(pe, s["xn"], ni, item=True)
                        wait(pe, s["ht"], ni.shift(-PER), item=True)
                        for t in range(NT):
                            mm = pe.transpose(ht_ps[:, t * P:(t + 1) * P], n.xn[:, t, :], k.ident[:])
                        mm.then_inc(s["ht_mm"], 1)
                    if at.p == 8 and ni.real:
                        wait(pe, s["ht"], ni, item=True)
                        wait(pe, s["logits"], ni.shift(-PER), item=True)
                        for t in range(NT):
                            mm = pe.matmul(rt_ps[:, t * E:(t + 1) * E], n.hT[:, r, t * P:(t + 1) * P], w["rw"][:],
                                           start=True, stop=True)
                        mm.then_inc(s["rt_mm"], 1)
                    if at.p == 13 and ni.real:
                        wait(pe, s["cw"], ni, item=True)
                        wait(pe, s["cwT"], ni.shift(-PER), item=True)
                        for t in range(NT):
                            mm = pe.transpose(cwT_ps[0:16, t * P:(t + 1) * P], b["cw"][:, r, t, :], k.ident[:])
                        mm.then_inc(s["cwT_mm"], 1)
                    if at.real:
                        wait(pe, s["hidden"], at)
                        wait(pe, s["acc"], at.shift(-2), 2)
                        last = at.p == LAST
                        if last:
                            wait(pe, s["cwT"], at, item=True)
                        for t in range(NT):
                            y = y_ps[at.ring(2)][:, t * P:(t + 1) * P]
                            mm = pe.matmul(y, hidden[:, at.ring(2), t * P:(t + 1) * P], w["e2w"][:, at.p, :],
                                           start=(t == 0), stop=not last, skip_group_check=True)
                            if last:
                                mm = pe.matmul(y, cwT[:, at.s // PER % 2, t * P:(t + 1) * P], w["e2b"][:],
                                               start=False, stop=True, skip_group_check=True)
                        mm.then_inc(s["y_mm"], 1)

                walk(pe, PER, 2, 12, 2, step)

            @block.vector
            def _(dve):
                start_norms(dve, n, s)
                dve.memset(b["probs"][:], -1.0)
                dve.memset(b["top"][:], -1.0)
                dve.memset(b["cw"][:], 1.0).then_inc(s["pads"], 1)
                dve.wait_ge(s["pads"], 1)
                dve.wait_ge(k.weights_in[phase], 16 * len(WEIGHTS[phase]))
                for e in range(0, PER, 4):
                    dve.wait_ge(s["w_rounded"], e // 4 + 1)
                    dve.tensor_tensor(e1w[:, e:e + 4, 1, :], w["e1w"][:, e:e + 4, :], e1w[:, e:e + 4, 0, :], ALU.subtract
                                      ).then_inc(s["w_cut"], 1)
                dve.wait_ge(k.gate_in[phase], 16)

                def step(at):
                    ni = at.shift(PER)
                    r = (at.s // PER + 1) % 2
                    if at.p == 4 and ni.real:
                        normalise(dve, n, ni, s["ht_mm"], s["xn"])
                    if at.p == 9 and ni.real:
                        wait(dve, s["rt_mm"], ni, item=True)
                        dve.tensor_tensor(b["logits"][:], rt_ps[:, 0:NT * E].rearrange("p (t e) -> p t e", t=NT),
                                          w["rb"][:].unsqueeze(1).to_broadcast([P, NT, E]), ALU.add).then_inc(s["logits"], 1)
                        wait(dve, s["logits"], ni, item=True)
                        dve.tensor_reduce(b["nmax"][:], b["logits"][:], AX_X, ALU.max, negate=True).then_inc(s["nmax"], 1)
                    if at.p == 11 and ni.real:
                        softmax_top(dve, s, k.spare, ni, E, K, r, b, acc_each=2)
                    if at.real:
                        wait(dve, s["y_mm"], at)
                        place = at.s // PER % 2
                        y, c = y_ps[at.ring(2)], b["cw"][:, at.s // PER % 2]
                        if at.p == 0:
                            wait(dve, s["cw"], at, item=True)
                            wait(dve, s["weighted"], at.shift(-2 * PER), item=True)
                        if at.p == LAST:
                            wait(dve, s["acc"], at.shift(-1), 2)
                            dve.tensor_tensor(acc[:, place], acc[:, place], y[:, 0:T].rearrange("p (t d) -> p t d", t=NT),
                                              ALU.add).then_inc(s["acc"], 2)
                            return
                        for t in range(NT):
                            a, z = acc[:, place, t, :], y[:, t * P:(t + 1) * P]
                            wait(dve, s["acc"], at.shift(-1), 2, 1 - t)
                            if at.p == 0:
                                i = dve.tensor_scalar(a, z, c[:, t, 0:1], None, ALU.mult)
                            else:
                                i = dve.scalar_tensor_tensor(out=a, in0=z, scalar=c[:, t, at.p:at.p + 1], in1=a,
                                                             op0=ALU.mult, op1=ALU.add)
                            i.then_inc(s["acc"], 1)
                    if at.p == 1 and at.shift(-2).real:
                        row_stats(dve, n, at.shift(-2), s["added"])

                walk(dve, PER, 2, 12, 2, step)


def attention1(nc, d, k):
    phase, PER = 2, 8
    n = k.norms
    w = weights(k, phase)
    SCALE = P ** -0.5
    SPAN = T + P - 1
    PITCH = SPAN + 1
    with ExitStack() as ctx:
        def sb(name, shape):
            return ctx.enter_context(nc.sbuf_tensor("a1_" + name, shape, F32))

        def cut_sb(name, shape):
            return ctx.enter_context(nc.sbuf_tensor("a1_" + name, shape, F32R))

        A = cut_sb("A", [P, PER, 2, P])
        R = cut_sb("R", [P, PER, 2, 2 * T])
        c_col = sb("c_col", [P, PER])
        r_rows = sb("r_rows", [P, PER, 2 * T])
        Wrel_bias = sb("Wrel_bias", [96, 2, PER])
        xA = cut_sb("xA", [P, 2, 2, T])
        v = sb("v", [P, 4, NT, P])
        pos = sb("pos", [P, 2, NT, PITCH])
        shifted = sb("shifted", [P, 2, NT, T])
        p = sb("p", [P, 4, NT, T])
        WrelWq = p[0:96, 0].rearrange("q h (c d) -> q h c d", c=2)
        pT = sb("pT", [P, 2, NT, T])
        oT = sb("oT", [P, 2, T])
        r_row = oT[0:PER].rearrange("h a b -> h (a b)")
        top = sb("top", [P, 2, NT])
        nmax = sb("nmax", [P, 2, NT])
        sums = sb("sums", [P, 2, NT])
        rec = sb("rec", [P, 2, NT])
        r_dram = nc.dram_tensor("r_dram", (PER, 2 * T), F32, kind="Internal").ap()
        pos_dram = nc.dram_tensor("pos_dram", (4, NT, P, PITCH), F32, kind="Internal").ap()
        qh_ps, v_ps, pos_ps = k.banks[0], k.banks[1], k.banks[2:4]
        s_ps, pT_ps, o_ps, y_ps = k.banks[4:8]
        names = ("chain", "var", "std", "rstd", "xn", "ht_mm", "ht", "ht_rounded", "ht_cut", "bias_mm", "bias", "r_mm",
                 "r_row", "r_out", "r_in", "A_mm", "A_rounded", "A_cut", "WW_mm", "WW", "R_mm", "R_rounded", "R_cut",
                 "xA_mm", "xA_rounded", "xA", "v_mm", "v", "pos_mm", "pos", "s_mm", "sc", "nmax", "exp", "rec", "p",
                 "pT_mm", "pT", "o_mm", "oT", "y_mm", "res")
        s = signals(nc, ctx, "a1_", names + tuple(f"{x}{i}" for x in ("written", "shifted") for i in range(4)))
        written, shifted_in = ([s[f"{x}{i}"] for i in range(4)] for x in ("written", "shifted"))
        LAST = PER - 1
        LEAD, LAG = 7, 4

        def halves(x, i, first, end):
            return [x[:, i, part, first:end] for part in range(2)]

        with nc.Block() as block:

            @block.sync
            def _(sp):
                prefetch(sp, nc, k, d, phase)
                sp.wait_ge(s["r_row"], 1)
                sp.dma_start(r_dram, r_row).then_inc(s["r_out"], 16)
                sp.wait_ge(s["r_out"], 16)
                sp.dma_start(r_rows[:].rearrange("p h d -> p (h d)"), bass.AP(r_dram.tensor, 0, [[0, P], [1, PER * 2 * T]])
                             ).then_inc(s["r_in"], 16)

                def step(at):
                    n1, n2 = at.shift(1), at.shift(2)
                    if n1.real:
                        wait_ring(sp, written, n1)
                        start = n1.ring(4) * NT * P * PITCH + P - 1
                        skewed = bass.AP(pos_dram.tensor, start, [[PITCH - 1, P], [P * PITCH, NT], [1, T]])
                        sp.dma_start(shifted[:, n1.ring(2)], skewed).then_inc(shifted_in[n1.ring(4)], 16)
                    if n2.real:
                        wait(sp, s["pos"], n2)
                        sp.dma_start(pos_dram[n2.ring(4)].rearrange("t p c -> p t c")[:, :, 0:SPAN],
                                     pos[:, n2.ring(2), :, 0:SPAN]).then_inc(written[n2.ring(4)], 16)

                walk(sp, PER, 2, LEAD, LAG, step)

            @block.gpsimd
            def _(pool):
                def step(at):
                    ni = at.shift(5)
                    if at.p == 3 and ni.real:
                        cut_hT_rest(pool, n, ni, s["ht_rounded"], s["ht_cut"])

                walk(pool, PER, 2, LEAD, LAG, step)

            @block.scalar
            def _(act):
                std_of_rows(act, n, s["var"], s["std"])

                def round_R(h):
                    act.wait_ge(s["R_mm"], h + 1)
                    act.copy(R[:, h, 0, :], k.banks[4 + h % 2][:]).then_inc(s["R_rounded"], 1)

                for h in range(PER):
                    act.wait_ge(s["A_mm"], h + 1)
                    act.activation(A[:, h, 0, :], k.banks[h % 2][:, 0:P], ACT.Identity, scale=SCALE
                                   ).then_inc(s["A_rounded"], 1)
                    act.wait_ge(s["WW_mm"], h + 1)
                    if h >= 2:
                        act.wait_ge(s["R_mm"], h - 1)
                    act.activation(WrelWq[:, h % 2].rearrange("p c d -> p (c d)"), k.banks[2 + h % 2][0:96, 0:T],
                                   ACT.Identity, scale=SCALE).then_inc(s["WW"], 1)
                    if h:
                        round_R(h - 1)
                round_R(PER - 1)

                def step(at):
                    n1, n2, b2, b3 = at.shift(1), at.shift(2), at.shift(-2), at.shift(-3)
                    if b3.real:
                        wait(act, s["o_mm"], b3)
                        wait(act, s["y_mm"], b3.shift(-2))
                        act.copy(oT[:, b3.ring(2), :], o_ps[:, 0:T]).then_inc(s["oT"], 1)
                    if b2.real:
                        wait(act, s["pT_mm"], b2)
                        wait(act, s["o_mm"], b2.shift(-2))
                        act.copy(pT[:, b2.ring(2)], pT_ps[:].rearrange("p (j q) -> p j q", j=NT)
                                 ).then_inc(s["pT"], 1)
                    if n2.real:
                        wait(act, s["xA_mm"], n2)
                        wait(act, s["s_mm"], n2.shift(-2))
                        act.activation(xA[:, n2.ring(2), 0, :], qh_ps[:, 0:T], ACT.Identity,
                                       bias=c_col[:, n2.p:n2.p + 1]).then_inc(s["xA_rounded"], 1)
                    if n1.real:
                        wait(act, s["v_mm"], n1)
                        wait(act, s["o_mm"], n1.shift(-4))
                        act.copy(v[:, n1.ring(4)], v_ps[:, 0:T].rearrange("p (t d) -> p t d", t=NT)
                                 ).then_inc(s["v"], 1)
                    if at.p == 3:
                        ni = at.shift(5)
                        if ni.real:
                            wait(act, s["ht_mm"], ni, item=True)
                            modulated(act, k, phase, ni, qh_ps[:, T:2 * T], n.hT[:, ni.s // PER % 2, :], s["ht"])
                            cut_hT(act, n, ni, s["ht"], s["ht_rounded"])
                    if at.real:
                        r = at.ring(2)
                        wait(act, s["nmax"], at)
                        wait(act, s["pT_mm"], at.shift(-4))
                        for t in range(NT):
                            i = act.activation(p[:, at.ring(4), t, :], p[:, at.ring(4), t, :], ACT.Exp, bias=nmax[:, r, t:t + 1],
                                               accum_out=sums[:, r, t:t + 1])
                        i.then_inc(s["exp"], 1)

                walk(act, PER, 2, LEAD, LAG, step)

            @block.tensor
            def _(pe):
                pe.wait_ge(k.weights_in[phase], 16 * len(WEIGHTS[phase]))
                for h in range(PER):
                    pe.matmul(k.banks[6][:, h:h + 1], w["wkT"][:, h, :], w["qb1"][:, 0, h:h + 1], start=True, stop=True)
                    for c in range(2):
                        col = (1 + c) * PER + h
                        mm = pe.matmul(k.banks[6][0:96, col:col + 1], w["w_relT"][:, h, c, :], w["qb1"][:, 1, h:h + 1],
                                       start=True, stop=True)
                mm.then_inc(s["bias_mm"], 1)

                def make_R(h):
                    pe.wait_ge(s["WW"], h + 1)
                    if h >= 2:
                        pe.wait_ge(s["R_cut"], h - 1)
                    for c in range(2):
                        mm = pe.matmul(k.banks[4 + h % 2][:], WrelWq[:, h % 2, c, :], w["positions"][:, c, :],
                                       start=(c == 0), stop=(c == 1))
                    mm.then_inc(s["R_mm"], 1)

                for h in range(PER):
                    if h >= 2:
                        pe.wait_ge(s["A_cut"], h - 1)
                    pe.matmul(k.banks[h % 2][:, 0:P], w["wqT"][:, h, :], w["wkT"][:, h, :], start=True, stop=True
                              ).then_inc(s["A_mm"], 1)
                    if h >= 2:
                        pe.wait_ge(s["WW"], h - 1)
                    for c in range(2):
                        mm = pe.matmul(k.banks[2 + h % 2][0:96, c * P:(c + 1) * P], w["w_relT"][:, h, c, :],
                                       w["wqT"][:, h, :], start=True, stop=True)
                    mm.then_inc(s["WW_mm"], 1)
                    if h == 1:
                        pe.wait_ge(s["bias"], 1)
                        for c in range(2):
                            mm = pe.matmul(k.banks[7][0:PER, :], Wrel_bias[:, c, :], w["positions"][:, c, :],
                                           start=(c == 0), stop=(c == 1))
                        mm.then_inc(s["r_mm"], 1)
                    if h:
                        make_R(h - 1)
                make_R(PER - 1)
                pe.wait_ge(s["A_cut"], PER)
                pe.wait_ge(s["R_cut"], PER)
                pe.wait_ge(s["r_row"], 1)

                def step(at):
                    n1, n2, b2, b3 = at.shift(1), at.shift(2), at.shift(-2), at.shift(-3)
                    if b2.real:
                        wait(pe, s["p"], b2)
                        wait(pe, s["pT"], b2.shift(-1))
                        for j in range(NT):
                            for t in range(NT):
                                mm = pe.transpose(pT_ps[:, j * T + t * P:j * T + (t + 1) * P],
                                                  p[:, b2.ring(4), t, j * P:(j + 1) * P], k.ident[:])
                        mm.then_inc(s["pT_mm"], 1)
                    if n2.real:
                        item = n2.s // PER % 2
                        if n2.p == 0:
                            wait(pe, s["ht_cut"], n2, item=True)
                        wait(pe, s["xA"], n2.shift(-1))
                        if at.p == 4:
                            wait(pe, s["ht"], at.shift(4), item=True)
                        matmul3(pe, qh_ps[:, 0:T], halves(A, n2.p, 0, P), halves(n.hT2, item, 0, T)
                                ).then_inc(s["xA_mm"], 1)
                    if at.real:
                        wait(pe, s["xA"], at)
                        wait(pe, s["sc"], at.shift(-1))
                        for t in range(NT):
                            mm = matmul3(pe, s_ps[:, t * T:(t + 1) * T], halves(xA, at.ring(2), t * P, (t + 1) * P),
                                         halves(n.hT2, at.s // PER % 2, 0, T))
                        mm.then_inc(s["s_mm"], 1)
                    if n1.real:
                        c, item = n1.p * P, n1.s // PER % 2
                        wait(pe, s["v"], n1.shift(-1))
                        for t in range(NT):
                            mm = pe.matmul(v_ps[:, t * P:(t + 1) * P], n.hT[:, item, t * P:(t + 1) * P],
                                           w["wv1"][:, c:c + P], start=True, stop=True)
                        mm.then_inc(s["v_mm"], 1)
                    ni = at.shift(5)
                    if at.p == 3 and ni.real:
                        wait(pe, s["xn"], ni, item=True)
                        wait(pe, s["xA"], n2)
                        for t in range(NT):
                            mm = pe.transpose(qh_ps[:, T + t * P:T + (t + 1) * P], n.xn[:, t, :], k.ident[:])
                        mm.then_inc(s["ht_mm"], 1)
                    if b3.real:
                        wait(pe, s["oT"], b3)
                        before = b3.shift(-PER)
                        if b3.p == 0 and before.real:
                            pe.wait_ge(s["chain"], before.item * 3 + 3)
                        for t in range(NT):
                            mm = pe.matmul(y_ps[:, t * P:(t + 1) * P], oT[:, b3.ring(2), t * P:(t + 1) * P],
                                           w["wo1"][:, b3.p, :], start=(b3.p == 0 and t == 0), stop=(b3.p == LAST),
                                           skip_group_check=True)
                        mm.then_inc(s["y_mm"], 1)
                    if n2.real:
                        wait(pe, s["pos"], n2.shift(-1))
                        for t in range(NT):
                            first = P if t == 0 else 0
                            mm = matmul3(pe, pos_ps[t][:, 0:PITCH], halves(n.hT2, n2.s // PER % 2, t * P, (t + 1) * P),
                                         halves(R, n2.p, first, first + PITCH))
                        mm.then_inc(s["pos_mm"], 1)
                    if b2.real:
                        wait(pe, s["pT"], b2)
                        wait(pe, s["v"], b2)
                        wait(pe, s["oT"], b2.shift(-1))
                        for j in range(NT):
                            mm = pe.matmul(o_ps[:, 0:T], v[:, b2.ring(4), j, :], pT[:, b2.ring(2), j, :],
                                           start=(j == 0), stop=(j == 1))
                        mm.then_inc(s["o_mm"], 1)

                walk(pe, PER, 2, LEAD, LAG, step)

            @block.vector
            def _(dve):
                start_norms(dve, n, s)
                dve.wait_ge(s["bias_mm"], 1)
                dve.tensor_copy(c_col[:], k.banks[6][:, 0:PER])
                dve.tensor_copy(Wrel_bias[:].rearrange("p c h -> p (c h)"), k.banks[6][0:96, PER:3 * PER]
                                ).then_inc(s["bias"], 1)

                def cut_R(h):
                    dve.wait_ge(s["R_rounded"], h + 1)
                    dve.tensor_tensor(R[:, h, 1, :], k.banks[4 + h % 2][:], R[:, h, 0, :], ALU.subtract
                                      ).then_inc(s["R_cut"], 1)

                for h in range(PER):
                    dve.wait_ge(s["A_rounded"], h + 1)
                    dve.scalar_tensor_tensor(out=A[:, h, 1, :], in0=k.banks[h % 2][:, 0:P], scalar=SCALE,
                                             in1=A[:, h, 0, :], op0=ALU.mult, op1=ALU.subtract).then_inc(s["A_cut"], 1)
                    if h == 1:
                        dve.wait_ge(s["r_mm"], 1)
                        dve.tensor_copy(r_row, k.banks[7][0:PER, :]).then_inc(s["r_row"], 1)
                    if h:
                        cut_R(h - 1)
                cut_R(PER - 1)
                dve.wait_ge(s["r_in"], 16)
                dve.wait_ge(k.gate_in[phase], 16)

                def residual(item, *parts):
                    return add_residual(dve, n, item, y_ps[:, 0:T].rearrange("p (t d) -> p t d", t=NT),
                                        k.gate[phase % 2], w["bo1"].unsqueeze(1).to_broadcast([P, NT, P]), s["chain"],
                                        3, parts)

                def step(at):
                    n2, b1, b3 = at.shift(2), at.shift(-1), at.shift(-3)
                    ended = b3.real and b3.p == LAST
                    after = at.shift(-4).real and at.p == 3
                    if after:
                        residual(at.shift(-4), "add")
                    if at.p == 1 and at.shift(7).real:
                        normalise(dve, n, at.shift(7), s["ht_mm"], s["xn"])
                    if b1.real:
                        r = b1.ring(2)
                        wait(dve, s["exp"], b1)
                        dve.reciprocal(rec[:, r], sums[:, r]).then_inc(s["rec"], 1)
                        wait(dve, s["rec"], b1)
                        for t in range(NT):
                            i = dve.tensor_scalar(p[:, b1.ring(4), t, :], p[:, b1.ring(4), t, :], rec[:, r, t:t + 1], None, ALU.mult)
                        i.then_inc(s["p"], 1)
                    if n2.real:
                        wait(dve, s["xA_rounded"], n2)
                        dve.scalar_tensor_tensor(out=xA[:, n2.ring(2), 1, :], in0=qh_ps[:, 0:T],
                                                 scalar=c_col[:, n2.p:n2.p + 1], in1=xA[:, n2.ring(2), 0, :],
                                                 op0=ALU.add, op1=ALU.subtract).then_inc(s["xA"], 1)
                    if after:
                        residual(at.shift(-4), "stats").then_inc(s["res"], 1)
                    if at.real:
                        r = at.ring(2)
                        wait(dve, s["s_mm"], at)
                        wait_ring(dve, shifted_in, at)
                        wait(dve, s["pT_mm"], at.shift(-4))
                        hold(dve, k.spare)
                        for t in range(NT):
                            i = dve.tensor_tensor_reduce(p[:, at.ring(4), t, :], s_ps[:, t * T:(t + 1) * T],
                                                         shifted[:, r, t, :], 1.0, -3e38, ALU.add, ALU.max,
                                                         top[:, r, t:t + 1])
                        i.then_inc(s["sc"], 1)
                        wait(dve, s["sc"], at)
                        dve.tensor_scalar(nmax[:, r], top[:, r], -1.0, None, ALU.mult).then_inc(s["nmax"], 1)
                    if n2.real:
                        wait(dve, s["pos_mm"], n2)
                        wait_ring(dve, written, n2.shift(-2))
                        for t in range(NT):
                            first = P if t == 0 else 0
                            i = dve.tensor_tensor(pos[:, n2.ring(2), t, :], pos_ps[t][:, 0:PITCH],
                                                  r_rows[:, n2.p, first:first + PITCH], ALU.add)
                        i.then_inc(s["pos"], 1)
                    if ended:
                        wait(dve, s["y_mm"], b3)
                        residual(b3, "bias")
                    if ended:
                        residual(b3, "gate")

                walk(dve, PER, 2, LEAD, LAG, step)


def ffn1(nc, d, k):
    phase, PER, E = 3, 8, 8
    n = k.norms
    w = weights(k, phase)
    LOWEST = -3e38
    with ExitStack() as ctx:
        def sb(name, shape):
            return ctx.enter_context(nc.sbuf_tensor("f1_" + name, shape, F32))

        silu = sb("silu", [P, 2, 2 * T])
        hidden = sb("hidden", [P, 2, 2 * T])
        acc = sb("acc", [P, 2, NT, P])
        logits = sb("logits", [P, NT, 2 * E])
        max8 = sb("max8", [P, NT, 8])
        top = sb("top", [P, 2, NT, 8])
        rest = sb("rest", [P, 2, NT, 2 * E])
        is_top = sb("is_top", [P, 2, NT, E])
        gap = sb("gap", [P, NT])
        tilt = sb("tilt", [P, NT])
        second = sb("second", [P, NT])
        part = sb("part", [P, NT, E])
        cw = sb("cw", [P, 2, NT, E])
        w12 = ctx.enter_context(nc.sbuf_tensor("f1_w12", [P, E, 2, 2 * T], F32R))
        h1_ps, h2_ps, y_ps = k.banks[0:2], k.banks[2:4], k.banks[4:6]
        ht_ps, rt_ps = k.banks[6:8]
        names = ("chain", "var", "std", "rstd", "xn", "ht_mm", "ht", "ht_rounded", "ht_cut", "w_rounded", "w_cut", "rt_mm", "logits", "gap", "tilt", "top", "cw",
                 "h1_mm", "h2_mm", "silu", "hidden", "y_mm", "acc", "weighted", "added", "pads")
        s = signals(nc, ctx, "f1_", names)
        LAST, LEAD, LAG = PER - 1, 8, 2

        with nc.Block() as block:

            @block.sync
            def _(sp):
                prefetch(sp, nc, k, d, phase)

            @block.gpsimd
            def _(pool):
                pool.wait_ge(k.gate_in[phase], 16)

                def step(at):
                    ni = at.shift(PER)
                    if at.real and at.p == LAST:
                        residual_by_pool(pool, n, at, acc[:, at.s // PER % 2], k.gate[phase % 2], s["acc"], 2,
                                         s["weighted"], s["added"])
                    if at.p == 2 and ni.real:
                        cut_hT_rest(pool, n, ni, s["ht_rounded"], s["ht_cut"])

                walk(pool, PER, 2, LEAD, LAG, step)

            @block.scalar
            def _(act):
                std_of_rows(act, n, s["var"], s["std"])
                act.wait_ge(k.weights_in[phase], 16 * len(WEIGHTS[phase]))
                for e in range(E):
                    act.copy(w12[:, e, 0, :], w["w12"][:, e, :]).then_inc(s["w_rounded"], 1)

                def step(at):
                    nx, ni = at.shift(1), at.shift(PER)
                    if nx.real:
                        wait(act, s["h1_mm"], nx)
                        wait(act, s["hidden"], nx.shift(-2))
                        act.activation(silu[:, nx.ring(2), :], h1_ps[nx.ring(2)][:], ACT.Silu).then_inc(s["silu"], 1)
                    if at.p == 2 and ni.real:
                        wait(act, s["ht_mm"], ni, item=True)
                        wait(act, s["h2_mm"], at.shift(-3))
                        modulated(act, k, phase, ni, ht_ps[:, 0:T], n.hT[:, (at.s // PER + 1) % 2, :], s["ht"])
                        cut_hT(act, n, ni, s["ht"], s["ht_rounded"])
                    if at.p == 4 and ni.real:
                        wait(act, s["gap"], ni, item=True)
                        act.activation(tilt[:], gap[:], ACT.Tanh, scale=0.5).then_inc(s["tilt"], 1)

                walk(act, PER, 2, LEAD, LAG, step)

            @block.tensor
            def _(pe):
                pe.wait_ge(k.weights_in[phase], 16 * len(WEIGHTS[phase]))

                def step(at):
                    nx, ni = at.shift(1), at.shift(PER)
                    if nx.real:
                        if nx.p == 0:
                            wait(pe, s["ht_cut"], nx, item=True)
                        if isinstance(at.base, int) and nx.s < E:
                            pe.wait_ge(s["w_cut"], nx.s + 1)
                        hT = [n.hT2[:, nx.s // PER % 2, part, :] for part in range(2)]

                        def cols(c):
                            return [w12[:, nx.p, part, c * P:(c + 1) * P] for part in range(2)]

                        wait(pe, s["silu"], nx.shift(-2))
                        for c in range(2):
                            mm = matmul3(pe, h1_ps[nx.ring(2)][:, c * T:(c + 1) * T], cols(c), hT)
                        mm.then_inc(s["h1_mm"], 1)
                        wait(pe, s["hidden"], nx.shift(-2))
                        for c in range(2):
                            mm = matmul3(pe, h2_ps[nx.ring(2)][:, c * T:(c + 1) * T], cols(2 + c), hT)
                        mm.then_inc(s["h2_mm"], 1)
                    if at.p == 1 and ni.real:
                        wait(pe, s["xn"], ni, item=True)
                        wait(pe, s["ht"], ni.shift(-PER), item=True)
                        for t in range(NT):
                            mm = pe.transpose(ht_ps[:, t * P:(t + 1) * P], n.xn[:, t, :], k.ident[:])
                        mm.then_inc(s["ht_mm"], 1)
                    if at.p == 3 and ni.real:
                        wait(pe, s["ht"], ni, item=True)
                        wait(pe, s["logits"], ni.shift(-PER), item=True)
                        for t in range(NT):
                            mm = pe.matmul(rt_ps[:, t * E:(t + 1) * E],
                                           n.hT[:, (at.s // PER + 1) % 2, t * P:(t + 1) * P], w["gw1"][:],
                                           start=True, stop=True)
                        mm.then_inc(s["rt_mm"], 1)
                    if at.real:
                        wait(pe, s["hidden"], at)
                        wait(pe, s["acc"], at.shift(-2), 2)
                        for t in range(NT):
                            for c in range(2):
                                mm = pe.matmul(y_ps[at.ring(2)][:, t * P:(t + 1) * P],
                                               hidden[:, at.ring(2), c * T + t * P:c * T + (t + 1) * P],
                                               w["w3"][:, at.p, c, :], start=(c == 0), stop=(c == 1))
                        mm.then_inc(s["y_mm"], 1)

                walk(pe, PER, 2, LEAD, LAG, step)

            @block.vector
            def _(dve):
                start_norms(dve, n, s)
                dve.memset(logits[:], LOWEST)
                dve.memset(top[:], LOWEST).then_inc(s["pads"], 1)
                dve.wait_ge(s["pads"], 1)
                for e in range(E):
                    dve.wait_ge(s["w_rounded"], e + 1)
                    dve.tensor_tensor(w12[:, e, 1, :], w["w12"][:, e, :], w12[:, e, 0, :], ALU.subtract
                                      ).then_inc(s["w_cut"], 1)
                dve.wait_ge(k.gate_in[phase], 16)

                def step(at):
                    nx, ni = at.shift(1), at.shift(PER)
                    if at.p == 0 and ni.real:
                        normalise(dve, n, ni, s["ht_mm"], s["xn"])
                    if nx.real:
                        wait(dve, s["silu"], nx)
                        wait(dve, s["h2_mm"], nx)
                        wait(dve, s["y_mm"], nx.shift(-2))
                        dve.tensor_tensor(hidden[:, nx.ring(2), :], silu[:, nx.ring(2), :], h2_ps[nx.ring(2)][:],
                                          ALU.mult).then_inc(s["hidden"], 1)
                    steps = ni.item * 4

                    def link(i, m):
                        i.then_inc(s["top"], 1)
                        dve.wait_ge(s["top"], steps + m)

                    if at.p == 3 and ni.real:
                        wait(dve, s["rt_mm"], ni, item=True)
                        dve.tensor_copy(logits[:, :, 0:E], rt_ps[:, 0:NT * E].rearrange("p (t e) -> p t e", t=NT)
                                        ).then_inc(s["logits"], 1)
                        wait(dve, s["logits"], ni, item=True)
                        hold(dve, k.spare)
                        for t in range(NT):
                            i = dve.max(max8[:, t, :], logits[:, t, :])
                        link(i, 1)
                        dve.tensor_tensor(gap[:], max8[:, :, 0], max8[:, :, 1], ALU.subtract).then_inc(s["gap"], 1)
                        dve.tensor_copy(top[:, 0, :, 0:1], max8[:, :, 0:1])
                        link(dve.tensor_copy(top[:, 1, :, 0:2], max8[:, :, 0:2]), 2)
                        hold(dve, k.spare)
                        for m in range(2):
                            for t in range(NT):
                                i = dve.match_replace(rest[:, m, t, :], top[:, m, t, :], logits[:, t, :], LOWEST)
                        link(i, 3)
                    if at.p == 5 and ni.real:
                        wait(dve, s["tilt"], ni, item=True)
                        for m in range(2):
                            dve.tensor_tensor(is_top[:, m], rest[:, m, :, 0:E], logits[:, :, 0:E], ALU.not_equal)
                        link(dve.tensor_scalar(second[:], tilt[:], -0.5, 0.5, ALU.mult, ALU.add), 4)
                        wait(dve, s["acc"], Step(at.base, at.s - at.p - 1, PER), 2)
                        for t in range(NT):
                            i = dve.tensor_scalar(part[:, t, :], is_top[:, 1, t, :], second[:, t:t + 1], None, ALU.mult)
                        i.then_inc(s["cw"], 1)
                        dve.wait_ge(s["cw"], 2 * ni.item + 1)
                        for t in range(NT):
                            i = dve.scalar_tensor_tensor(out=cw[:, (at.s // PER + 1) % 2, t, :], in0=is_top[:, 0, t, :],
                                                         scalar=tilt[:, t:t + 1], in1=part[:, t, :], op0=ALU.mult,
                                                         op1=ALU.add)
                        i.then_inc(s["cw"], 1)
                    if at.real:
                        wait(dve, s["y_mm"], at)
                        place = at.s // PER % 2
                        c = cw[:, at.s // PER % 2]
                        if at.p == 0:
                            wait(dve, s["cw"], at, 2, item=True)
                            wait(dve, s["weighted"], at.shift(-2 * PER), item=True)
                        for t in range(NT):
                            a, z = acc[:, place, t, :], y_ps[at.ring(2)][:, t * P:(t + 1) * P]
                            wait(dve, s["acc"], at.shift(-1), 2, 1 - t)
                            if at.p == 0:
                                i = dve.tensor_scalar(a, z, c[:, t, 0:1], None, ALU.mult)
                            else:
                                i = dve.scalar_tensor_tensor(out=a, in0=z, scalar=c[:, t, at.p:at.p + 1], in1=a,
                                                             op0=ALU.mult, op1=ALU.add)
                            i.then_inc(s["acc"], 1)
                    if at.p == 1 and at.shift(-2).real:
                        row_stats(dve, n, at.shift(-2), s["added"])

                walk(dve, PER, 2, LEAD, LAG, step)


def rope_attention(nc, d, k, phase):
    PER, H, DH, PARTS = 8, 16, 8, 3
    ROWS = DH * sum(PARTS - a for a in range(PARTS))
    n = k.norms
    w = weights(k, phase)
    for name in list(w):
        w[name[:-1]] = w[name]
    C = 3 * P
    with ExitStack() as ctx:
        def sb(name, shape):
            return ctx.enter_context(nc.sbuf_tensor(f"a{phase}_{name}", shape, F32))

        terms = sb("terms", [P, 2, 2, T])
        rotated = sb("rotated", [P, 2, T])
        rest = sb("rest", [P, 2, T])
        cut = ctx.enter_context(nc.sbuf_tensor(f"a{phase}_cut", [P, PARTS, 2, T], BF16))
        stack = ctx.enter_context(nc.sbuf_tensor(f"a{phase}_stack", [ROWS, 2, 2, H, T], BF16))
        v = sb("v", [P, 2, NT, H, 32])
        p = sb("p", [P, 2, 2, C])
        pT = sb("pT", [P, 2, 2, C])
        o = sb("o", [P, T])
        oT = sb("oT", [P, T])
        nmax = sb("nmax", [P, 2, 2, NT])
        sums = sb("sums", [P, 2, NT, H])
        rec = sb("rec", [P, NT, H])
        recT = sb("recT", [H, T])
        scale = sb("scale", [P, T])
        cut_dram = nc.dram_tensor(f"cut_dram{phase}", (2, PARTS, 2, DH * H, T), BF16, kind="Internal").ap()
        misc_ps, o_ps = k.banks[0:2]
        s_ps, pT_ps = (k.banks[2:4], k.banks[4:6]), k.banks[6:8]
        names = ("chain", "var", "std", "rstd", "xn", "ht_mm", "ht", "q_mm", "q_terms", "k_mm", "k_terms", "cut",
                 "written_q", "written_k", "stacked0", "stacked1", "v_mm", "v", "s_mm", "nmax", "exp", "pT_mm", "pT0", "pT1", "o_mm", "o",
                 "rec", "recT_mm", "recT", "scale_mm", "scale", "oT", "y_mm", "res", "v0")
        s = signals(nc, ctx, f"a{phase}_", names)
        stacked, written = [s["stacked0"], s["stacked1"]], [s["written_q"], s["written_k"]]
        LEAD, LAG = 2 * PER - 3, 8

        def place(at):
            return at.s // PER % 2

        def diagonal(at, t):
            whole = v[:, place(at), t]
            return bass.AP(whole.tensor, whole.offset, [list(whole.ap[0]), [4 * 32, 4], [32 + DH, 4], [1, DH]])

        with nc.Block() as block:

            @block.sync
            def _(sp):
                prefetch(sp, nc, k, d, phase)
                ROW = H * DH * T

                def step(at):
                    ni = at.shift(PER)
                    for which in range(2):
                        if at.p == 1 + 2 * which and ni.real:
                            wait(sp, s["cut"], ni, 10, 5 - 5 * which, item=True)
                            sp.dma_start(cut_dram[place(ni), :, which].rearrange("a r t -> r a t"), cut[:, :, which]
                                         ).then_inc(written[which], 16)
                        if at.p == 2 + 2 * which and ni.real:
                            wait(sp, written[which], ni, 16, item=True)
                            row = 0
                            for a in range(PARTS):
                                rows = (PARTS - a) * DH
                                start = (place(ni) * PARTS * 2 + (1 if which else 2 * a)) * ROW
                                src = bass.AP(cut_dram.tensor, start,
                                              [[2 * ROW if which else 0, PARTS - a], [H * T, DH], [1, H * T]])
                                sp.dma_start(stack[row:row + rows, place(ni), which].rearrange("r h t -> r (h t)"), src
                                             ).then_inc(stacked[place(ni)], 16)
                                row += rows

                walk(sp, PER, 2, LEAD, LAG, step)

            @block.gpsimd
            def _(pool):
                def cut_up(which, at, terms_ready):
                    def link(i, m):
                        i.then_inc(s["cut"], 1)
                        if m < 5:
                            pool.wait_ge(s["cut"], at.item * 10 + 5 * which + m)

                    wait(pool, terms_ready, at, item=True)
                    wait(pool, written[which], at.shift(-PER), 16, item=True)
                    x, y, c = terms[:, which, 0, :], terms[:, which, 1, :], cut[:, :, which, :]
                    link(pool.tensor_tensor(c[:, 0], x, y, ALU.add), 1)
                    link(pool.tensor_tensor(rotated[:, which], x, y, ALU.add), 2)
                    link(pool.tensor_tensor(rest[:, which], rotated[:, which], c[:, 0], ALU.subtract), 3)
                    link(pool.tensor_tensor(c[:, 1], rotated[:, which], c[:, 0], ALU.subtract), 4)
                    link(pool.tensor_tensor(c[:, 2], rest[:, which], c[:, 1], ALU.subtract), 5)

                def step(at):
                    ni, pi, ni2 = at.shift(PER), at.shift(-PER), at.shift(2 * PER)
                    if at.p == 7 and ni2.real:
                        cut_up(0, ni2, s["q_terms"])
                    if at.p == 0 and ni.real:
                        cut_up(1, ni, s["k_terms"])
                    if at.p == 5 and pi.real:
                        wait(pool, s["o"], pi, item=True)
                        wait(pool, s["scale"], pi, item=True)
                        wait(pool, s["y_mm"], pi.shift(-PER), item=True)
                        pool.tensor_tensor(oT[:], o[:], scale[:], ALU.mult).then_inc(s["oT"], 1)

                walk(pool, PER, 2, LEAD, LAG, step)

            @block.scalar
            def _(act):
                std_of_rows(act, n, s["var"], s["std"])
                act.wait_ge(s["v0"], 1)

                def step(at):
                    b1, ni, ni2, pi = at.shift(-1), at.shift(PER), at.shift(2 * PER), at.shift(-PER)
                    def exps(h):
                        r, head = at.ring(2), at.p + 8 * h
                        wait(act, s["nmax"], at, 2, 1 - h)
                        for t in range(NT):
                            c = slice(0, P) if t == 0 else slice(P, C)
                            i = act.activation(p[:, r, h, c], s_ps[at.ring(2)][h][:, c], ACT.Exp,
                                               bias=nmax[:, r, h, t:t + 1],
                                               accum_out=sums[:, place(at), t, head:head + 1])
                        i.then_inc(s["exp"], 1)

                    if at.real:
                        if at.p == 0:
                            wait(act, s["rec"], at.shift(-2 * PER), item=True)
                        wait(act, s["pT_mm"], at.shift(-2), 2)
                        exps(0)
                    if b1.real:
                        wait(act, s["pT_mm"], b1, 2)
                        wait(act, s["o_mm"], b1.shift(-2))
                        act.copy(pT[:, b1.ring(2), 1, :], pT_ps[1][:, 0:C]).then_inc(s["pT1"], 1)
                    if at.p == 3 and pi.real:
                        wait(act, s["recT_mm"], pi, item=True)
                        wait(act, s["scale_mm"], pi.shift(-PER), item=True)
                        act.copy(recT[:], misc_ps[0:H, 0:T]).then_inc(s["recT"], 1)
                    if at.p == 4 and pi.real:
                        wait(act, s["scale_mm"], pi, item=True)
                        wait(act, s["oT"], pi.shift(-PER), item=True)
                        act.copy(scale[:], misc_ps[:, T:2 * T]).then_inc(s["scale"], 1)
                    if at.p == 2 and ni.real:
                        wait(act, s["v_mm"], ni, item=True)
                        for t in range(NT):
                            i = act.copy(diagonal(ni, t),
                                         misc_ps[:, t * P:(t + 1) * P].rearrange("p (g r c) -> p g r c", g=4, r=4))
                        i.then_inc(s["v"], 1)
                    if at.p == 5 and ni2.real:
                        wait(act, s["ht_mm"], ni2, item=True)
                        wait(act, s["v_mm"], ni, item=True)
                        modulated(act, k, phase, ni2, misc_ps[:, T:2 * T], n.hT[:, 0, :], s["ht"])
                    if at.real:
                        exps(1)

                walk(act, PER, 2, LEAD, LAG, step)

            @block.tensor
            def _(pe):
                pe.wait_ge(k.weights_in[phase], 16 * len(WEIGHTS[phase]))

                def projections(at, which, sem):
                    for c in range(2):
                        mm = pe.matmul(misc_ps[:, c * T:(c + 1) * T], w["wqk"][:, 2 * which + c, :], n.hT[:, 0, :],
                                       start=True, stop=True)
                    mm.then_inc(sem, 1)

                def step(at):
                    b1, b2, ni, pi = at.shift(-1), at.shift(-2), at.shift(PER), at.shift(-PER)
                    ni2, n1 = at.shift(2 * PER), at.shift(1)
                    if n1.real and n1.p == 0:
                        i = n1.s // PER
                        pe.wait_ge(stacked[i % 2], at.base * (2 * PARTS * 16 // 2) + (i // 2 + 1) * (2 * PARTS * 16))
                    for h in range(2):
                        if b1.real:
                            wait(pe, s[("pT0", "pT1")[h]], b1.shift(-1))
                            wait(pe, s["exp"], b1, 2, 1 - h)
                            causal_transposes(pe, pT_ps[h], p[:, b1.ring(2), h, :], k.ident[:]).then_inc(s["pT_mm"], 1)
                        if n1.real:
                            q, keys = (stack[:, place(n1), which, n1.p + 8 * h, :] for which in range(2))
                            bank = s_ps[n1.ring(2)][h]
                            wait(pe, s["exp"], n1.shift(-2), 2, 1 - h)
                            pe.matmul(bank[:, 0:P], q[:, 0:P], keys[:, 0:P], start=True, stop=False,
                                      skip_group_check=True)
                            pe.matmul(bank[:, P:C], q[:, P:T], keys, start=False, stop=False,
                                      skip_group_check=True)
                            for c in (0, 2 * P):
                                mm = pe.matmul(bank[:, c:c + P], k.ident_bf[:], k.causal_bf[:], start=False,
                                               stop=True, skip_group_check=True)
                            mm.then_inc(s["s_mm"], 1)
                    if b2.real:
                        wait(pe, s["pT0"], b2)
                        wait(pe, s["pT1"], b2)
                        if b2.p == 0:
                            wait(pe, s["v"], b2, item=True)
                            wait(pe, s["o"], b2.shift(-PER), item=True)
                        for j in range(NT):
                            for h in range(2):
                                head = b2.p + 8 * h
                                g = head // 4 * 32
                                mm = pe.matmul(o_ps[g:g + 32, j * P:T], v[:, place(b2), j, head, :],
                                               pT[:, b2.ring(2), h, 0:T] if j == 0 else pT[:, b2.ring(2), h, T:C],
                                               start=(j == 0 and head % 4 == 0), stop=(j == 1 and head % 4 == 3),
                                               skip_group_check=True)
                        mm.then_inc(s["o_mm"], 1)
                    if at.p == 1 and ni.real:
                        wait(pe, s["k_terms"], ni, item=True)
                        for t in range(NT):
                            mm = pe.matmul(misc_ps[:, t * P:(t + 1) * P], n.hT[:, 0, t * P:(t + 1) * P], w["wv"][:],
                                           start=True, stop=True)
                        mm.then_inc(s["v_mm"], 1)
                    if at.p == 2 and pi.real:
                        wait(pe, s["v"], ni, item=True)
                        wait(pe, s["rec"], pi, item=True)
                        wait(pe, s["res"], pi.shift(-PER), item=True)
                        for t in range(NT):
                            mm = pe.transpose(misc_ps[0:H, t * P:(t + 1) * P], rec[:, t, :], k.ident[:])
                        mm.then_inc(s["recT_mm"], 1)
                    if at.p == 3 and pi.real:
                        wait(pe, s["recT"], pi, item=True)
                        pe.matmul(misc_ps[:, T:2 * T], w["head_rows"][:], recT[:], start=True, stop=True
                                  ).then_inc(s["scale_mm"], 1)
                    if at.p == 4 and ni2.real:
                        wait(pe, s["xn"], ni2, item=True)
                        wait(pe, s["scale"], pi, item=True)
                        wait(pe, s["v"], ni, item=True)
                        for t in range(NT):
                            mm = pe.transpose(misc_ps[:, T + t * P:T + (t + 1) * P], n.xn[:, t, :], k.ident[:])
                        mm.then_inc(s["ht_mm"], 1)
                    if at.p == 5 and pi.real:
                        wait(pe, s["oT"], pi, item=True)
                        wait(pe, s["ht"], ni2, item=True)
                        for t in range(NT):
                            mm = pe.matmul(misc_ps[:, t * P:(t + 1) * P], oT[:, t * P:(t + 1) * P], w["wproj"][:],
                                           start=True, stop=True)
                        mm.then_inc(s["y_mm"], 1)
                    if at.p == 6 and ni2.real:
                        wait(pe, s["ht"], ni2, item=True)
                        if pi.real:
                            pe.wait_ge(s["chain"], pi.item * 2 + 3)
                        projections(ni2, 0, s["q_mm"])
                    if at.p == 7 and ni2.real:
                        wait(pe, s["q_terms"], ni2, item=True)
                        projections(ni2, 1, s["k_mm"])

                walk(pe, PER, 2, LEAD, LAG, step)

            @block.vector
            def _(dve):
                start_norms(dve, n, s)
                dve.memset(v[:], 0.0).then_inc(s["v0"], 1)
                dve.wait_ge(k.weights_in[phase], 16 * len(WEIGHTS[phase]))
                dve.wait_ge(k.gate_in[phase], 16)

                def rotation_terms(which, at, mm, table, done):
                    wait(dve, mm, at, item=True)
                    wait(dve, s["cut"], at.shift(-PER), 10, 5 - 5 * which, item=True)
                    dve.tensor_tensor(terms[:, which], misc_ps[:].rearrange("p (c t) -> p c t", c=2), table, ALU.mult
                                      ).then_inc(done, 1)

                def residual(item, part):
                    return add_residual(dve, n, item, misc_ps[:, 0:T].rearrange("p (t d) -> p t d", t=NT),
                                        k.gate[phase % 2], None, s["chain"], 2, (part,))

                def step(at):
                    b1, ni, pi, ni2 = at.shift(-1), at.shift(PER), at.shift(-PER), at.shift(2 * PER)
                    if at.real:
                        for h in range(2):
                            wait(dve, s["s_mm"], at, 2, 1 - h)
                            wait(dve, s["exp"], at.shift(-2), 2)
                            for t in range(NT):
                                i = dve.tensor_reduce(nmax[:, at.ring(2), h, t:t + 1],
                                                      s_ps[at.ring(2)][h][:, 0:P] if t == 0 else s_ps[at.ring(2)][h][:, P:C], AX_X, ALU.max,
                                                      negate=True)
                            i.then_inc(s["nmax"], 1)
                    if at.p == 0 and pi.real:
                        wait(dve, s["exp"], at.shift(-1), 2)
                        wait(dve, s["recT_mm"], pi.shift(-PER), item=True)
                        dve.reciprocal(rec[:], sums[:, (at.s // PER + 1) % 2]).then_inc(s["rec"], 1)
                    if at.p == 2 and pi.real:
                        wait(dve, s["o_mm"], at.shift(-3))
                        wait(dve, s["oT"], pi.shift(-PER), item=True)
                        dve.tensor_copy(o[:], o_ps[:, 0:T]).then_inc(s["o"], 1)
                    if at.p == 6 and pi.real:
                        wait(dve, s["y_mm"], pi, item=True)
                        residual(pi, "gate")
                    if at.p == 7 and pi.real:
                        residual(pi, "add")
                        residual(pi, "stats").then_inc(s["res"], 1)
                    if at.p == 3 and ni2.real:
                        normalise(dve, n, ni2, s["ht_mm"], s["xn"])
                    if at.p == 7 and ni2.real:
                        rotation_terms(0, ni2, s["q_mm"], w["rope_q"], s["q_terms"])
                    if at.p == 0 and ni.real:
                        rotation_terms(1, ni, s["k_mm"], w["rope_k"], s["k_terms"])
                    if b1.real:
                        wait(dve, s["pT_mm"], b1, 2, 1)
                        wait(dve, s["o_mm"], b1.shift(-2))
                        dve.tensor_copy(pT[:, b1.ring(2), 0, :], pT_ps[0][:, 0:C]).then_inc(s["pT0"], 1)

                walk(dve, PER, 2, LEAD, LAG, step)


def attention2(nc, d, k):
    rope_attention(nc, d, k, 4)


def attention3(nc, d, k):
    rope_attention(nc, d, k, 6)


CAT = 2 * 512 + 4 + P


def ffn2(nc, d, k):
    phase, PER, E = 5, 4, 8
    n = k.norms
    w = weights(k, phase)
    with ExitStack() as ctx:
        def sb(name, shape):
            return ctx.enter_context(nc.sbuf_tensor("f2_" + name, shape, F32))

        merged = sb("merged", [P, 2, CAT])
        hT = sb("hT", [P, 4, T])
        uT = sb("uT", [P, 2, T])
        gate_hidden = sb("gate_hidden", [P, T])
        hidden_sum = sb("hidden_sum", [P, 1])
        sum_cols = sb("sum_cols", [P, P])
        g = sb("g", [P, 2, E])
        biased = sb("biased", [P, 2, NT, P])
        ht_ps, gh_ps, g_ps, u_ps, y_ps = k.banks[0], k.banks[1], k.banks[2], k.banks[3:5], k.banks[5]
        names = ("chain", "var", "std", "rstd", "xn", "ht_mm", "ht", "gh_mm", "sum", "cols", "g_mm", "g", "merge",
                 "u_mm", "u", "y_mm", "biased", "weighted", "added")
        s = signals(nc, ctx, "f2_", names)
        LEAD, LAG = 8, 2

        with nc.Block() as block:

            @block.sync
            def _(sp):
                prefetch(sp, nc, k, d, phase)

            @block.gpsimd
            def _(pool):
                pool.wait_ge(k.gate_in[phase], 16)

                def step(at):
                    if at.real and at.p == 3:
                        residual_by_pool(pool, n, at, biased[:, at.s // PER % 2], k.gate[phase % 2], s["biased"], 1,
                                         s["weighted"], s["added"], item=True)

                walk(pool, PER, 4, LEAD, LAG, step)

            @block.scalar
            def _(act):
                std_of_rows(act, n, s["var"], s["std"])
                act.wait_ge(k.weights_in[phase], 16 * len(WEIGHTS[phase]))

                def step(at):
                    i2 = at.shift(2 * PER)
                    if at.real:
                        wait(act, s["u_mm"], at)
                        wait(act, s["y_mm"], at.shift(-2))
                        c = 2 * 512 + at.p
                        act.activation(uT[:, at.ring(2), :], u_ps[at.ring(2)][:, 0:T], ACT.Gelu_apprx_tanh,
                                       bias=merged[:, at.s // PER % 2, c:c + 1]).then_inc(s["u"], 1)
                    if at.p == 1 and i2.real:
                        wait(act, s["ht_mm"], i2, item=True)
                        wait(act, s["u_mm"], at.shift(-6))
                        modulated(act, k, phase, i2, ht_ps[:, 0:T], hT[:, i2.s // PER % 4, :], s["ht"])
                    if at.p == 2 and i2.real:
                        wait(act, s["gh_mm"], i2, item=True)
                        act.activation(gate_hidden[:], gh_ps[:, 0:T], ACT.Relu, bias=w["gb1"][:, 0:1],
                                       accum_out=hidden_sum[:]).then_inc(s["sum"], 1)
                        wait(act, s["sum"], i2, item=True)
                        wait(act, s["g_mm"], i2.shift(-PER), item=True)
                        act.activation(sum_cols[:], k.ident[:], ACT.Identity, scale=0.0, bias=hidden_sum[:, 0:1]
                                       ).then_inc(s["cols"], 1)

                walk(act, PER, 4, LEAD, LAG, step)

            @block.tensor
            def _(pe):
                pe.wait_ge(k.weights_in[phase], 16 * len(WEIGHTS[phase]))

                def step(at):
                    b1, i2 = at.shift(-1), at.shift(2 * PER)
                    if b1.real:
                        wait(pe, s["u"], b1)
                        if b1.p == 0:
                            wait(pe, s["biased"], b1.shift(-PER), item=True)
                        for t in range(NT):
                            mm = pe.matmul(y_ps[:, t * P:(t + 1) * P], uT[:, b1.ring(2), t * P:(t + 1) * P],
                                           merged[:, b1.s // PER % 2, 512 + b1.p * P:512 + (b1.p + 1) * P],
                                           start=(b1.p == 0 and t == 0), stop=(b1.p == PER - 1),
                                           skip_group_check=True)
                        mm.then_inc(s["y_mm"], 1)
                    if at.p == 1 and i2.real:
                        wait(pe, s["xn"], i2, item=True)
                        wait(pe, s["ht"], i2.shift(-PER), item=True)
                        for t in range(NT):
                            mm = pe.transpose(ht_ps[:, t * P:(t + 1) * P], n.xn[:, t, :], k.ident[:])
                        mm.then_inc(s["ht_mm"], 1)
                    if at.p == 2 and i2.real:
                        wait(pe, s["ht"], i2, item=True)
                        wait(pe, s["sum"], i2.shift(-PER), item=True)
                        pe.matmul(gh_ps[:, 0:T], w["gw1_2"][:], hT[:, i2.s // PER % 4, :], start=True, stop=True
                                  ).then_inc(s["gh_mm"], 1)
                    if at.p == 3 and i2.real:
                        wait(pe, s["cols"], i2, item=True)
                        wait(pe, s["g"], i2.shift(-PER), item=True)
                        pe.matmul(g_ps[:, 0:E], sum_cols[:], w["gw2"][:], start=True, stop=True).then_inc(s["g_mm"], 1)
                    if at.real:
                        wait(pe, s["merge"], at, E, item=True)
                        wait(pe, s["u"], at.shift(-2))
                        pe.matmul(u_ps[at.ring(2)][:, 0:T], merged[:, at.s // PER % 2, at.p * P:(at.p + 1) * P],
                                  hT[:, at.s // PER % 4, :], start=True, stop=True).then_inc(s["u_mm"], 1)

                walk(pe, PER, 4, LEAD, LAG, step)

            @block.vector
            def _(dve):
                start_norms(dve, n, s)
                dve.wait_ge(k.weights_in[phase], 16 * len(WEIGHTS[phase]))
                dve.wait_ge(k.gate_in[phase], 16)

                def step(at):
                    ni, i2 = at.shift(PER), at.shift(2 * PER)
                    if at.p == 0 and i2.real:
                        normalise(dve, n, i2, s["ht_mm"], s["xn"])
                    if ni.real:
                        if ni.p == 0:
                            wait(dve, s["g"], Step(ni.base, ni.s, PER), item=True)
                            wait(dve, s["y_mm"], at.shift(-PER + 3))
                            wait(dve, s["biased"], at.shift(-PER), item=True)
                        m = merged[:, ni.s // PER % 2, :]
                        for e in (2 * ni.p, 2 * ni.p + 1):
                            if e:
                                dve.wait_ge(s["merge"], ni.item * E + e)
                            dve.scalar_tensor_tensor(out=m, in0=w["task"][:, e, :], scalar=g[:, ni.s // PER % 2, e:e + 1],
                                                     in1=m if e else w["base"][:], op0=ALU.mult, op1=ALU.add
                                                     ).then_inc(s["merge"], 1)
                    if at.p == 3 and i2.real:
                        wait(dve, s["g_mm"], i2, item=True)
                        wait(dve, s["merge"], i2.shift(-2 * PER), E, item=True)
                        dve.scalar_tensor_tensor(out=g[:, i2.s // PER % 2, :], in0=g_ps[:, 0:E], scalar=1.0 / T,
                                                 in1=w["gb2"][:], op0=ALU.mult, op1=ALU.add).then_inc(s["g"], 1)
                    if at.p == 3 and at.real:
                        wait(dve, s["y_mm"], at)
                        wait(dve, s["weighted"], at.shift(-2 * PER), item=True)
                        dve.tensor_tensor(biased[:, at.s // PER % 2], y_ps[:, 0:T].rearrange("p (t d) -> p t d", t=NT),
                                          merged[:, at.s // PER % 2, CAT - P:CAT].unsqueeze(1).to_broadcast([P, NT, P]),
                                          ALU.add).then_inc(s["biased"], 1)
                    if at.p == 1 and at.shift(-2).real:
                        row_stats(dve, n, at.shift(-2), s["added"])

                walk(dve, PER, 4, LEAD, LAG, step)


def ffn3(nc, d, k):
    phase, PER, E, K = 7, 5, 8, 6
    n = k.norms
    w = weights(k, phase)
    with ExitStack() as ctx:
        def sb(name, shape):
            return ctx.enter_context(nc.sbuf_tensor("f3_" + name, shape, F32))

        tanh = sb("tanh", [P, 2, T])
        gated = sb("gated", [P, 2, T])
        hidden = sb("hidden", [P, 2, T])
        acc = sb("acc", [P, 2, NT, P])
        b = router_tiles(nc, ctx, "f3_", E)
        gu_ps, y_ps = k.banks[0:2], k.banks[2:4]
        ht_ps, rt_ps = k.banks[4], k.banks[5]
        names = ("chain", "var", "std", "rstd", "xn", "ht_mm", "ht", "rt_mm", "nmax", "rexp", "top", "cw", "cwT_mm",
                 "gu_mm", "tanh", "gated", "hidden", "y_mm", "acc", "weighted", "added", "pads")
        s = signals(nc, ctx, "f3_", names)
        LAST, LEAD, LAG = PER - 1, 5, 2

        with nc.Block() as block:

            @block.gpsimd
            def _(pool):
                pool.wait_ge(k.gate_in[phase], 16)

                def step(at):
                    if at.real and at.p == LAST:
                        residual_by_pool(pool, n, at, acc[:, at.s // PER % 2], k.gate[phase % 2], s["acc"], 4,
                                         s["weighted"], s["added"])

                walk(pool, PER, 2, LEAD, LAG, step)

            @block.scalar
            def _(act):
                std_of_rows(act, n, s["var"], s["std"])

                def step(at):
                    nx, ni = at.shift(1), at.shift(PER)
                    if nx.real:
                        wait(act, s["gu_mm"], nx)
                        wait(act, s["gated"], nx.shift(-2))
                        act.activation(tanh[:, nx.ring(2), :], gu_ps[nx.ring(2)][:, 0:T], ACT.Tanh, scale=0.5
                                       ).then_inc(s["tanh"], 1)
                    if at.p == 1 and ni.real:
                        wait(act, s["ht_mm"], ni, item=True)
                        wait(act, s["gu_mm"], at.shift(-2))
                        modulated(act, k, phase, ni, ht_ps[:, 0:T], n.hT[:, (at.s // PER + 1) % 2, :], s["ht"])
                    if at.p == 2 and ni.real:
                        wait(act, s["nmax"], ni, item=True)
                        wait(act, s["top"], ni.shift(-PER), 5, item=True)
                        for t in range(NT):
                            i = act.activation(b["e"][:, t, :], rt_ps[:, t * E:(t + 1) * E], ACT.Exp,
                                               bias=b["nmax"][:, t:t + 1], accum_out=b["sums"][:, t:t + 1])
                        i.then_inc(s["rexp"], 1)

                walk(act, PER, 2, LEAD, LAG, step)

            @block.tensor
            def _(pe):
                pe.wait_ge(k.weights_in[phase], 16 * len(WEIGHTS[phase]))

                def step(at):
                    nx, ni = at.shift(1), at.shift(PER)
                    if nx.real:
                        if nx.p == 0:
                            wait(pe, s["ht"], nx, item=True)
                        wait(pe, s["hidden"], nx.shift(-2))
                        for c in range(2):
                            mm = pe.matmul(gu_ps[nx.ring(2)][:, c * T:(c + 1) * T], w["gu"][:, nx.p, c, :],
                                           n.hT[:, nx.s // PER % 2, :], start=True, stop=True)
                        mm.then_inc(s["gu_mm"], 1)
                    if at.p == 1 and ni.real:
                        wait(pe, s["xn"], ni, item=True)
                        wait(pe, s["ht"], ni.shift(-PER), item=True)
                        for t in range(NT):
                            mm = pe.transpose(ht_ps[:, t * P:(t + 1) * P], n.xn[:, t, :], k.ident[:])
                        mm.then_inc(s["ht_mm"], 1)
                    if at.p == 2 and ni.real:
                        wait(pe, s["ht"], ni, item=True)
                        wait(pe, s["rexp"], ni.shift(-PER), item=True)
                        for t in range(NT):
                            mm = pe.matmul(rt_ps[:, t * E:(t + 1) * E],
                                           n.hT[:, (at.s // PER + 1) % 2, t * P:(t + 1) * P], w["rw3"][:],
                                           start=True, stop=True)
                        mm.then_inc(s["rt_mm"], 1)
                    if at.real:
                        wait(pe, s["hidden"], at)
                        wait(pe, s["acc"], at.shift(-2), 4)
                        width = P if at.p == LAST else 2 * P
                        for t in range(NT):
                            mm = pe.matmul(y_ps[at.ring(2)][:, t * width:(t + 1) * width],
                                           hidden[:, at.ring(2), t * P:(t + 1) * P],
                                           w["shared"][:] if at.p == LAST else w["down"][:, at.p, :],
                                           start=True, stop=True)
                        mm.then_inc(s["y_mm"], 1)

                walk(pe, PER, 2, LEAD, LAG, step)

            @block.vector
            def _(dve):
                start_norms(dve, n, s)
                dve.memset(b["probs"][:], -1.0)
                dve.memset(b["top"][:], -1.0).then_inc(s["pads"], 1)
                dve.wait_ge(s["pads"], 1)
                dve.wait_ge(k.gate_in[phase], 16)

                def step(at):
                    nx, ni = at.shift(1), at.shift(PER)
                    if at.p == 0 and ni.real:
                        normalise(dve, n, ni, s["ht_mm"], s["xn"])
                    if nx.real:
                        r = nx.ring(2)
                        wait(dve, s["tanh"], nx)
                        dve.scalar_tensor_tensor(out=gated[:, r, :], in0=tanh[:, r, :], scalar=1.0,
                                                 in1=gu_ps[r][:, 0:T], op0=ALU.add, op1=ALU.mult
                                                 ).then_inc(s["gated"], 1)
                        wait(dve, s["gated"], nx)
                        wait(dve, s["y_mm"], nx.shift(-2))
                        dve.scalar_tensor_tensor(out=hidden[:, r, :], in0=gated[:, r, :], scalar=0.5,
                                                 in1=gu_ps[r][:, T:2 * T], op0=ALU.mult, op1=ALU.mult
                                                 ).then_inc(s["hidden"], 1)
                    if at.p == 2 and ni.real:
                        wait(dve, s["rt_mm"], ni, item=True)
                        dve.tensor_reduce(b["nmax"][:], rt_ps[:, 0:NT * E].rearrange("p (t e) -> p t e", t=NT), AX_X,
                                          ALU.max, negate=True).then_inc(s["nmax"], 1)
                    if at.real:
                        wait(dve, s["y_mm"], at)
                        place = at.s // PER % 2
                        y, c = y_ps[at.ring(2)], b["cw"][:, at.s // PER % 2]
                        if at.p == 0:
                            wait(dve, s["cw"], at, item=True)
                            wait(dve, s["weighted"], at.shift(-2 * PER), item=True)
                        if at.p == LAST:
                            wait(dve, s["acc"], at.shift(-1), 4)
                            dve.tensor_tensor(acc[:, place], acc[:, place], y[:, 0:T].rearrange("p (t d) -> p t d", t=NT),
                                              ALU.add).then_inc(s["acc"], 4)
                        else:
                            for j in range(2):
                                for t in range(NT):
                                    a, z = acc[:, place, t, :], y[:, t * 2 * P + j * P:t * 2 * P + (j + 1) * P]
                                    e = 2 * at.p + j
                                    if j:
                                        wait(dve, s["acc"], at, 4, 3 - t)
                                    else:
                                        wait(dve, s["acc"], at.shift(-1), 4, 1 - t)
                                    if e == 0:
                                        i = dve.tensor_scalar(a, z, c[:, t, 0:1], None, ALU.mult)
                                    else:
                                        i = dve.scalar_tensor_tensor(out=a, in0=z, scalar=c[:, t, e:e + 1], in1=a,
                                                                     op0=ALU.mult, op1=ALU.add)
                                    i.then_inc(s["acc"], 1)
                    if at.p == 3 and ni.real:
                        softmax_top(dve, s, k.spare, ni, E, K, (at.s // PER + 1) % 2, b, acc_each=4, transposed=False)
                    if at.p == 1 and at.shift(-2).real:
                        row_stats(dve, n, at.shift(-2), s["added"])

                walk(dve, PER, 2, LEAD, LAG, step)


PHASES = [attention0, ffn0, attention1, ffn1, attention2, ffn2, attention3, ffn3]


def position_table(length, features):
    dist = np.arange(-length + 1, length, dtype=np.float64)
    n, a = features // 6, np.abs(dist)[:, None]
    decay = np.exp(-math.log(2.0) / 2.0 ** np.linspace(3.0, math.log2(length), n)[None] * a)
    central = (2.0 ** np.arange(1, n + 1)[None] - 1.0 > a).astype(np.float64)
    stddev = length / (2.0 * n)
    mean = np.linspace(length / n, float(length), n)[None]
    conc, rate = (mean / stddev) ** 2, mean / stddev ** 2
    log_a = np.log(np.maximum(a, 1e-300))
    log_norm = np.array([[math.lgamma(c) for c in conc[0]]]) - conc * np.log(rate)
    gamma = np.exp((conc - 1.0) * log_a - rate * a - log_norm) + 1e-8
    gamma = gamma / gamma.max(axis=-1, keepdims=True)
    emb = np.concatenate([decay, central, gamma], axis=-1)
    return np.concatenate([emb, np.sign(dist)[:, None] * emb], axis=-1).astype(np.float32)


def laid_out(i):
    f = {x: np.asarray(v) for x, v in i.items()}
    o = {}
    o["x"] = f["L0_attn_x"]
    o["cT"] = np.concatenate([f[f"L{n}_c"].T for n in range(4)], axis=1)
    o["wmod"] = np.stack([f[f"L{n}_wmod"] for n in range(4)], axis=1)
    o["ident"] = np.eye(P, dtype=np.float32)
    q = np.arange(P)
    o["causal"] = np.where(q[None, :] > q[:, None], MASKED, 0.0).astype(np.float32)

    def rows(a, k):
        return a.reshape(k, -1, a.shape[-1]).transpose(1, 0, 2)

    def bcast(a):
        return np.broadcast_to(a, (P, *a.shape))

    o["wqT0"], o["wkT0"] = (x.reshape(P, 16, 64).transpose(2, 1, 0) for x in (f["L0_attn_Wq"], f["L0_attn_Wkv"][:, :1024]))
    o["wv0"] = f["L0_attn_Wkv"][:, 1024:]
    o["wo0"] = rows(f["L0_attn_Wo"], 8)
    o["bo0"] = bcast(f["L0_attn_bo"])
    o["e1w"] = np.concatenate([f["L0_ffn_eW1"], f["L0_ffn_sW1"][None]]).transpose(1, 0, 2)
    o["e2w"] = np.concatenate([f["L0_ffn_eW2"], f["L0_ffn_sW2"][None]]).transpose(1, 0, 2)
    o["e1b"] = np.concatenate([f["L0_ffn_eb1"], f["L0_ffn_sb1"][None]]).T
    o["e2b"] = np.concatenate([f["L0_ffn_eb2"], f["L0_ffn_sb2"][None]])
    o["rw"] = f["L0_ffn_router_W"]
    o["rb"] = bcast(f["L0_ffn_router_b"])
    o["wqT"], o["wkT"] = (f[f"L1_attn_{x}"].reshape(P, 8, P).transpose(2, 1, 0) for x in ("w_qs", "w_ks"))
    o["wv1"] = f["L1_attn_w_vs"]
    o["wo1"] = rows(f["L1_attn_w_out"], 8)
    o["bo1"] = bcast(f["L1_attn_b_out"])
    o["qb1"] = np.stack([f["L1_attn_rel_embed_bias"][0, :, 0].T, f["L1_attn_rel_pos_bias"][0, :, 0].T], axis=1)
    o["w_relT"] = f["L1_attn_w_rel_pos_k"].reshape(2, 96, 8, P).transpose(3, 2, 0, 1)
    table = position_table(T, f["L1_attn_w_rel_pos_k"].shape[0])
    o["positions"] = rows(np.pad(table.T, ((0, 0), (0, 1))), 2)
    o["w12"] = f["L1_ffn_w12"].transpose(2, 0, 1)
    o["w3"] = f["L1_ffn_w3"].reshape(8, P, 2, P).transpose(3, 0, 2, 1)
    o["gw1"] = f["L1_ffn_gate_w"].T
    qkv = f["L2_attn_Wqkv"]
    swapped = np.arange(P) ^ 1
    angle = np.arange(T)[None, :] * (10000.0 ** (-(np.arange(P) % 8 // 2) / 4.0))[:, None]
    sign = np.where(np.arange(P) % 2 == 0, -1.0, 1.0)[:, None]
    by_feature = np.arange(P).reshape(16, 8).T.ravel()
    rope = np.stack([np.cos(angle), np.sin(angle) * sign], axis=1)[by_feature]
    for x, (wq, wk, wv), wo in ((2, [qkv[:, i * P:(i + 1) * P] for i in range(3)], f["L2_attn_Wproj"]),
                                (3, [f[f"L3_attn_W_{c}"].T for c in "qkv"], f["L3_attn_W_o"].T)):
        o[f"wqk{x}"] = np.stack([c[:, by_feature] for c in (wq, wq[:, swapped], wk, wk[:, swapped])], axis=1)
        o[f"wv{x}"], o[f"wproj{x}"] = wv, wo
        o[f"rope_q{x}"] = (rope / math.sqrt(8.0)).astype(np.float32)
        o[f"rope_k{x}"] = rope.astype(np.float32)
        o[f"head_rows{x}"] = (np.arange(16)[:, None] == np.arange(P)[None, :] // 8).astype(np.float32)

    def joined(w1, w2, b1, b2):
        return np.concatenate([w1.T, w2.T.reshape(4, P, P).transpose(1, 0, 2).reshape(P, -1), b1.reshape(4, P).T,
                               bcast(b2)], axis=1)

    o["base"] = joined(*(f[f"L2_ffn_{x}"] for x in ("W1", "W2", "b1", "b2")))
    o["task"] = np.stack([joined(*(f[f"L2_ffn_T{x}"][e] for x in ("W1", "W2", "b1", "b2"))) for e in range(8)], axis=1)
    o["gw1_2"], o["gb1"] = f["L2_ffn_gate_w1"].T, f["L2_ffn_gate_b1"][:, None]
    o["gw2"], o["gb2"] = f["L2_ffn_gate_w2"].T, bcast(f["L2_ffn_gate_b2"])
    pairs = [np.concatenate([f[f"L3_ffn_w_{x}"][e::2] for e in range(2)], axis=2) for x in ("gate", "up")]
    gu = np.stack([np.concatenate([pair, f[f"L3_ffn_ws_{x}"][None]]) for pair, x in zip(pairs, ("gate", "up"))], axis=1)
    o["gu"] = gu.transpose(2, 0, 1, 3)
    down = np.zeros((P, 4, 2, P), np.float32)
    down[0:64, :, 0], down[64:, :, 1] = (f["L3_ffn_w_down"][e::2].transpose(1, 0, 2) for e in range(2))
    o["down"], o["shared"], o["rw3"] = down, f["L3_ffn_ws_down"], f["L3_ffn_router_w"]
    for name, shape, parts in (w for ph in WEIGHTS for w in ph):
        o[name] = o[name].reshape(parts, -1)
    return o


def kernel(**inputs):
    import numpy as _np
    import concourse.bacc as _bacc
    from concourse import mybir as _mybir
    from concourse.bass_utils import run_bass_kernel_spmd as _run

    nc = _bacc.Bacc("TRN2", target_bir_lowering=False, num_devices=1)
    arrays, d = {}, {}
    for name, a in laid_out(inputs).items():
        a = _np.ascontiguousarray(a)
        arrays[f"in_{name}"] = a
        d[name] = nc.dram_tensor(f"in_{name}", a.shape, _mybir.dt.from_np(a.dtype), kind="ExternalInput").ap()
    out = nc.dram_tensor("out_0", (NB, T, P), _mybir.dt.float32, kind="ExternalOutput").ap()
    build(nc, d, out, PHASES)
    r = _run(nc, [arrays], core_ids=[0])
    return r.results[0]["out_0"]
```
